# Optimizing a Trainium2 kernel written in Bass

```python
import numpy as np
import jax
import jax.numpy as jnp

def _softmax(x, axis=-1):
    return jax.nn.softmax(x, axis=axis)

def _gelu(x):
    return jax.nn.gelu(x, approximate=True)

def _silu(x):
    return jax.nn.silu(x)

def _sigmoid(x):
    return jax.nn.sigmoid(x)

def _layernorm(x, axis=-1, eps=1e-05):
    m = jnp.mean(x, axis=axis, keepdims=True)
    v = jnp.var(x, axis=axis, keepdims=True)
    return (x - m) / jnp.sqrt(v + eps)

def _scatter_add(tgt, idx, src, axis=0):
    return tgt.at[idx].add(src)

def _segment_sum(src, seg, n):
    return jax.ops.segment_sum(src, seg, n)
kernel_name = 'mk_conv_preact_d4_conv_nchw128_r2_8325ff'

def setup_inputs(seed: int=0):
    np.random.seed(seed)
    _w = jnp.asarray

    def _rec_inputs():
        import jax
        import jax.numpy as jnp
        _gk = jax.random.key(seed)
        x = -0.0001732 + 1 * jax.random.normal(jax.random.fold_in(_gk, 1), (4, 64, 48, 48), jnp.float32)
        return x
    x = _rec_inputs()

    def _L0_conv_setup():
        import jax, jax.numpy as jnp
        import numpy as np
        N, C, H, W = (4, 64, 48, 48)
        G = 4
        GC = C // G
        K = 3
        PAD = 1
        P = K * K
        EPS = 1e-05

        def _dcnv3_core(xp, offset, mask):
            n, h, w, _ = xp.shape
            xpad = jnp.pad(xp, ((0, 0), (PAD, PAD), (PAD, PAD), (0, 0)))
            H_in, W_in = (h + 2 * PAD, w + 2 * PAD)
            Ho, Wo = (h, w)
            base = (K - 1) // 2 + 0.5
            ref_y = (jnp.arange(Ho, dtype=jnp.float32) + base) / H_in
            ref_x = (jnp.arange(Wo, dtype=jnp.float32) + base) / W_in
            lin = jnp.arange(K, dtype=jnp.float32) - (K - 1) // 2
            gx, gy = jnp.meshgrid(lin, lin, indexing='ij')
            gridx = (gx / W_in).reshape(P)
            gridy = (gy / H_in).reshape(P)
            off = offset.reshape(n, Ho, Wo, G, P, 2)
            loc_x = ref_x[None, None, :, None, None] + gridx[None, None, None, None, :] + off[..., 0] / W_in
            loc_y = ref_y[None, :, None, None, None] + gridy[None, None, None, None, :] + off[..., 1] / H_in
            ix = (loc_x * W_in - 0.5).transpose(0, 3, 1, 2, 4)
            iy = (loc_y * H_in - 0.5).transpose(0, 3, 1, 2, 4)
            x0 = jnp.floor(ix)
            y0 = jnp.floor(iy)
            wx1 = ix - x0
            wx0 = 1.0 - wx1
            wy1 = iy - y0
            wy0 = 1.0 - wy1
            x0i = x0.astype(jnp.int32)
            y0i = y0.astype(jnp.int32)
            x1i = x0i + 1
            y1i = y0i + 1
            img = xpad.reshape(n, H_in * W_in, G, GC).transpose(0, 2, 1, 3)

            def samp(yi, xi, wgt):
                valid = (yi >= 0) & (yi < H_in) & (xi >= 0) & (xi < W_in)
                idx = jnp.clip(yi, 0, H_in - 1) * W_in + jnp.clip(xi, 0, W_in - 1)
                idxf = idx.reshape(n, G, Ho * Wo * P, 1)
                v = jnp.take_along_axis(img, idxf, axis=2)
                w_eff = jnp.where(valid, wgt, 0.0).reshape(n, G, Ho * Wo * P, 1)
                return v * w_eff
            val = samp(y0i, x0i, wy0 * wx0) + samp(y0i, x1i, wy0 * wx1) + samp(y1i, x0i, wy1 * wx0) + samp(y1i, x1i, wy1 * wx1)
            val = val.reshape(n, G, Ho, Wo, P, GC)
            m = mask.transpose(0, 3, 1, 2, 4)[..., None]
            out = (val * m).sum(axis=4)
            return out.transpose(0, 2, 3, 1, 4).reshape(n, Ho, Wo, G * GC)
        key = jax.random.key(seed)
        ks = jax.random.split(key, 8)
        d = {}
        d['x'] = jax.random.normal(ks[0], (N, C, H, W), jnp.float32)
        d['dw_w'] = jax.random.normal(ks[1], (C, 1, K, K), jnp.float32) * 0.1
        d['dw_b'] = jnp.zeros((C,), jnp.float32)
        d['ln_g'] = jnp.ones((C,), jnp.float32)
        d['ln_b'] = jnp.zeros((C,), jnp.float32)
        d['w_off'] = jax.random.normal(ks[2], (C, G * P * 2), jnp.float32) * 0.01
        d['b_off'] = jnp.zeros((G * P * 2,), jnp.float32)
        d['w_mask'] = jax.random.normal(ks[3], (C, G * P), jnp.float32) * 0.02
        d['b_mask'] = jnp.zeros((G * P,), jnp.float32)
        d['w_in'] = jax.random.normal(ks[4], (C, C), jnp.float32) * (1.0 / np.sqrt(C))
        d['b_in'] = jnp.zeros((C,), jnp.float32)
        d['w_out'] = jax.random.normal(ks[5], (C, C), jnp.float32) * (1.0 / np.sqrt(C))
        d['b_out'] = jnp.zeros((C,), jnp.float32)
        d['bn_g'] = jnp.ones((C,), jnp.float32)
        d['bn_b'] = jnp.zeros((C,), jnp.float32)
        d['bn_mean'] = jnp.zeros((C,), jnp.float32)
        d['bn_var'] = jnp.ones((C,), jnp.float32)
        return d
    _L0_conv_all = _L0_conv_setup()
    _L0_conv_in = {k: v for k, v in _L0_conv_all.items() if k in ('dw_w', 'dw_b', 'ln_g', 'ln_b', 'w_off', 'b_off', 'w_mask', 'b_mask', 'w_in', 'b_in', 'w_out', 'b_out', 'bn_g', 'bn_b', 'bn_mean', 'bn_var')}
    del _L0_conv_all

    def _L1_conv_setup():
        import jax, jax.numpy as jnp
        import numpy as np
        K = 3
        K2 = K * K
        PAD = 1

        def conv3x3(x, w, b):
            y = jax.lax.conv_general_dilated(x, w, window_strides=(1, 1), padding=[(PAD, PAD), (PAD, PAD)], dimension_numbers=('NCHW', 'OIHW', 'NCHW'))
            return y + b[None, :, None, None]

        def conv1x1(x, w, b):
            return jnp.einsum('bchw,oc->bohw', x, w) + b[None, :, None, None]

        def bilinear_gather(x, py, px):
            B, C, H, W = x.shape
            y0 = jnp.floor(py)
            x0 = jnp.floor(px)
            wy = py - y0
            wx = px - x0
            y0i = y0.astype(jnp.int32)
            x0i = x0.astype(jnp.int32)
            xf = x.reshape(B, C, H * W)
            out = jnp.zeros((B, C) + py.shape[1:], x.dtype)
            corners = [(y0i, x0i, (1 - wy) * (1 - wx)), (y0i, x0i + 1, (1 - wy) * wx), (y0i + 1, x0i, wy * (1 - wx)), (y0i + 1, x0i + 1, wy * wx)]
            for yi, xi, wgt in corners:
                valid = (yi >= 0) & (yi < H) & (xi >= 0) & (xi < W)
                yc = jnp.clip(yi, 0, H - 1)
                xc = jnp.clip(xi, 0, W - 1)
                idx = (yc * W + xc).reshape(B, -1)
                g = jnp.take_along_axis(xf, idx[:, None, :], axis=2).reshape(B, C, K2, H, W)
                out = out + g * (wgt * valid.astype(x.dtype))[:, None]
            return out

        def deform_conv(x, offset, w, b):
            B, C, H, W = x.shape
            off = offset.reshape(B, K2, 2, H, W)
            dy, dx = (off[:, :, 0], off[:, :, 1])
            ki, kj = jnp.meshgrid(jnp.arange(K), jnp.arange(K), indexing='ij')
            base_y = jnp.arange(H)[None, None, :, None] + (ki.reshape(-1) - PAD)[None, :, None, None]
            base_x = jnp.arange(W)[None, None, None, :] + (kj.reshape(-1) - PAD)[None, :, None, None]
            py = base_y.astype(x.dtype) + dy
            px = base_x.astype(x.dtype) + dx
            sampled = bilinear_gather(x, py, px)
            O = w.shape[0]
            out = jnp.einsum('bckhw,ock->bohw', sampled, w.reshape(O, C, K2))
            return out + b[None, :, None, None]
        key = jax.random.key(seed)
        ks = jax.random.split(key, 16)
        Cin, Cout = (64, 64)
        B, H, W = (4, 48, 48)
        Hh = 8
        G1, G2 = (32, 32)

        def n(k, shape, s=0.05):
            return jax.random.normal(k, shape, jnp.float32) * s
        return {'x': jax.random.normal(ks[0], (B, Cin, H, W), jnp.float32), 'off_w0': n(ks[1], (2 * K2, Cin, 3, 3), 0.01), 'off_b0': jnp.zeros((2 * K2,), jnp.float32), 'dw0': n(ks[2], (Cout, Cin, 3, 3)), 'db0': jnp.zeros((Cout,), jnp.float32), 'off_w1': n(ks[3], (2 * K2, Cin, 3, 3), 0.01), 'off_b1': jnp.zeros((2 * K2,), jnp.float32), 'dw1': n(ks[4], (Cout, Cin, 3, 3)), 'db1': jnp.zeros((Cout,), jnp.float32), 'wg_w1': n(ks[5], (Hh, 2 * Cout)), 'wg_b1': jnp.zeros((Hh,), jnp.float32), 'wg_w2': n(ks[6], (2, Hh)), 'wg_b2': jnp.zeros((2,), jnp.float32), 'gp_w1': n(ks[7], (G1, Cin)), 'gp_b1': jnp.zeros((G1,), jnp.float32), 'gp_w2': n(ks[8], (G2, G1)), 'gp_b2': jnp.zeros((G2,), jnp.float32), 'gp_w3': n(ks[9], (Cout, G2)), 'gp_b3': jnp.zeros((Cout,), jnp.float32), 'cr_w': n(ks[10], (Cout, Cin)), 'cr_b': jnp.zeros((Cout,), jnp.float32)}
    _L1_conv_all = _L1_conv_setup()
    _L1_conv_in = {k: v for k, v in _L1_conv_all.items() if k in ('off_w0', 'off_b0', 'dw0', 'db0', 'off_w1', 'off_b1', 'dw1', 'db1', 'wg_w1', 'wg_b1', 'wg_w2', 'wg_b2', 'gp_w1', 'gp_b1', 'gp_w2', 'gp_b2', 'gp_w3', 'gp_b3', 'cr_w', 'cr_b')}
    del _L1_conv_all

    def _L2_conv_setup():
        import jax, jax.numpy as jnp
        import numpy as np

        def _prelu(x, a):
            return jnp.where(x >= 0, x, a * x)

        def _conv1x1(x, w, b, a):
            y = jnp.einsum('oc,nchw->nohw', w, x) + b[None, :, None, None]
            return _prelu(y, a)
        key = jax.random.key(seed)
        ks = jax.random.split(key, 8)
        N, C, H, W = (4, 64, 32, 32)
        Cr = C // 2
        sC = 1.0 / np.sqrt(C)
        x = jax.random.normal(ks[0], (N, C, H, W), dtype=jnp.float32)
        w1 = jax.random.normal(ks[1], (Cr, C), dtype=jnp.float32) * sC
        b1 = jnp.zeros((Cr,), dtype=jnp.float32)
        a1 = jnp.asarray(0.25, dtype=jnp.float32)
        w2 = jax.random.normal(ks[2], (Cr, C), dtype=jnp.float32) * sC
        b2 = jnp.zeros((Cr,), dtype=jnp.float32)
        a2 = jnp.asarray(0.25, dtype=jnp.float32)
        wa = jax.random.normal(ks[3], (C, C), dtype=jnp.float32) * sC
        ba = jnp.zeros((C,), dtype=jnp.float32)
        aa = jnp.asarray(0.25, dtype=jnp.float32)
        return {'x': x, 'w1': w1, 'b1': b1, 'a1': a1, 'w2': w2, 'b2': b2, 'a2': a2, 'wa': wa, 'ba': ba, 'aa': aa}
    _L2_conv_all = _L2_conv_setup()
    _L2_conv_in = {k: v for k, v in _L2_conv_all.items() if k in ('w1', 'b1', 'a1', 'w2', 'b2', 'a2', 'wa', 'ba', 'aa')}
    del _L2_conv_all

    def _L3_conv_setup():
        import jax, jax.numpy as jnp
        import numpy as np
        K = 3
        key = jax.random.key(seed)
        k0, k1, k2 = jax.random.split(key, 3)
        B, C, O, H, W, HID = (32, 64, 64, 32, 32, 32)
        x = jax.random.normal(k0, (B, C, H, W), dtype=jnp.float32)
        W1 = jax.random.normal(k1, (HID, C), dtype=jnp.float32) * 0.05
        b1 = jnp.zeros((HID,), dtype=jnp.float32)
        W2 = jax.random.normal(k2, (O * C * K * K, HID), dtype=jnp.float32) * 0.02
        b2 = jnp.zeros((O * C * K * K,), dtype=jnp.float32)
        return {'x': x, 'W1': W1, 'b1': b1, 'W2': W2, 'b2': b2}
    _L3_conv_all = _L3_conv_setup()
    _L3_conv_in = {k: v for k, v in _L3_conv_all.items() if k in ('W1', 'b1', 'W2', 'b2')}
    del _L3_conv_all
    return {'x': x, 'L0_conv_dw_w': _L0_conv_in['dw_w'], 'L0_conv_dw_b': _L0_conv_in['dw_b'], 'L0_conv_ln_g': _L0_conv_in['ln_g'], 'L0_conv_ln_b': _L0_conv_in['ln_b'], 'L0_conv_w_off': _L0_conv_in['w_off'], 'L0_conv_b_off': _L0_conv_in['b_off'], 'L0_conv_w_mask': _L0_conv_in['w_mask'], 'L0_conv_b_mask': _L0_conv_in['b_mask'], 'L0_conv_w_in': _L0_conv_in['w_in'], 'L0_conv_b_in': _L0_conv_in['b_in'], 'L0_conv_w_out': _L0_conv_in['w_out'], 'L0_conv_b_out': _L0_conv_in['b_out'], 'L0_conv_bn_g': _L0_conv_in['bn_g'], 'L0_conv_bn_b': _L0_conv_in['bn_b'], 'L0_conv_bn_mean': _L0_conv_in['bn_mean'], 'L0_conv_bn_var': _L0_conv_in['bn_var'], 'L1_conv_off_w0': _L1_conv_in['off_w0'], 'L1_conv_off_b0': _L1_conv_in['off_b0'], 'L1_conv_dw0': _L1_conv_in['dw0'], 'L1_conv_db0': _L1_conv_in['db0'], 'L1_conv_off_w1': _L1_conv_in['off_w1'], 'L1_conv_off_b1': _L1_conv_in['off_b1'], 'L1_conv_dw1': _L1_conv_in['dw1'], 'L1_conv_db1': _L1_conv_in['db1'], 'L1_conv_wg_w1': _L1_conv_in['wg_w1'], 'L1_conv_wg_b1': _L1_conv_in['wg_b1'], 'L1_conv_wg_w2': _L1_conv_in['wg_w2'], 'L1_conv_wg_b2': _L1_conv_in['wg_b2'], 'L1_conv_gp_w1': _L1_conv_in['gp_w1'], 'L1_conv_gp_b1': _L1_conv_in['gp_b1'], 'L1_conv_gp_w2': _L1_conv_in['gp_w2'], 'L1_conv_gp_b2': _L1_conv_in['gp_b2'], 'L1_conv_gp_w3': _L1_conv_in['gp_w3'], 'L1_conv_gp_b3': _L1_conv_in['gp_b3'], 'L1_conv_cr_w': _L1_conv_in['cr_w'], 'L1_conv_cr_b': _L1_conv_in['cr_b'], 'L2_conv_w1': _L2_conv_in['w1'], 'L2_conv_b1': _L2_conv_in['b1'], 'L2_conv_a1': _L2_conv_in['a1'], 'L2_conv_w2': _L2_conv_in['w2'], 'L2_conv_b2': _L2_conv_in['b2'], 'L2_conv_a2': _L2_conv_in['a2'], 'L2_conv_wa': _L2_conv_in['wa'], 'L2_conv_ba': _L2_conv_in['ba'], 'L2_conv_aa': _L2_conv_in['aa'], 'L3_conv_W1': _L3_conv_in['W1'], 'L3_conv_b1': _L3_conv_in['b1'], 'L3_conv_W2': _L3_conv_in['W2'], 'L3_conv_b2': _L3_conv_in['b2']}

def reference(x, L0_conv_dw_w, L0_conv_dw_b, L0_conv_ln_g, L0_conv_ln_b, L0_conv_w_off, L0_conv_b_off, L0_conv_w_mask, L0_conv_b_mask, L0_conv_w_in, L0_conv_b_in, L0_conv_w_out, L0_conv_b_out, L0_conv_bn_g, L0_conv_bn_b, L0_conv_bn_mean, L0_conv_bn_var, L1_conv_off_w0, L1_conv_off_b0, L1_conv_dw0, L1_conv_db0, L1_conv_off_w1, L1_conv_off_b1, L1_conv_dw1, L1_conv_db1, L1_conv_wg_w1, L1_conv_wg_b1, L1_conv_wg_w2, L1_conv_wg_b2, L1_conv_gp_w1, L1_conv_gp_b1, L1_conv_gp_w2, L1_conv_gp_b2, L1_conv_gp_w3, L1_conv_gp_b3, L1_conv_cr_w, L1_conv_cr_b, L2_conv_w1, L2_conv_b1, L2_conv_a1, L2_conv_w2, L2_conv_b2, L2_conv_a2, L2_conv_wa, L2_conv_ba, L2_conv_aa, L3_conv_W1, L3_conv_b1, L3_conv_W2, L3_conv_b2):
    import jax
    import jax.numpy as jnp

    def _L0_conv_ref(x, dw_w, dw_b, ln_g, ln_b, w_off, b_off, w_mask, b_mask, w_in, b_in, w_out, b_out, bn_g, bn_b, bn_mean, bn_var):
        import jax, jax.numpy as jnp
        import numpy as np
        N, C, H, W = (4, 64, 48, 48)
        G = 4
        GC = C // G
        K = 3
        PAD = 1
        P = K * K
        EPS = 1e-05

        def _dcnv3_core(xp, offset, mask):
            n, h, w, _ = xp.shape
            xpad = jnp.pad(xp, ((0, 0), (PAD, PAD), (PAD, PAD), (0, 0)))
            H_in, W_in = (h + 2 * PAD, w + 2 * PAD)
            Ho, Wo = (h, w)
            base = (K - 1) // 2 + 0.5
            ref_y = (jnp.arange(Ho, dtype=jnp.float32) + base) / H_in
            ref_x = (jnp.arange(Wo, dtype=jnp.float32) + base) / W_in
            lin = jnp.arange(K, dtype=jnp.float32) - (K - 1) // 2
            gx, gy = jnp.meshgrid(lin, lin, indexing='ij')
            gridx = (gx / W_in).reshape(P)
            gridy = (gy / H_in).reshape(P)
            off = offset.reshape(n, Ho, Wo, G, P, 2)
            loc_x = ref_x[None, None, :, None, None] + gridx[None, None, None, None, :] + off[..., 0] / W_in
            loc_y = ref_y[None, :, None, None, None] + gridy[None, None, None, None, :] + off[..., 1] / H_in
            ix = (loc_x * W_in - 0.5).transpose(0, 3, 1, 2, 4)
            iy = (loc_y * H_in - 0.5).transpose(0, 3, 1, 2, 4)
            x0 = jnp.floor(ix)
            y0 = jnp.floor(iy)
            wx1 = ix - x0
            wx0 = 1.0 - wx1
            wy1 = iy - y0
            wy0 = 1.0 - wy1
            x0i = x0.astype(jnp.int32)
            y0i = y0.astype(jnp.int32)
            x1i = x0i + 1
            y1i = y0i + 1
            img = xpad.reshape(n, H_in * W_in, G, GC).transpose(0, 2, 1, 3)

            def samp(yi, xi, wgt):
                valid = (yi >= 0) & (yi < H_in) & (xi >= 0) & (xi < W_in)
                idx = jnp.clip(yi, 0, H_in - 1) * W_in + jnp.clip(xi, 0, W_in - 1)
                idxf = idx.reshape(n, G, Ho * Wo * P, 1)
                v = jnp.take_along_axis(img, idxf, axis=2)
                w_eff = jnp.where(valid, wgt, 0.0).reshape(n, G, Ho * Wo * P, 1)
                return v * w_eff
            val = samp(y0i, x0i, wy0 * wx0) + samp(y0i, x1i, wy0 * wx1) + samp(y1i, x0i, wy1 * wx0) + samp(y1i, x1i, wy1 * wx1)
            val = val.reshape(n, G, Ho, Wo, P, GC)
            m = mask.transpose(0, 3, 1, 2, 4)[..., None]
            out = (val * m).sum(axis=4)
            return out.transpose(0, 2, 3, 1, 4).reshape(n, Ho, Wo, G * GC)
        x_nhwc = x.transpose(0, 2, 3, 1)
        x_proj = x_nhwc @ w_in + b_in
        x1 = jax.lax.conv_general_dilated(x, dw_w, (1, 1), ((PAD, PAD), (PAD, PAD)), feature_group_count=C, dimension_numbers=('NCHW', 'OIHW', 'NCHW'))
        x1 = x1.transpose(0, 2, 3, 1) + dw_b
        mu = x1.mean(-1, keepdims=True)
        var = ((x1 - mu) ** 2).mean(-1, keepdims=True)
        x1 = (x1 - mu) * jax.lax.rsqrt(var + EPS) * ln_g + ln_b
        x1 = jax.nn.gelu(x1, approximate=False)
        offset = x1 @ w_off + b_off
        mask = jax.nn.softmax((x1 @ w_mask + b_mask).reshape(N, H, W, G, P), axis=-1)
        out = _dcnv3_core(x_proj, offset, mask)
        out = out @ w_out + b_out
        y = out.transpose(0, 3, 1, 2)
        inv = jax.lax.rsqrt(bn_var + EPS)
        y = (y - bn_mean[:, None, None]) * (inv * bn_g)[:, None, None] + bn_b[:, None, None]
        return y * jax.nn.sigmoid(y)

    def _L1_conv_ref(x, off_w0, off_b0, dw0, db0, off_w1, off_b1, dw1, db1, wg_w1, wg_b1, wg_w2, wg_b2, gp_w1, gp_b1, gp_w2, gp_b2, gp_w3, gp_b3, cr_w, cr_b):
        import jax, jax.numpy as jnp
        import numpy as np
        K = 3
        K2 = K * K
        PAD = 1

        def conv3x3(x, w, b):
            y = jax.lax.conv_general_dilated(x, w, window_strides=(1, 1), padding=[(PAD, PAD), (PAD, PAD)], dimension_numbers=('NCHW', 'OIHW', 'NCHW'))
            return y + b[None, :, None, None]

        def conv1x1(x, w, b):
            return jnp.einsum('bchw,oc->bohw', x, w) + b[None, :, None, None]

        def bilinear_gather(x, py, px):
            B, C, H, W = x.shape
            y0 = jnp.floor(py)
            x0 = jnp.floor(px)
            wy = py - y0
            wx = px - x0
            y0i = y0.astype(jnp.int32)
            x0i = x0.astype(jnp.int32)
            xf = x.reshape(B, C, H * W)
            out = jnp.zeros((B, C) + py.shape[1:], x.dtype)
            corners = [(y0i, x0i, (1 - wy) * (1 - wx)), (y0i, x0i + 1, (1 - wy) * wx), (y0i + 1, x0i, wy * (1 - wx)), (y0i + 1, x0i + 1, wy * wx)]
            for yi, xi, wgt in corners:
                valid = (yi >= 0) & (yi < H) & (xi >= 0) & (xi < W)
                yc = jnp.clip(yi, 0, H - 1)
                xc = jnp.clip(xi, 0, W - 1)
                idx = (yc * W + xc).reshape(B, -1)
                g = jnp.take_along_axis(xf, idx[:, None, :], axis=2).reshape(B, C, K2, H, W)
                out = out + g * (wgt * valid.astype(x.dtype))[:, None]
            return out

        def deform_conv(x, offset, w, b):
            B, C, H, W = x.shape
            off = offset.reshape(B, K2, 2, H, W)
            dy, dx = (off[:, :, 0], off[:, :, 1])
            ki, kj = jnp.meshgrid(jnp.arange(K), jnp.arange(K), indexing='ij')
            base_y = jnp.arange(H)[None, None, :, None] + (ki.reshape(-1) - PAD)[None, :, None, None]
            base_x = jnp.arange(W)[None, None, None, :] + (kj.reshape(-1) - PAD)[None, :, None, None]
            py = base_y.astype(x.dtype) + dy
            px = base_x.astype(x.dtype) + dx
            sampled = bilinear_gather(x, py, px)
            O = w.shape[0]
            out = jnp.einsum('bckhw,ock->bohw', sampled, w.reshape(O, C, K2))
            return out + b[None, :, None, None]
        s0 = deform_conv(x, conv3x3(x, off_w0, off_b0), dw0, db0)
        s1 = deform_conv(x, conv3x3(x, off_w1, off_b1), dw1, db1)
        cat_pool = jnp.concatenate([s0, s1], axis=1).mean(axis=(2, 3), keepdims=True)
        h = jax.nn.relu(conv1x1(cat_pool, wg_w1, wg_b1))
        wts = jax.nn.softmax(conv1x1(h, wg_w2, wg_b2), axis=1)
        fused = wts[:, 0:1] * s0 + wts[:, 1:2] * s1
        g = x.mean(axis=(2, 3), keepdims=True)
        g = jax.nn.relu(conv1x1(g, gp_w1, gp_b1))
        g = jax.nn.relu(conv1x1(g, gp_w2, gp_b2))
        g = jax.nn.sigmoid(conv1x1(g, gp_w3, gp_b3))
        x_reduced = conv1x1(x, cr_w, cr_b)
        return fused + x_reduced * g

    def _L2_conv_ref(x, w1, b1, a1, w2, b2, a2, wa, ba, aa):
        import jax, jax.numpy as jnp
        import numpy as np

        def _prelu(x, a):
            return jnp.where(x >= 0, x, a * x)

        def _conv1x1(x, w, b, a):
            y = jnp.einsum('oc,nchw->nohw', w, x) + b[None, :, None, None]
            return _prelu(y, a)
        N, C, H, W = x.shape
        HW = H * W
        e1 = _conv1x1(x, w1, b1, a1).reshape(N, -1, HW)
        e2 = _conv1x1(x, w2, b2, a2).reshape(N, -1, HW)
        asm = _conv1x1(x, wa, ba, aa).reshape(N, C, HW)
        score = jnp.einsum('nci,ncj->nij', e1, e2)
        score = jax.nn.softmax(score, axis=2)
        out = jnp.einsum('nij,ncj->nci', score, asm)
        return out.reshape(N, C, H, W)

    def _L3_conv_ref(x, W1, b1, W2, b2):
        import jax, jax.numpy as jnp
        import numpy as np
        K = 3
        B, C, H, Wd = x.shape
        O = W2.shape[0] // (C * K * K)
        pooled = jnp.mean(x, axis=(2, 3))
        h = jax.nn.relu(pooled @ W1.T + b1)
        w = (h @ W2.T + b2).reshape(B, O, C, K, K)

        def conv_one(xi, wi):
            return jax.lax.conv_general_dilated(xi[None], wi, window_strides=(1, 1), padding=[(1, 1), (1, 1)], dimension_numbers=('NCHW', 'OIHW', 'NCHW'))[0]
        return jax.vmap(conv_one)(x, w)

    def _gn(v, G=32, eps=1e-05):
        B_, C_, H_, W_ = v.shape
        g = v.reshape(B_, G, C_ // G, H_, W_)
        m = jnp.mean(g, axis=(2, 3, 4), keepdims=True)
        s = jnp.var(g, axis=(2, 3, 4), keepdims=True)
        return ((g - m) / jnp.sqrt(s + eps)).reshape(v.shape)

    def _ln_c(v, eps=1e-06):
        m = jnp.mean(v, axis=1, keepdims=True)
        s = jnp.var(v, axis=1, keepdims=True)
        return (v - m) / jnp.sqrt(s + eps)

    def _ln_t(v, eps=1e-05):
        m = jnp.mean(v, axis=-1, keepdims=True)
        s = jnp.var(v, axis=-1, keepdims=True)
        return (v - m) / jnp.sqrt(s + eps)

    def _to_tokens(v):
        B_, C_, H_, W_ = v.shape
        return v.reshape(B_, C_, H_ * W_).transpose(0, 2, 1)

    def _from_tokens(t, like):
        B_, C_, H_, W_ = like.shape
        return t.transpose(0, 2, 1).reshape(B_, C_, H_, W_)
    x = x + _L0_conv_ref(_gn(x), L0_conv_dw_w, L0_conv_dw_b, L0_conv_ln_g, L0_conv_ln_b, L0_conv_w_off, L0_conv_b_off, L0_conv_w_mask, L0_conv_b_mask, L0_conv_w_in, L0_conv_b_in, L0_conv_w_out, L0_conv_b_out, L0_conv_bn_g, L0_conv_bn_b, L0_conv_bn_mean, L0_conv_bn_var)
    x = x + _L1_conv_ref(_gn(x), L1_conv_off_w0, L1_conv_off_b0, L1_conv_dw0, L1_conv_db0, L1_conv_off_w1, L1_conv_off_b1, L1_conv_dw1, L1_conv_db1, L1_conv_wg_w1, L1_conv_wg_b1, L1_conv_wg_w2, L1_conv_wg_b2, L1_conv_gp_w1, L1_conv_gp_b1, L1_conv_gp_w2, L1_conv_gp_b2, L1_conv_gp_w3, L1_conv_gp_b3, L1_conv_cr_w, L1_conv_cr_b)
    x = x + _L2_conv_ref(_gn(x), L2_conv_w1, L2_conv_b1, L2_conv_a1, L2_conv_w2, L2_conv_b2, L2_conv_a2, L2_conv_wa, L2_conv_ba, L2_conv_aa)
    x = x + _L3_conv_ref(_gn(x), L3_conv_W1, L3_conv_b1, L3_conv_W2, L3_conv_b2)
    return x

_drawn_inputs = setup_inputs


def setup_inputs(seed=0):
    import zlib

    import numpy as np

    out = dict(_drawn_inputs(seed))
    spreads = {'L0_conv_dw_b': (0.0, 0.8),
     'L0_conv_ln_g': (1.0, 0.6),
     'L0_conv_ln_b': (0.0, 2.0),
     'L0_conv_b_off': (0.0, 0.1),
     'L0_conv_b_in': (0.0, 0.1),
     'L0_conv_b_out': (0.0, 0.1),
     'L0_conv_bn_g': (1.0, 0.2),
     'L0_conv_bn_b': (0.0, 0.1),
     'L0_conv_bn_mean': (0.0, 0.1),
     'L0_conv_bn_var': (1.0, 0.584),
     'L1_conv_off_b0': (0.0, 0.1),
     'L1_conv_db0': (0.0, 0.1),
     'L1_conv_off_b1': (0.0, 0.1),
     'L1_conv_db1': (0.0, 0.292),
     'L1_conv_wg_b1': (0.0, 0.8),
     'L1_conv_wg_b2': (0.0, 0.277),
     'L1_conv_gp_b1': (0.0, 0.8),
     'L1_conv_gp_b2': (0.0, 0.8),
     'L1_conv_gp_b3': (0.0, 1.745),
     'L1_conv_cr_b': (0.0, 0.1),
     'L2_conv_b1': (0.0, 0.1),
     'L2_conv_b2': (0.0, 0.538),
     'L2_conv_ba': (0.0, 0.1),
     'L3_conv_b1': (0.0, 0.1),
     'L3_conv_b2': (0.0, 0.1)}
    factors = {'L1_conv_wg_w1': 4.987,
     'L1_conv_wg_w2': 8.0,
     'L1_conv_gp_w1': 22.706,
     'L1_conv_gp_w2': 8.0,
     'L1_conv_gp_w3': 8.0,
     'L0_conv_dw_w': 3.09}
    for name, (base, spread) in spreads.items():
        noise = np.random.default_rng([zlib.crc32(name.encode()), seed]).standard_normal(out[name].shape)
        drawn = base * np.exp(spread * noise) if base else spread * noise
        out[name] = jnp.asarray(drawn.astype(out[name].dtype))
    for name, factor in factors.items():
        out[name] = (out[name] * factor).astype(out[name].dtype)
    return out
```

```python
import concourse.bass as bass
from concourse import mybir
from contextlib import ExitStack, contextmanager

F32 = mybir.dt.float32
U32 = mybir.dt.uint32
ALU = mybir.AluOpType
ACT = mybir.ActivationFunctionType
AX = mybir.AxisListType

NB, C, HH, WW = 4, 64, 48, 48
PIX = HH * WW
COLS = 2 * PIX
PT = 128
TPI = PIX // PT
NT = 2 * TPI
PH = HH + 2
PQ = HH + 4
TAPS = 9
G = 4
ROWS = 8
CH = ROWS * WW
CPI = HH // ROWS
TPC = CH // PT
TR = PH - 1
ROUND = 12582912.0
MG = G * TAPS
OM = 3 * MG
S1 = 2 * TAPS
HID = 32

V64 = ["b_in", "dw_b", "ln_g", "ln_b", "b_out", "bn_g", "bn_b", "bn_mean", "bn_var", "gp_b3", "cr_b"]
VC = {n: i for i, n in enumerate(V64)}


class Chain:

    def __init__(self, eng, sem):
        self.eng, self.sem, self.off, self.n = eng, sem, 0, 0

    def __call__(self, ins):
        self.n += 1
        ins.then_inc(self.sem, 1)
        self.eng.wait_ge(self.sem, self.off + self.n)

    @contextmanager
    def body(self, i, per, count):
        before, self.off, self.n = self.n, self.n + i * per, 0
        yield
        assert self.n == per, self.n
        self.off, self.n = 0, before + per * count


def signal(k, name):
    k["signals"].append(k["nc"].alloc_semaphore(name))
    return k["signals"][-1]


def end_layer(nc, k):
    nc.all_engine_barrier()
    nc.clear_and_free_semaphores(k["signals"])
    nc.all_engine_barrier()
    k["signals"] = []


def load_stage(nc, k):
    ctx, d = k["ctx"], k["dram"]
    t_x = k["x"]
    loaded = signal(k, "weights_loaded")
    cleared = signal(k, "weights_cleared")
    built = signal(k, "diag_built")
    with nc.Block() as block:
        n = [0]

        @block.sync
        def _(sp):
            def load(dst, src):
                sp.dma_start(dst, src).then_inc(loaded, 16)
                n[0] += 16

            for h in range(2):
                load(t_x[64 * h:64 * h + 64, :].rearrange("c (b n) -> c b n", b=2),
                     d["x"][2 * h:2 * h + 2].rearrange("b c y x -> c b (y x)"))
                load(k["vec"][64 * h:64 * h + 64, :], d["vec64"])
                load(k["dw"][64 * h:64 * h + 64, :], d["dw_w"])
            load(k["ident"][:, :], d["ident"])
            load(k["sel"][:, :, :], d["sel"])
            load(k["pairm"][:, :], d["pairm"])
            load(k["halfm"][:, :], d["halfm"])
            for name in ("b_om", "b1_3", "ba"):
                load(k[name][:, :], d[name].partition_broadcast(128))
            for name in ("offb", "dbs", "wg1T", "wgb1", "wg2T", "gp1T", "gpb1", "gp2T", "gpb2", "gp3T",
                         "l2b", "stack2"):
                load(k[name][:, :], d[name])
            load(k["wgb2"][:, :], d["wgb2"].partition_broadcast(4))
            load(k["alphas"][:, :], d["alphas"])
            sp.wait_ge(cleared, 1)
            for h in range(2):
                r = slice(64 * h, 64 * h + 64)
                load(k["wom"][r, OM * h:OM * h + OM], d["w_om"])
                load(k["win"][r, r], d["w_in"])
                load(k["wout"][r, r], d["w_out"])
                load(k["crT"][r, r], d["crT"])
                load(k["waT"][r, r], d["waT"])
                load(k["w31T"][r, :], d["w31T"])
                load(k["offw"][r, :, 36 * h:36 * h + 36], d["offw"])
                load(k["l2w"][r, r], d["l2w"])
            for m in range(TAPS):
                for u in range(2):
                    s = 2 * m + u
                    v, tap = s // TAPS, s % TAPS
                    load(k["dws"][64 * u:64 * u + 64, m, 64 * v:64 * v + 64], d["dws"][v, tap])
            sp.wait_ge(loaded, n[0])

        @block.gpsimd
        def _(pool):
            for name in ("wom", "win", "wout", "crT", "waT", "offw", "l2w", "dws", "xp"):
                ins = pool.memset(k[name + "_flat"], 0.0)
            pool.memset(k["eps"][:, :], 1e-5)
            pool.memset(k["ones"][:, :], 1.0).then_inc(cleared, 1)

        @block.vector
        def _(v):
            v.wait_ge(cleared, 1)


def vector_setup(nc, k):
    ctx = k["ctx"]
    steps = signal(k, "setup_steps")
    rooted = signal(k, "bn_rooted")
    with nc.Block() as block:
        @block.scalar
        def _(act):
            act.activation(k["bn"][:, 0:1], k["vec"][:, VC["bn_var"]:VC["bn_var"] + 1], ACT.Sqrt,
                           bias=k["eps"][:, 0:1]).then_inc(rooted, 1)

        @block.vector
        def _(v):
            step = Chain(v, steps)
            v.tensor_copy(k["identb"][:, :], k["ident"][:, :])
            for t in range(TAPS):
                v.tensor_scalar(k["dwdiag"][:, t, :], k["ident"][:, :], k["dw"][:, t:t + 1], None, ALU.mult)
            bn, vec = k["bn"], k["vec"]

            def col(n):
                return vec[:, VC[n]:VC[n] + 1]
            v.wait_ge(rooted, 1)
            step(v.reciprocal(bn[:, 1:2], bn[:, 0:1]))
            step(v.tensor_tensor(bn[:, 2:3], bn[:, 1:2], col("bn_g"), ALU.mult))
            step(v.tensor_tensor(bn[:, 3:4], col("b_out"), col("bn_mean"), ALU.subtract))
            step(v.tensor_tensor(bn[:, 4:5], bn[:, 3:4], bn[:, 2:3], ALU.mult))
            step(v.tensor_tensor(bn[:, 5:6], bn[:, 4:5], col("bn_b"), ALU.add))


def group_norm(nc, k, tag, padded):
    ctx = k["ctx"]
    x, xn, xp, st = k["x"], k["xn"], k["xp"], k["stats"]
    ps = k["psum"]
    sums = signal(k, tag + "_sums")
    mean_ps = signal(k, tag + "_mean_ps")
    means = signal(k, tag + "_means")
    squares = signal(k, tag + "_squares")
    var_ps = signal(k, tag + "_var_ps")
    rooted = signal(k, tag + "_rooted")
    normed = signal(k, tag + "_normed")
    steps = signal(k, tag + "_steps")
    x3 = x[:, :].rearrange("p (b n) -> p b n", b=2)
    with nc.Block() as block:
        @block.vector
        def _(v):
            step = Chain(v, steps)
            v.tensor_reduce(st[:, 0:2], x3, AX.X, ALU.add).then_inc(sums, 1)
            v.wait_ge(mean_ps, 1)
            step(v.tensor_copy(st[:, 2:4], ps[:, 0:2]))
            v.tensor_scalar(st[:, 4:6], st[:, 2:4], -1.0, None, ALU.mult).then_inc(means, 1)
            v.wait_ge(rooted, 1)
            step(v.reciprocal(st[:, 10:12], st[:, 8:10]))
            for b in range(2):
                v.tensor_scalar(xn[:, PIX * b:PIX * b + PIX], x[:, PIX * b:PIX * b + PIX], st[:, 2 + b:3 + b],
                                st[:, 10 + b:11 + b], ALU.subtract, ALU.mult).then_inc(normed, 1)

        @block.tensor
        def _(pe):
            pe.wait_ge(sums, 1)
            pe.matmul(ps[:, 0:2], k["pairm"][:, :], st[:, 0:2], start=True, stop=True).then_inc(mean_ps, 1)
            pe.wait_ge(squares, 2)
            pe.matmul(ps[:, 512:514], k["pairm"][:, :], st[:, 6:8], start=True, stop=True).then_inc(var_ps, 1)

        @block.scalar
        def _(act):
            act.wait_ge(means, 1)
            for b in range(2):
                act.activation(xn[:, PIX * b:PIX * b + PIX], x[:, PIX * b:PIX * b + PIX], ACT.Square,
                               bias=st[:, 4 + b:5 + b], accum_out=st[:, 6 + b:7 + b]).then_inc(squares, 1)
            act.wait_ge(var_ps, 1)
            act.activation(st[:, 8:10], ps[:, 512:514], ACT.Sqrt, bias=k["eps"][:, 0:1]).then_inc(rooted, 1)
            if padded:
                for b in range(2):
                    act.wait_ge(normed, b + 1)
                    act.activation(xp[:, b, 1:HH + 1, 1:WW + 1],
                                   xn[:, PIX * b:PIX * b + PIX].rearrange("p (y x) -> p y x", y=HH), ACT.Copy)


def chunk_window(xp, b2, r, tap):
    dy, dx = divmod(tap, 3)
    return xp[:, b2, bass.ds(r * ROWS + dy, ROWS), dx:dx + WW]


def offsets0(nc, k, om):
    ctx, ps, xp, xn = k["ctx"], k["psum"], k["xp"], k["xn"]
    big = k["work0"]
    conv, cent, sq, root, inv, z, gel, xs = (big[:, CH * i:CH * i + CH] for i in range(8))
    xq = k["xproj"]
    S = {n: signal(k, "off0_" + n) for n in
         ("conv_ps", "conv", "mean_ps", "cent", "sq", "var_ps", "root", "z", "gelu", "om_ps", "om",
          "proj_ps", "proj", "steps", "cleared")}
    p_conv, p_mean, p_var = ps[:, 0:CH], ps[:, 512:512 + CH], ps[:, 1024:1024 + CH]
    p_om = ps[:, 1536:1536 + TPC * 256].rearrange("p (t n) -> p t n", t=TPC)
    p_proj = ps[:, 2560:2560 + CH]
    vec = k["vec"]

    def turns(eng):
        for b2 in range(2):
            with eng.Fori(0, CPI) as r:
                yield b2, r, b2 * CPI + r + 1

    with nc.Block() as block:
        @block.tensor
        def _(pe):
            pe.sem_inc(S["om"], 1)
            pe.sem_inc(S["proj"], 1)
            for b2, r, n in turns(pe):
                pe.wait_ge(S["om"], n)
                for t in range(TAPS):
                    mm = pe.matmul(p_conv.rearrange("p (y x) -> p y x", y=ROWS), k["dwdiag"][:, t, :],
                                   chunk_window(xp, b2, r, t), start=(t == 0), stop=(t == TAPS - 1))
                mm.then_inc(S["conv_ps"], 1)
                pe.wait_ge(S["conv"], n)
                pe.matmul(p_mean, k["halfm"][:, :], conv, start=True, stop=True).then_inc(S["mean_ps"], 1)
                pe.wait_ge(S["proj"], n)
                pe.matmul(p_proj, k["win"][:, :], xn[:, bass.ds(r * CH + b2 * PIX, CH)], start=True, stop=True)\
                    .then_inc(S["proj_ps"], 1)
                pe.wait_ge(S["sq"], n)
                pe.matmul(p_var, k["halfm"][:, :], sq, start=True, stop=True).then_inc(S["var_ps"], 1)
                pe.wait_ge(S["gelu"], n)
                for t in range(TPC):
                    mm = pe.matmul(p_om[:, t, 0:2 * OM], gel[:, PT * t:PT * t + PT], k["wom"][:, :],
                                   start=True, stop=True)
                mm.then_inc(S["om_ps"], 1)

        @block.scalar
        def _(act):
            for b2, r, n in turns(act):
                act.wait_ge(S["conv_ps"], n)
                act.activation(conv, p_conv, ACT.Identity, bias=vec[:, VC["dw_b"]:VC["dw_b"] + 1])\
                    .then_inc(S["conv"], 1)
                if b2 == 0:
                    act.wait_ge(S["cleared"], 1)
                act.wait_ge(S["proj_ps"], n)
                act.activation(xq[:, b2, bass.ds(r * ROWS + 2, ROWS), 2:2 + WW],
                               p_proj.rearrange("p (y x) -> p y x", y=ROWS), ACT.Identity,
                               bias=vec[:, VC["b_in"]:VC["b_in"] + 1]).then_inc(S["proj"], 1)
                act.wait_ge(S["cent"], n)
                act.activation(sq, cent, ACT.Square).then_inc(S["sq"], 1)
                act.wait_ge(S["var_ps"], n)
                act.activation(root, p_var, ACT.Sqrt, bias=k["eps"][:, 0:1]).then_inc(S["root"], 1)
                act.wait_ge(S["z"], n)
                act.activation(gel, z, ACT.Gelu, scale=vec[:, VC["ln_g"]:VC["ln_g"] + 1],
                               bias=vec[:, VC["ln_b"]:VC["ln_b"] + 1]).then_inc(S["gelu"], 1)

        @block.vector
        def _(v):
            step = Chain(v, S["steps"])
            for b2 in range(2):
                with v.Fori(0, CPI) as r, step.body(r, 1, CPI):
                    n = b2 * CPI + r + 1
                    v.wait_ge(S["mean_ps"], n)
                    v.tensor_tensor(cent, conv, p_mean, ALU.subtract).then_inc(S["cent"], 1)
                    v.wait_ge(S["root"], n)
                    step(v.reciprocal(inv, root))
                    v.tensor_tensor(z, cent, inv, ALU.mult).then_inc(S["z"], 1)
                    v.wait_ge(S["om_ps"], n)
                    v.tensor_tensor(om[:, bass.ds((r + b2 * CPI) * (2 * TPC), 2 * TPC), :]
                                    .rearrange("p (t h) n -> p t h n", h=2),
                                    p_om[:, :, 0:2 * OM].rearrange("p t (h n) -> p t h n", h=2),
                                    k["b_om"][:, :].unsqueeze(1).unsqueeze(1).to_broadcast([128, TPC, 2, OM]),
                                    ALU.add).then_inc(S["om"], 1)

        @block.gpsimd
        def _(pool):
            pool.memset(xq.rearrange("p b y x -> p (b y x)"), 0.0).then_inc(S["cleared"], 1)


def window_counts(nc, k, om):
    ctx, ps, st = k["ctx"], k["psum"], k["small"]
    S = {n: signal(k, "wide_" + n) for n in ("top", "turned", "steps", "flag")}
    with nc.Block() as block:
        @block.vector
        def _(v):
            step = Chain(v, S["steps"])
            v.tensor_reduce(st[:, 0:1], om[:, :, 0:2 * MG], AX.XY, ALU.max, apply_absolute_value=True)\
                .then_inc(S["top"], 1)
            v.wait_ge(S["turned"], 1)
            step(v.tensor_reduce(st[0:1, 1:2], ps[0:1, 0:128], AX.X, ALU.max))
            v.tensor_scalar(k["flag"][:, :], st[0:1, 1:2], 1.0, None, ALU.is_gt).then_inc(S["flag"], 1)

        @block.tensor
        def _(pe):
            pe.wait_ge(S["top"], 1)
            pe.transpose(ps[0:1, 0:128], st[:, 0:1], k["ident"][:, :]).then_inc(S["turned"], 1)


W = 5


def window_weights(nc, k, om, hp, hn, A, parts, rest, tmp):
    ctx = k["ctx"]
    S = {n: signal(k, "ww_" + n) for n in
         ("shifted", "exped", "steps", "hats", "ready", "prod", "used", "a", "part", "cleared")}
    M = 2 * NT
    TG = M * G
    logits = om[:, :, 2 * MG:OM].rearrange("p t (g s) -> p t g s", g=G)
    off = om[:, :, 0:2 * MG]
    hp3, hn3 = hp.rearrange("p (t n) -> p t n", t=M), hn.rearrange("p (t n) -> p t n", t=M)
    top = tmp[0][:, 0:TG].rearrange("p (t g) -> p t g", g=G)
    topb = top.unsqueeze(3).to_broadcast([128, M, G, TAPS])
    hats = [hn3, off, hp3]
    mask = om[:, :, 2 * MG:OM]
    A4 = A.rearrange("p (n u v) -> p n u v", u=W, v=W)
    pr = [t[:, 0:TG * TAPS].rearrange("p (n x y) -> p n x y", x=3, y=3) for t in tmp]

    def axis(h, a):
        return h.rearrange("p t (s a) -> p t s a", a=2)[:, :, :, a]

    def by_row(a, u):
        return a.rearrange("p (j n u v) -> p j n u v", n=2 * G, u=W, v=W)[:, :, :, u, :]

    POOLED = (1, 4, 7)
    with nc.Block() as block:
        @block.scalar
        def _(act):
            act.activation(hp3, off, ACT.Relu).then_inc(S["hats"], 1)
            act.activation(hn3, off, ACT.Relu, scale=-1.0).then_inc(S["hats"], 1)
            act.wait_ge(S["shifted"], 1)
            act.activation(mask, mask, ACT.Exp).then_inc(S["exped"], 1)
            for q in range(3):
                act.wait_ge(S["a"], q + 1)
                for u in range(W):
                    last = act.activation(parts[:, :, u, q, :, :], by_row((A, rest, A)[q], u), ACT.Copy)
                last.then_inc(S["part"], 1)

        @block.gpsimd
        def _(pool):
            pool.memset(A, 0.0).then_inc(S["cleared"], 1)
            pool.wait_ge(S["ready"], 1)
            for n, q in enumerate(POOLED):
                dy, dx = divmod(q, 3)
                if n:
                    pool.wait_ge(S["used"], n)
                pool.tensor_tensor(tmp[1][:, 0:TG * TAPS].rearrange("p (t s) -> p t s", s=MG),
                                   axis(hats[dy], 1), axis(hats[dx], 0), ALU.mult).then_inc(S["prod"], 1)

        @block.vector
        def _(v):
            step = Chain(v, S["steps"])
            step(v.tensor_reduce(top, logits, AX.X, ALU.max))
            v.tensor_tensor(logits, logits, topb, ALU.subtract).then_inc(S["shifted"], 1)
            v.wait_ge(S["hats"], 2)
            step(v.scalar_tensor_tensor(off, hp3, 1.0, hn3, ALU.subtract, ALU.add))
            step(v.tensor_scalar(off, off, -1.0, None, ALU.mult))
            v.wait_ge(S["exped"], 1)
            step(v.tensor_reduce(top, logits, AX.X, ALU.add))
            step(v.reciprocal(top, top))
            step(v.tensor_tensor(logits, logits, topb, ALU.mult))
            for n, h in enumerate(hats):
                ins = v.tensor_tensor(axis(h, 1), axis(h, 1), mask, ALU.mult)
            ins.then_inc(S["ready"], 1)
            v.wait_ge(S["ready"], 1)
            v.wait_ge(S["cleared"], 1)
            own = [q for q in range(9) if q not in POOLED]
            for n in range(9):
                q = own[n - (n + 1) // 3] if n % 3 != 2 else POOLED[n // 3]
                dy, dx = divmod(q, 3)
                if n % 3 == 2:
                    v.wait_ge(S["prod"], n // 3 + 1)
                    src = pr[1]
                else:
                    step(v.tensor_tensor(tmp[0][:, 0:TG * TAPS].rearrange("p (t s) -> p t s", s=MG),
                                         axis(hats[dy], 1), axis(hats[dx], 0), ALU.mult))
                    src = pr[0]
                dst = A4[:, :, dy:dy + 3, dx:dx + 3]
                add = v.tensor_tensor(dst, dst, src.rearrange("p n x y -> p n y x"), ALU.add)
                if n == 8:
                    add.then_inc(S["a"], 1)
                elif n % 3 == 2:
                    add.then_inc(S["used"], 1)
                    v.wait_ge(S["used"], n // 3 + 1)
                else:
                    step(add)
            for q in range(2):
                v.wait_ge(S["part"], q + 1)
                dst, src = ((rest, A), (A, rest))[q]
                for u in range(W):
                    last = v.tensor_tensor(by_row(dst, u), by_row(src, u), parts[:, :, u, q, :, :], ALU.subtract)
                last.then_inc(S["a"], 1)


def window_taps(nc, k, parts, att, pr, tail):
    ctx, ps, xq, x = k["ctx"], k["psum"], k["xproj"], k["x"]
    BF = mybir.dt.bfloat16
    S = {n: signal(k, "wt_" + n) for n in
         ("turned", "at", "spread", "prod", "sum1", "sum2", "acc", "gated", "added", "steps")}
    sel = k["sel"]
    R = 3 * 8 * W
    p_t = ps[0:R, 3072:4096].bitcast(BF).rearrange("p (n c) -> p n c", c=PT)
    p_b = [ps[:, 512 * v:512 * v + CH] for v in range(W)]
    p_y = ps[:, 2560:2560 + CH]
    prod = [[pr[:, (W * u + v) * CH:(W * u + v + 1) * CH] for v in range(W)] for u in range(W)]
    yb = [tail[:, CH * i:CH * i + CH] for i in range(2)]

    def turns(eng):
        for b2 in range(2):
            with eng.Fori(0, CPI) as r:
                yield b2, r, b2 * CPI + r + 1

    flat = parts.rearrange("p j u q n v -> p (j u q n v)")
    with nc.Block() as block:
        @block.gpsimd
        def _(pool):
            for b2, r, n in turns(pool):
                for u in range(W):
                    m = (n - 1) * W + (u + 1)
                    pool.wait_ge(S["prod"], (n - 1) * (W * W) + (W * u + 4 + W))
                    a = pr[:, W * u * CH:(W * u + 2) * CH]
                    pool.tensor_tensor(a, a, pr[:, (W * u + 2) * CH:(W * u + 4) * CH], ALU.add).then_inc(S["sum1"], 1)
                    pool.wait_ge(S["sum1"], m)
                    pool.tensor_tensor(prod[u][0], prod[u][0], prod[u][1], ALU.add).then_inc(S["sum2"], 1)

        @block.scalar
        def _(act):
            for b2, r, n in turns(act):
                act.wait_ge(S["turned"], n)
                act.wait_ge(S["spread"], (n - 1) * (W * W) + 1)
                act.activation(att[0:R, :].rearrange("p (n c) -> p n c", c=PT)[:, 0:15, :], p_t[:, 0:15, :],
                               ACT.Copy).then_inc(S["at"], 1)
                act.wait_ge(S["acc"], n * W + W)
                act.wait_ge(S["added"], n)
                act.activation(yb[0], p_y, ACT.Identity, scale=k["bn"][:, 2:3], bias=k["bn"][:, 5:6])
                act.activation(yb[1], p_y, ACT.Sigmoid, scale=k["bn"][:, 2:3], bias=k["bn"][:, 5:6])\
                    .then_inc(S["gated"], 1)

        @block.tensor
        def _(pe):
            pe.sem_inc(S["spread"], 1)
            pe.sem_inc(S["added"], 1)
            pe.sem_inc(S["prod"], W)
            pe.sem_inc(S["at"], 1)
            pe.sem_inc(S["gated"], 1)
            for b2, r, n in turns(pe):
                pe.wait_ge(S["at"], n)
                for t in range(TPC):
                    for u in range(W):
                        mm = pe.transpose(p_t[:, u * TPC + t, :], flat[:, bass.ds(r * (TPC * W * R) + (b2 * TPI + t) * (W * R) + u * R, R)],
                                          k["identb"][:, :])
                mm.then_inc(S["turned"], 1)
                pe.wait_ge(S["at"], n + 1)

                def gather_sums(u):
                    pe.wait_ge(S["sum2"], (n - 1) * W + (u + 1))
                    if u == 0:
                        pe.wait_ge(S["gated"], n)
                    pe.matmul(p_y, k["wout"][:, :], prod[u][0], start=(u == 0), stop=False)
                    pe.wait_ge(S["prod"], (n - 1) * (W * W) + (W * u + 5 + W))
                    mm = pe.matmul(p_y, k["wout"][:, :], prod[u][4], start=False, stop=(u == W - 1))
                    mm.then_inc(S["acc"], 1)

                for u in range(W):
                    for v in range(W):
                        c = (n - 1) * (W * W) + (W * u + v + 1)
                        pe.wait_ge(S["prod"], c)
                        pe.matmul(p_b[v], sel[0:R, v, :], att[0:R, CH * u:CH * u + CH], start=True, stop=True)\
                            .then_inc(S["spread"], 1)
                    if u >= 1:
                        gather_sums(u - 1)
                gather_sums(W - 1)

        @block.vector
        def _(v_):
            step = Chain(v_, S["steps"])
            v_.sem_inc(S["acc"], W)
            for b2 in range(2):
                with v_.Fori(0, CPI) as r, step.body(r, 1, CPI):
                    n = b2 * CPI + r + 1
                    for u in range(W):
                        v_.wait_ge(S["acc"], (n - 1) * W + (u + 1))
                        for v in range(W):
                            v_.wait_ge(S["spread"], (n - 1) * (W * W) + (W * u + v + 2))
                            v_.tensor_tensor(prod[u][v].rearrange("p (y x) -> p y x", y=ROWS),
                                             p_b[v].rearrange("p (y x) -> p y x", y=ROWS),
                                             xq[:, b2, bass.ds(r * ROWS + u, ROWS), v:v + WW], ALU.mult)\
                                .then_inc(S["prod"], 1)
                    v_.wait_ge(S["gated"], n + 1)
                    step(v_.tensor_tensor(yb[0], yb[0], yb[1], ALU.mult))
                    xs = x[:, bass.ds(r * CH + b2 * PIX, CH)]
                    v_.tensor_tensor(xs, xs, yb[0], ALU.add).then_inc(S["added"], 1)


def pixels_out(nc, k, tag, window, buf):
    ctx, ps = k["ctx"], k["psum"]
    xs, pp = buf[:, 0:CH], buf[:, CH:2 * CH]
    S = {n: signal(k, tag + "_" + n) for n in ("xs", "turned", "pp", "stored")}

    def turns(eng):
        for b2 in range(2):
            with eng.Fori(0, CPI) as r:
                yield b2, r, b2 * CPI + r + 1

    with nc.Block() as block:
        @block.vector
        def _(v):
            v.sem_inc(S["turned"], 1)
            for b2, r, n in turns(v):
                v.wait_ge(S["turned"], n)
                v.tensor_copy(xs.rearrange("p (y x) -> p y x", y=ROWS), window(b2, r)).then_inc(S["xs"], 1)

        @block.tensor
        def _(pe):
            pe.sem_inc(S["pp"], 1)
            for b2, r, n in turns(pe):
                pe.wait_ge(S["xs"], n)
                pe.wait_ge(S["pp"], n)
                for t in range(TPC):
                    mm = pe.transpose(ps[:, PT * t:PT * t + PT], xs[:, PT * t:PT * t + PT], k["ident"][:, :])
                mm.then_inc(S["turned"], 1)

        @block.scalar
        def _(act):
            for b2, r, n in turns(act):
                act.wait_ge(S["turned"], n + 1)
                act.wait_ge(S["stored"], 32 * n)
                act.activation(pp, ps[:, 0:CH], ACT.Copy).then_inc(S["pp"], 1)

        @block.sync
        def _(sp):
            sp.sem_inc(S["stored"], 32)
            store_pixels(sp, pp, k["xpd"], S["pp"], S["stored"], 1)


def store_pixels(sp, pp, xpd, ready, out, credit=0):
    for b2 in range(2):
        with sp.Fori(0, CPI) as r:
            sp.wait_ge(ready, b2 * CPI + r + 1 + credit)
            for h in range(2):
                sp.dma_start(xpd[2 * h + b2, bass.ds(r * TPC, TPC), :, :].rearrange("t p c -> p t c"),
                             pp.rearrange("p (t h c) -> p t h c", h=2, c=C)[:, :, h, :]).then_inc(out, 16)
    sp.wait_ge(out, 32 * (2 * CPI + 1))


def quads(nc, k, tag, groups):
    ctx = k["ctx"]
    A = k["arena"]
    n = C // groups
    rows = [A[0:2 * TR, 3200 * i:3200 * i + 3200].rearrange("p (x c) -> p x c", c=C) for i in range(2)]
    T = A[0:2 * TR, 6400:6400 + TR * 4 * C]
    T6 = T.rearrange("p (x g q n) -> p x g q n", g=groups, q=4, n=n)
    cleared = signal(k, tag + "_cleared")
    loaded = signal(k, tag + "_loaded")
    spread = signal(k, tag + "_spread")
    stored = signal(k, tag + "_stored")
    img = k["xpd"].rearrange("b t p c -> b (t p) c").rearrange("b (y x) c -> b y x c", y=HH)
    tab = k["tab"]

    def copy(eng, run, q):
        dy, dx = divmod(q, 2)
        return run(T6[:, :, :, q, :], rows[dy][:, dx:dx + TR, :].rearrange("p x (g n) -> p x g n", g=groups))

    with nc.Block() as block:
        @block.gpsimd
        def _(pool):
            pool.memset(A[0:2 * TR, 0:6400], 0.0).then_inc(cleared, 1)
            for bb in range(2):
                pool.wait_ge(loaded, 64 * (bb + 1))
                if bb:
                    pool.wait_ge(stored, 16 * bb)
                copy(pool, pool.tensor_copy, 0).then_inc(spread, 1)

        @block.scalar
        def _(act):
            for bb in range(2):
                act.wait_ge(loaded, 64 * (bb + 1))
                if bb:
                    act.wait_ge(stored, 16 * bb)
                copy(act, lambda o, i: act.activation(o, i, ACT.Copy), 1).then_inc(spread, 1)

        @block.vector
        def _(v):
            for bb in range(2):
                v.wait_ge(loaded, 64 * (bb + 1))
                if bb:
                    v.wait_ge(stored, 16 * bb)
                for q in (2, 3):
                    copy(v, v.tensor_copy, q).then_inc(spread, 1)

        @block.sync
        def _(sp):
            sp.wait_ge(cleared, 1)
            for bb in range(2):
                if bb:
                    sp.wait_ge(spread, 4 * bb)
                for dy in range(2):
                    for u in range(2):
                        sp.dma_start(rows[dy][TR * u + 1 - dy:TR * u + 1 - dy + HH, 1:WW + 1, :],
                                     img[2 * bb + u]).then_inc(loaded, 16)
                sp.wait_ge(spread, 4 * (bb + 1))
                sp.dma_start(tab[2 * TR * bb:2 * TR * bb + 2 * TR, :], T).then_inc(stored, 16)
            sp.wait_ge(stored, 32)


def places(nc, k, tag, om, base, goff, idx, frac, ns, xfirst, tmp, mask):
    ctx = k["ctx"]
    steps = signal(k, tag + "_steps")
    shifted = signal(k, tag + "_shifted")
    exped = signal(k, tag + "_exped")
    M = 2 * NT
    cf = frac[:, :, :]
    r1, r2 = tmp
    with nc.Block() as block:
        @block.vector
        def _(v):
            step = Chain(v, steps)
            if mask is not None:
                logits = om[:, :, 2 * MG:OM].rearrange("p t (g k) -> p t g k", g=G)
                m4 = mask[:, 0:M, :].rearrange("p t (g k) -> p t g k", g=G)
                top = r1[:, 0:M * G].rearrange("p (t g) -> p t g", g=G)
                topb = top.unsqueeze(3).to_broadcast([128, M, G, TAPS])
                step(v.tensor_reduce(top, logits, AX.X, ALU.max))
                v.tensor_tensor(m4, logits, topb, ALU.subtract).then_inc(shifted, 1)
                v.wait_ge(exped, 1)
                step(v.tensor_reduce(top, m4, AX.X, ALU.add))
                step(v.reciprocal(top, top))
                step(v.tensor_tensor(m4, m4, topb, ALU.mult))
            for b2 in range(2):
                for h in range(2):
                    o = om[:, :, 0:2 * ns].rearrange("p (b t h) n -> p b t h n", b=2, h=2)[:, b2, :, h, :]
                    f = cf.rearrange("p (b t h) n -> p b t h n", b=2, h=2)[:, b2, :, h, :]
                    last = v.tensor_tensor(f, o, base, ALU.add)
            step(last)
            flat = cf.rearrange("p t n -> p (t n)")
            a, b = r1[:, 0:M * 2 * ns], r2[:, 0:M * 2 * ns]
            step(v.tensor_scalar(flat, flat, float(PH - 1), 0.0, ALU.min, ALU.max))
            step(v.tensor_scalar(a, flat, ROUND, ROUND, ALU.add, ALU.subtract))
            step(v.tensor_tensor(b, a, flat, ALU.is_gt))
            step(v.tensor_tensor(a, a, b, ALU.subtract))
            step(v.tensor_scalar(a, a, float(PH - 2), None, ALU.min))
            step(v.tensor_tensor(flat, flat, a, ALU.subtract))
            ax = a.rearrange("p (t n a) -> p t n a", n=ns, a=2)
            y0, x0 = (ax[:, :, :, 1], ax[:, :, :, 0]) if xfirst else (ax[:, :, :, 0], ax[:, :, :, 1])
            lin = b[:, 0:M * ns].rearrange("p (t n) -> p t n", n=ns)
            step(v.scalar_tensor_tensor(lin, y0, float(TR), x0, ALU.mult, ALU.add))
            for b2 in range(2):
                for h in range(2):
                    src = lin.rearrange("p (b t h) n -> p b t h n", b=2, h=2)[:, b2, :, h, :]
                    dst = idx[:, 0:M, :].rearrange("p (b t h) n -> p b t h n", b=2, h=2)[:, b2, :, h, :]
                    gb = goff[:, 2 * h + b2, :].unsqueeze(1).to_broadcast([128, TPI, ns])
                    v.scalar_tensor_tensor(dst, src, float(G if mask is not None else 1), gb, ALU.mult, ALU.add)
            v.memset(idx[:, M:M + 2, :], 0)

        if mask is not None:
            @block.scalar
            def _(act):
                act.wait_ge(shifted, 1)
                fl = mask[:, 0:M, :].rearrange("p t n -> p (t n)")
                act.activation(fl, fl, ACT.Exp).then_inc(exped, 1)


def sample(nc, k, tag, idx, frac, mask, ns, xfirst, row, first):
    ctx, ps = k["ctx"], k["psum"]
    A = k["arena"]
    gat = [A[:, ns * row * i:ns * row * (i + 1)].rearrange("p (s n) -> p s n", s=ns) for i in range(2)]
    at = 2 * ns * row
    w4 = A[:, at:at + 2 * ns * 4].rearrange("p (h s q) -> p h s q", h=2, q=4)
    at += 8 * ns
    S = {n: signal(k, f"{tag}_{n}") for n in
         ("idx0", "idx1", "got0", "got1", "turn", "summed0", "summed1", "turned", "turned_sb",
          "taken", "prod", "act", "add", "steps", "steps_act")}
    stage = k["istage"]
    table = k["tab"].rearrange("r (i n) -> (r i) n", n=row)
    sumw = 128 if first else ns * C
    n_sum = 1 if first else 2
    acc = A[:, at:at + n_sum * sumw].rearrange("p (u n) -> p u n", u=n_sum)
    at += n_sum * sumw
    turned = A[:, at:at + (128 if first else TAPS * 128)]
    at += 128 if first else TAPS * 128
    yb = A[:, at:at + 256]

    def tile(i, h):
        return bass.ds(i * 2 + h, 1)

    with nc.Block() as block:
        @block.gpsimd
        def _(pool):
            with pool.Fori(0, NT) as i:
                for h in range(2):
                    pool.wait_ge(S[f"summed{h}"], i + 1)
                    pool.wait_ge(S[f"idx{h}"], i + 1)
                    pool.sem_inc(S["turn"], 1)
                    for s in range(ns):
                        pool.indirect_dma_start(
                            out=gat[h][:, s, :], out_offset=None, in_=table,
                            in_offset=bass.IndirectOffsetOnAxis(ap=stage[:, h, s:s + 1], axis=0)
                        ).then_inc(S[f"got{h}"], 16)

        @block.vector
        def _(v):
            step = Chain(v, S["steps"])
            for h in range(2):
                v.sem_inc(S[f"summed{h}"], 1)
                v.tensor_copy(stage[:, h, 0:ns], idx[:, h, :]).then_inc(S[f"idx{h}"], 1)
            per = 6 + 2
            with v.Fori(0, NT) as i, step.body(i, per, NT):
                f4 = frac[:, bass.ds(i * 2, 2), :].rearrange("p t (s a) -> p t s a", a=2)
                wy, wx = (f4[:, :, :, 1], f4[:, :, :, 0]) if xfirst else (f4[:, :, :, 0], f4[:, :, :, 1])
                m = mask[:, bass.ds(i * 2, 2), :] if first else k["ones"][:, 0:1].unsqueeze(2).to_broadcast([128, 2, ns])
                w = [w4[:, :, :, q] for q in range(4)]
                step(v.tensor_tensor(w[2], m, wy, ALU.mult))
                step(v.tensor_tensor(w[0], m, w[2], ALU.subtract))
                step(v.tensor_tensor(w[3], w[2], wx, ALU.mult))
                step(v.tensor_tensor(w[1], w[0], wx, ALU.mult))
                step(v.tensor_tensor(w[2], w[2], w[3], ALU.subtract))
                step(v.tensor_tensor(w[0], w[0], w[1], ALU.subtract))
                for h in range(2):
                    v.wait_ge(S[f"got{h}"], (i + 1) * (16 * ns))
                    v.tensor_copy(stage[:, h, 0:ns], idx[:, tile(i + 1, h), :].rearrange("p a s -> p (a s)"))\
                        .then_inc(S[f"idx{h}"], 1)
                    n = row // 4
                    g4 = gat[h].rearrange("p s (q n) -> p (s q) n", n=n)
                    wb = w4[:, h, :, :].rearrange("p s q -> p (s q)").unsqueeze(2).to_broadcast([128, 4 * ns, n])
                    step(v.tensor_tensor(g4, g4, wb, ALU.mult))
                    if first:
                        if h == 0:
                            v.wait_ge(S["taken"], i + 1)
                        v.tensor_reduce(
                            acc[:, 0, 64 * h:64 * h + 64].rearrange("p (g n) -> p g n", g=G),
                            gat[h].rearrange("p (g s) (q n) -> p g n (s q)", g=G, n=n), AX.X, ALU.add)\
                            .then_inc(S[f"summed{h}"], 1)
                    else:
                        v.wait_ge(S["taken"], i * 2 + h + 1)
                        v.tensor_reduce(acc[:, h, :].rearrange("p (s n) -> p s n", n=C),
                                        gat[h].rearrange("p s (q n) -> p s n q", n=n), AX.X, ALU.add)\
                            .then_inc(S[f"summed{h}"], 1)
                if first:
                    v.wait_ge(S["act"], i + 1)
                    xs = k["x"][:, bass.ds(i * PT, PT)]
                    v.tensor_tensor(yb[:, 0:128], yb[:, 0:128], yb[:, 128:256], ALU.mult).then_inc(S["prod"], 1)
                    v.wait_ge(S["prod"], i + 1)
                    v.tensor_tensor(xs, xs, yb[:, 0:128], ALU.add).then_inc(S["add"], 1)

        if first:
            @block.tensor
            def _(pe):
                pe.sem_inc(S["taken"], 1)
                with pe.Fori(0, NT) as i:
                    pe.wait_ge(S["summed0"], i + 2)
                    pe.wait_ge(S["summed1"], i + 2)
                    pe.transpose(ps[:, 0:128], acc[:, 0, :], k["ident"][:, :]).then_inc(S["taken"], 1)
                    pe.wait_ge(S["turned_sb"], i + 1)
                    pe.matmul(ps[:, 512:640], k["wout"][:, :], turned, start=True, stop=True)\
                        .then_inc(S["turned"], 1)

            @block.scalar
            def _(act):
                act.sem_inc(S["add"], 1)
                with act.Fori(0, NT) as i:
                    act.wait_ge(S["taken"], i + 2)
                    act.activation(turned, ps[:, 0:128], ACT.Copy).then_inc(S["turned_sb"], 1)
                    act.wait_ge(S["turned"], i + 1)
                    act.wait_ge(S["add"], i + 1)
                    act.activation(yb[:, 0:128], ps[:, 512:640], ACT.Identity, scale=k["bn"][:, 2:3],
                                   bias=k["bn"][:, 5:6])
                    act.activation(yb[:, 128:256], ps[:, 512:640], ACT.Sigmoid, scale=k["bn"][:, 2:3],
                                   bias=k["bn"][:, 5:6]).then_inc(S["act"], 1)
        else:
            sc = k["sc"]

            @block.tensor
            def _(pe):
                pe.sem_inc(S["taken"], 2)
                with pe.Fori(0, NT) as i:
                    for h in range(2):
                        n = i * 2 + h + 1
                        pe.wait_ge(S[f"summed{h}"], i + 2)
                        for m in range(TAPS):
                            mm = pe.transpose(ps[:, 128 * m:128 * m + 128], acc[:, h, 128 * m:128 * m + 128],
                                              k["ident"][:, :])
                        mm.then_inc(S["taken"], 1)
                        pe.wait_ge(S["turned_sb"], n)
                        for m in range(TAPS):
                            mm = pe.matmul(ps[:, 2048:2176], k["dws"][:, m, :], turned[:, 128 * m:128 * m + 128],
                                           start=(m == 0), stop=(m == TAPS - 1))
                        mm.then_inc(S["prod"], 1)

            @block.scalar
            def _(act):
                with act.Fori(0, NT) as i:
                    for h in range(2):
                        n = i * 2 + h + 1
                        act.wait_ge(S["taken"], n + 2)
                        act.activation(turned, ps[:, 0:TAPS * 128], ACT.Copy).then_inc(S["turned_sb"], 1)
                        act.wait_ge(S["prod"], n)
                        act.activation(sc[:, h, bass.ds(i * PT, PT)], ps[:, 2048:2176], ACT.Identity,
                                       bias=k["dbs"][:, 0:1])


def offsets1(nc, k, om):
    ctx, ps, xp, xn = k["ctx"], k["psum"], k["xp"], k["xn"]
    big = k["work1"]
    off, xs, pp = (big[:, CH * i:CH * i + CH] for i in range(3))
    NO = 4 * S1
    S = {n: signal(k, "off1_" + n) for n in
         ("conv_ps", "conv", "om_ps", "om", "xs", "turn_ps", "pp", "stored")}
    p_conv = ps[0:NO, 0:CH]
    p_om = ps[:, 512:512 + TPC * NO]
    p_x = ps[:, 1024:1024 + CH]

    def turns(eng):
        for b2 in range(2):
            with eng.Fori(0, CPI) as r:
                yield b2, r, b2 * CPI + r + 1

    with nc.Block() as block:
        @block.tensor
        def _(pe):
            pe.sem_inc(S["om"], 1)
            for b2, r, n in turns(pe):
                pe.wait_ge(S["om"], n)
                for t in range(TAPS):
                    mm = pe.matmul(p_conv.rearrange("p (y x) -> p y x", y=ROWS), k["offw"][:, t, :],
                                   chunk_window(xp, b2, r, t), start=(t == 0), stop=(t == TAPS - 1))
                mm.then_inc(S["conv_ps"], 1)
                pe.wait_ge(S["xs"], n)
                for t in range(TPC):
                    mm = pe.transpose(p_x[:, PT * t:PT * t + PT], xs[:, PT * t:PT * t + PT], k["ident"][:, :])
                mm.then_inc(S["turn_ps"], 1)
                pe.wait_ge(S["conv"], n)
                for t in range(TPC):
                    mm = pe.transpose(p_om[:, NO * t:NO * t + NO], off[0:NO, PT * t:PT * t + PT],
                                      k["ident"][0:NO, 0:NO])
                mm.then_inc(S["om_ps"], 1)

        @block.scalar
        def _(act):
            for b2, r, n in turns(act):
                act.wait_ge(S["conv_ps"], n)
                act.activation(off[0:NO, :], p_conv, ACT.Identity, bias=k["offb"][:, 0:1]).then_inc(S["conv"], 1)
                act.wait_ge(S["turn_ps"], n)
                act.wait_ge(S["stored"], 32 * n)
                act.activation(pp, p_x, ACT.Copy).then_inc(S["pp"], 1)

        @block.vector
        def _(v):
            for b2, r, n in turns(v):
                v.tensor_copy(xs, xn[:, bass.ds(r * CH + b2 * PIX, CH)]).then_inc(S["xs"], 1)
                v.wait_ge(S["om_ps"], n)
                v.wait_ge(S["pp"], n)
                v.tensor_copy(om[:, bass.ds((r + b2 * CPI) * (2 * TPC), 2 * TPC), :]
                              .rearrange("p t n -> p (t n)"), p_om).then_inc(S["om"], 1)

        @block.sync
        def _(sp):
            sp.sem_inc(S["stored"], 32)
            store_pixels(sp, pp, k["xpd"], S["pp"], S["stored"])


def fuse1(nc, k):
    ctx, ps = k["ctx"], k["psum"]
    sc, xn, x, st = k["sc"], k["xn"], k["x"], k["small"]
    S = {n: signal(k, "fuse_" + n) for n in
         ("v", "pe", "act", "steps", "mix_ps", "mixed", "gated", "cleared", "gsteps")}
    pool4, gm = st[:, 0:4], st[:, 4:6]
    h8, lg, wts = st[0:8, 8:12], st[0:4, 12:14], st[0:4, 16:18]
    wide = k["wide"]
    g1, g2, gate = st[0:32, 20:24], st[0:32, 24:28], st[:, 28:32]
    mixw = k["mixw"]
    with nc.Block() as block:
        @block.vector
        def _(v):
            step = Chain(v, S["steps"])
            v.memset(k["mixw_flat"], 0.0)
            step(v.tensor_reduce(pool4, sc.rearrange("p h (b n) -> p (h b) n", b=2), AX.X, ALU.add))
            step(v.tensor_reduce(gm, xn[:, :].rearrange("p (b n) -> p b n", b=2), AX.X, ALU.add))
            v.tensor_scalar(st[:, 0:6], st[:, 0:6], 1.0 / PIX, None, ALU.mult).then_inc(S["v"], 1)
            v.wait_ge(S["pe"], 2)
            step(v.tensor_tensor(lg, ps[0:4, 2048:2050], k["wgb2"][:, :], ALU.add))
            step(v.tensor_reduce(st[0:4, 14:15], lg, AX.X, ALU.max, negate=True))
            v.tensor_scalar(lg, lg, st[0:4, 14:15], None, ALU.add).then_inc(S["v"], 1)
            v.wait_ge(S["act"], 2)
            step(v.tensor_reduce(st[0:4, 14:15], wts, AX.X, ALU.add))
            step(v.reciprocal(st[0:4, 15:16], st[0:4, 14:15]))
            step(v.tensor_scalar(wts, wts, st[0:4, 15:16], None, ALU.mult))
            v.tensor_copy(wide[:, :].rearrange("b (v c) -> b v c", v=2),
                          wts.unsqueeze(2).to_broadcast([4, 2, C])).then_inc(S["v"], 1)
            v.wait_ge(S["pe"], 3)
            step(v.tensor_copy(st[:, 32:36], ps[:, 2560:2564]))
            for b in range(NB):
                h = b // 2
                last = v.tensor_scalar(mixw[:, b, 64 * h:64 * h + 64], k["stack2"][:, :], st[:, 32 + b:33 + b],
                                       None, ALU.mult)
            last.then_inc(S["v"], 1)
            v.wait_ge(S["act"], 5)
            for b2 in range(2):
                with v.Fori(0, CPI) as r, step.body(r, 1, CPI):
                    n = b2 * CPI + r + 1
                    v.wait_ge(S["gated"], n)
                    v.wait_ge(S["mix_ps"], n)
                    xs = x[:, bass.ds(r * CH + b2 * PIX, CH)]
                    step(v.tensor_tensor(xs, xs, ps[:, 512:512 + CH], ALU.add))
                    v.tensor_tensor(xs, xs, k["gx"][:, :], ALU.add).then_inc(S["mixed"], 1)

        @block.tensor
        def _(pe):
            pe.wait_ge(S["v"], 1)
            pe.matmul(ps[0:8, 0:4], k["wg1T"][:, :], pool4, start=True, stop=True)
            for h in range(2):
                mm = pe.matmul(ps[0:32, 512 * (2 + h):512 * (2 + h) + 2], k["gp1T"][64 * h:64 * h + 64, :],
                               gm[64 * h:64 * h + 64, :], start=True, stop=True)
            mm.then_inc(S["pe"], 1)
            pe.wait_ge(S["act"], 1)
            pe.matmul(ps[0:4, 2048:2050], h8, k["wg2T"][:, :], start=True, stop=True).then_inc(S["pe"], 1)
            pe.wait_ge(S["v"], 3)
            pe.matmul(ps[:, 2560:2564], wide[:, :], k["ident"][0:4, 0:4], start=True, stop=True).then_inc(S["pe"], 1)
            pe.wait_ge(S["act"], 3)
            pe.matmul(ps[0:32, 3072:3076], k["gp2T"][:, :], g1, start=True, stop=True).then_inc(S["pe"], 1)
            pe.wait_ge(S["act"], 4)
            pe.matmul(ps[:, 3584:3588], k["gp3T"][:, :], g2, start=True, stop=True).then_inc(S["pe"], 1)
            pe.wait_ge(S["v"], 4)
            pe.sem_inc(S["mixed"], 1)
            for b2 in range(2):
                with pe.Fori(0, CPI) as r:
                    n = b2 * CPI + r + 1
                    pe.wait_ge(S["mixed"], n)
                    for h in range(2):
                        pe.matmul(ps[:, 512:512 + CH], mixw[:, 2 * h + b2, :],
                                  sc[:, h, bass.ds(r * CH + b2 * PIX, CH)], start=(h == 0), stop=(h == 1))
                    pe.matmul(ps[:, 1024:1024 + CH], k["crT"][:, :], xn[:, bass.ds(r * CH + b2 * PIX, CH)],
                              start=True, stop=True).then_inc(S["mix_ps"], 1)

        @block.scalar
        def _(act):
            act.wait_ge(S["pe"], 1)
            act.activation(g1[:, 0:2], ps[0:32, 1024:1026], ACT.Relu, bias=k["gpb1"][:, 0:1])
            act.activation(g1[:, 2:4], ps[0:32, 1536:1538], ACT.Relu, bias=k["gpb1"][:, 0:1])
            act.activation(h8, ps[0:8, 0:4], ACT.Relu, bias=k["wgb1"][:, 0:1]).then_inc(S["act"], 1)
            act.wait_ge(S["v"], 2)
            act.activation(wts, lg, ACT.Exp).then_inc(S["act"], 1)
            act.wait_ge(S["pe"], 3)
            act.sem_inc(S["act"], 1)
            act.wait_ge(S["pe"], 4)
            act.activation(g2, ps[0:32, 3072:3076], ACT.Relu, bias=k["gpb2"][:, 0:1]).then_inc(S["act"], 1)
            act.wait_ge(S["pe"], 5)
            act.activation(gate, ps[:, 3584:3588], ACT.Sigmoid,
                           bias=k["vec"][:, VC["gp_b3"]:VC["gp_b3"] + 1]).then_inc(S["act"], 1)
            act.wait_ge(S["act"], 5)
            for b2 in range(2):
                for h in range(2):
                    r = slice(64 * h, 64 * h + 64)
                    act.activation(st[r, 36 + b2:37 + b2], gate[r, 2 * h + b2:2 * h + b2 + 1], ACT.Copy)\
                        .then_inc(S["gsteps"], 1)
            act.wait_ge(S["gsteps"], 4)
            act.activation(st[:, 38:40], st[:, 36:38], ACT.Copy,
                           scale=k["vec"][:, VC["cr_b"]:VC["cr_b"] + 1]).then_inc(S["gsteps"], 1)
            act.wait_ge(S["gsteps"], 5)
            for b2 in range(2):
                with act.Fori(0, CPI) as r:
                    n = b2 * CPI + r + 1
                    act.wait_ge(S["mix_ps"], n)
                    act.activation(k["gx"][:, :], ps[:, 1024:1024 + CH], ACT.Identity,
                                   scale=st[:, 36 + b2:37 + b2], bias=st[:, 38 + b2:39 + b2])\
                        .then_inc(S["gated"], 1)


def project2(nc, k, y, t1, t2, parts, at):
    ctx, ps, xn = k["ctx"], k["psum"], k["xn"]
    xs, ya, ta = (k["work2"][:, CH * i:CH * i + CH] for i in range(3))
    S = {n: signal(k, "proj2_" + n) for n in
         ("xs", "ps", "done", "biased", "steps", "part", "rest", "ones")}
    al = k["alphas"]
    with nc.Block() as block:
        @block.gpsimd
        def _(pool):
            pool.memset(at[:, :, C:2 * C], 1.0)
            pool.sem_inc(S["done"], 1)
            for b2 in range(2):
                with pool.Fori(0, CPI) as r:
                    n = b2 * CPI + r + 1
                    pool.wait_ge(S["done"], n)
                    pool.tensor_copy(xs, xn[:, bass.ds(r * CH + b2 * PIX, CH)]).then_inc(S["xs"], 1)

        @block.tensor
        def _(pe):
            for b2 in range(2):
                with pe.Fori(0, CPI) as r:
                    n = b2 * CPI + r + 1
                    pe.wait_ge(S["xs"], n)
                    pe.matmul(ps[:, 0:CH], k["l2w"][:, :], xs, start=True, stop=True)
                    for t in range(TPC):
                        mm = pe.matmul(ps[:, 512 + PT * t:512 + PT * t + PT], xs[:, PT * t:PT * t + PT],
                                       k["waT"][:, :], start=True, stop=True)
                    mm.then_inc(S["ps"], 1)

        @block.scalar
        def _(act):
            for b2 in range(2):
                with act.Fori(0, CPI) as r:
                    n = b2 * CPI + r + 1
                    act.wait_ge(S["ps"], n)
                    act.activation(y[:, bass.ds(r * CH + b2 * PIX, CH)], ps[:, 0:CH], ACT.Identity,
                                   bias=k["l2b"][:, 0:1]).then_inc(S["biased"], 1)
            for q in range(3):
                act.wait_ge(S["rest"], q + 1)
                act.activation(parts[q], (y, t1, t2)[q], ACT.Copy).then_inc(S["part"], 1)

        @block.vector
        def _(v):
            step = Chain(v, S["steps"])
            for b2 in range(2):
                with v.Fori(0, CPI) as r, step.body(r, 2, CPI):
                    n = b2 * CPI + r + 1
                    v.wait_ge(S["ps"], n)
                    step(v.tensor_tensor(ya.rearrange("p (t c) -> p t c", c=C),
                                         ps[:, 512:512 + CH].rearrange("p (t c) -> p t c", c=C),
                                         k["ba"][:, :].unsqueeze(1).to_broadcast([128, 2 * TPC, C]), ALU.add))
                    step(v.tensor_scalar(ta, ya, 0.0, al[:, 1:2], ALU.min, ALU.mult))
                    v.wait_ge(S["biased"], n)
                    for h in range(2):
                        y3 = ya.rearrange("p (t h c) -> p t h c", h=2, c=C)[:, :, h, :]
                        t3 = ta.rearrange("p (t h c) -> p t h c", h=2, c=C)[:, :, h, :]
                        last = v.scalar_tensor_tensor(at[:, bass.ds((r + b2 * CPI) * TPC, TPC), 2 * C * h:2 * C * h + C],
                                                      y3, 0.0, t3, ALU.max, ALU.add)
                    last.then_inc(S["done"], 1)
            step(v.tensor_scalar(t1, y, 0.0, al[:, 0:1], ALU.min, ALU.mult))
            v.scalar_tensor_tensor(y, y, 0.0, t1, ALU.max, ALU.add).then_inc(S["rest"], 1)
            v.wait_ge(S["part"], 1)
            v.tensor_tensor(t1, y, parts[0], ALU.subtract).then_inc(S["rest"], 1)
            v.wait_ge(S["part"], 2)
            v.tensor_tensor(t2, t1, parts[1], ALU.subtract).then_inc(S["rest"], 1)


def stack2(nc, k, parts, qa, ka, qb, kb):
    ctx = k["ctx"]
    stacked = signal(k, "stacked")
    H_, M_, L_ = 0, 1, 2
    plan = [(qa, 0, (H_, H_, M_)), (ka, 1, (H_, M_, H_)), (qb, 0, (M_, L_, H_)), (kb, 1, (M_, H_, L_))]
    with nc.Block() as block:
        def moves(eng, b2):
            for dst, e, order in plan:
                for pos, q in enumerate(order):
                    for h in range(2):
                        u = 2 * b2 + h
                        eng.dma_start(dst[HID * pos:HID * pos + HID, PIX * u:PIX * u + PIX],
                                      parts[q][64 * h + HID * e:64 * h + HID * e + HID, PIX * b2:PIX * b2 + PIX])\
                            .then_inc(stacked, 16)

        @block.sync
        def _(sp):
            moves(sp, 0)
            sp.wait_ge(stacked, 16 * 48)

        @block.scalar
        def _(act):
            moves(act, 1)

        @block.gpsimd
        def _(pool):
            pool.memset(ka[96:99, :], 1.0)


def attend2(nc, k, qa, ka, qb, kb, at):
    ctx, ps, x = k["ctx"], k["psum"], k["x"]
    A = k["atwork"]
    BF = mybir.dt.bfloat16
    SLOTS = 3
    pt = [A[:, CH * i:CH * i + CH] for i in range(SLOTS)]
    recs = [A[:, (SLOTS + i) * CH:(SLOTS + i + 1) * CH] for i in range(2)]
    at0 = (SLOTS + 2) * CH
    part = A[:, at0:at0 + 18]
    mx = A[:, at0 + 18:at0 + 36]
    rest = A[:, at0 + 36:at0 + 72]
    mparts = A[:, at0 + 72:at0 + 99].bitcast(BF)
    mrow = A[:, at0 + 100:at0 + 164].bitcast(BF)
    S = {n: signal(k, "att_" + n) for n in
         ("scores", "probs", "pv", "maxmm", "maxred", "steps", "mparts", "mrow_ps", "mrow", "mset", "added")}
    KA, KB = 3 * HID + 3, 3 * HID
    NJ = TPI
    NS, NM = 3, 3
    p_s = [ps[:, 512 * i:512 * i + CH] for i in range(NS)]
    p_m = [ps[:, 512 * (NS + i):512 * (NS + i) + CH] for i in range(NM)]
    p_o = [ps[:, 3072 + 512 * i:3072 + 512 * i + CH] for i in range(2)]
    p_r = ps[0:3 * NJ, 512 * NS:512 * NS + 64].bitcast(BF)

    def blocks(eng):
        with eng.Fori(0, CPI // 2) as i:
            for par in range(2):
                yield i * 2 + par, par

    def last_step(u, ib):
        return ib * NJ + (u * CPI + 1) * NJ

    with nc.Block() as block:
        @block.gpsimd
        def _(pool):
            pool.memset(k["xp_flat"], 0.0)

        @block.sync
        def _(sp):
            for u in range(NB):
                sp.wait_ge(S["mrow"], u + 1)
                for q in range(3):
                    sp.dma_start(qa[96 + q:97 + q, PIX * u:PIX * u + PIX], mrow[NJ * q:NJ * q + NJ, :])\
                        .then_inc(S["mset"], 16)

        @block.tensor
        def _(pe):
            def maxima(u, ib, j):
                n = ib * NJ + (u * CPI * NJ + j + 1)
                pe.wait_ge(S["maxred"], n)
                pe.matmul(p_m[j % NM], qa[0:KB, bass.ds(ib * CH + (u * PIX + PT * (j // 6)), PT)],
                          ka[0:KB, u * PIX + CH * (j % 6):u * PIX + CH * (j % 6) + CH],
                          start=True, stop=True).then_inc(S["maxmm"], 1)

            def maxrow(u):
                pe.wait_ge(S["mparts"], u + 1)
                pe.transpose(p_r, mparts, k["identb"][:, :]).then_inc(S["mrow_ps"], 1)

            def scores(u, ib, j):
                n = ib * NJ + (u * CPI * NJ + j + 1)
                pe.wait_ge(S["probs"], n)
                q = bass.ds(ib * CH + u * PIX, CH)
                kk = slice(u * PIX + PT * j, u * PIX + PT * j + PT)
                pe.matmul(p_s[j % NS], ka[0:KA, kk], qa[0:KA, q], start=True, stop=False)
                pe.matmul(p_s[j % NS], kb[0:KB, kk], qb[0:KB, q], start=False, stop=True)\
                    .then_inc(S["scores"], 1)

            def values(u, ib, par, j):
                n = ib * NJ + (u * CPI * NJ + j + 1)
                pe.wait_ge(S["probs"], n + NS)
                h, b2 = u % 2, u // 2
                pe.matmul(p_o[par], at[:, b2 * TPI + j, C * h:C * h + 2 * C], pt[j % SLOTS],
                          start=(j == 0), stop=(j == NJ - 1)).then_inc(S["pv"], 1)

            pe.sem_inc(S["maxred"], NM)
            pe.sem_inc(S["probs"], NS)
            pe.sem_inc(S["pv"], SLOTS)
            pe.sem_inc(S["added"], 2)
            with pe.Fori(0, CPI) as ib:
                for j in range(NJ):
                    maxima(0, ib, j)
            maxrow(0)
            for u in range(NB):
                pe.wait_ge(S["mset"], 48 * (u + 1))
                for ib, par in blocks(pe):
                    scores(u, ib, 0)
                    for j in range(NJ):
                        if j + 1 < NJ:
                            scores(u, ib, j + 1)
                        if u + 1 < NB:
                            maxima(u + 1, ib, j)
                        if j == 1:
                            pe.wait_ge(S["added"], ib + (u * CPI + 1))
                        if j >= 1:
                            values(u, ib, par, j - 1)
                    values(u, ib, par, NJ - 1)
                if u + 1 < NB:
                    maxrow(u + 1)

        @block.scalar
        def _(act):
            for u in range(NB):
                with act.Fori(0, CPI) as ib:
                    for j in range(NJ):
                        n = ib * NJ + (u * CPI * NJ + j + 1)
                        act.wait_ge(S["scores"], n)
                        act.wait_ge(S["pv"], n)
                        act.activation(pt[j % SLOTS], p_s[j % NS], ACT.Exp).then_inc(S["probs"], 1)

        @block.vector
        def _(v):
            step = Chain(v, S["steps"])

            def maxima(u, ib):
                for j in range(NJ):
                    v.wait_ge(S["maxmm"], ib * NJ + (u * CPI * NJ + j + 1))
                    v.tensor_reduce(part[:, j:j + 1], p_m[j % NM], AX.X, ALU.max).then_inc(S["maxred"], 1)
                v.wait_ge(S["maxred"], last_step(u, ib) + NM)
                step(v.tensor_reduce(mx[:, bass.ds(ib * 3, 3)], part.rearrange("p (i c) -> p i c", c=6), AX.X,
                                     ALU.max, negate=True))

            def split_maxima(u):
                m = [mparts[:, NJ * q:NJ * q + NJ] for q in range(3)]
                step(v.tensor_copy(m[0], mx))
                step(v.tensor_tensor(rest[:, 0:NJ], mx, m[0], ALU.subtract))
                step(v.tensor_copy(m[1], rest[:, 0:NJ]))
                step(v.tensor_tensor(rest[:, NJ:2 * NJ], rest[:, 0:NJ], m[1], ALU.subtract))
                v.tensor_copy(m[2], rest[:, NJ:2 * NJ]).then_inc(S["mparts"], 1)
                v.wait_ge(S["mrow_ps"], u + 1)
                if u:
                    v.wait_ge(S["mset"], 48 * u)
                v.tensor_copy(mrow[0:3 * NJ, :], p_r).then_inc(S["mrow"], 1)

            with v.Fori(0, CPI) as ib, step.body(ib, 1, CPI):
                maxima(0, ib)
            split_maxima(0)
            for u in range(NB):
                h, b2 = u % 2, u // 2
                more = u + 1 < NB
                per = 3 if more else 2
                start = step.n
                for ib, par in blocks(v):
                    step.off, step.n = ib * per + start, 0
                    if more:
                        maxima(u + 1, ib)
                    v.wait_ge(S["pv"], last_step(u, ib) + SLOTS)
                    own, other = slice(64 * h, 64 * h + 64), slice(64 - 64 * h, 128 - 64 * h)
                    rec = recs[par]
                    v.wait_ge(S["added"], ib + (u * CPI + 1))
                    step(v.reciprocal(rec[own, :], p_o[par][other, :]))
                    step(v.tensor_tensor(rec[own, :], rec[own, :], p_o[par][own, :], ALU.mult))
                    xs = x[own, bass.ds(ib * CH + b2 * PIX, CH)]
                    v.tensor_tensor(xs, xs, rec[own, :], ALU.add).then_inc(S["added"], 1)
                step.off, step.n = 0, start + per * CPI
                if more:
                    split_maxima(u + 1)


def dynamic3(nc, k):
    ctx, ps, x, xn, xp, d = k["ctx"], k["psum"], k["x"], k["xn"], k["xp"], k["dram"]
    A = k["arena"]
    QO = C // 4
    n_w = QO * TAPS * HID
    w2, prod = A[:, 0:2 * n_w], A[:, 2 * n_w:3 * n_w]
    at = 3 * n_w
    gen = A[:, at:at + NB * TAPS * 32].rearrange("p (b t o) -> p b t o", b=NB, t=TAPS)
    at += NB * TAPS * 32
    b2t = A[:, at:at + 32 * TAPS]
    at += 32 * TAPS
    wbd = A[:, at:at + 2 * TAPS * 128].rearrange("p (b t o) -> p b t o", b=2, t=TAPS)
    at += 2 * TAPS * 128
    hb = A[:, at:at + NB * HID].rearrange("p (b n) -> p b n", b=NB)
    at += NB * HID
    pw = A[:, at:at + 2 * 128].rearrange("p (b n) -> p b n", b=2)
    at += 256
    gm = k["small"][:, 4:6]
    S = {n: signal(k, "dyn_" + n) for n in
         ("w2", "steps", "pooled", "h_ps", "gen", "cleared", "moved", "conv_ps", "added", "stored")}
    with nc.Block() as block:
        @block.gpsimd
        def _(pool):
            pool.memset(wbd.rearrange("p b t o -> p (b t o)"), 0.0).then_inc(S["cleared"], 1)

        @block.sync
        def _(sp):
            for half in range(2):
                sp.dma_start(w2[64 * half:64 * half + 64, :].rearrange("c (o n) -> c o n", o=32),
                             d["W2"].rearrange("(a o c t) n -> a c o (t n)", a=2, c=C, t=TAPS)[half])\
                    .then_inc(S["w2"], 16)
                sp.dma_start(b2t[64 * half:64 * half + 64, :].rearrange("c (o n) -> c o n", o=32),
                             d["b2"].rearrange("(a o c t) -> a c o t", a=2, c=C, t=TAPS)[half])\
                    .then_inc(S["w2"], 16)
            sp.wait_ge(S["cleared"], 1)
            for b in range(NB):
                sp.wait_ge(S["gen"], b + 1)
                h = b // 2
                for half in range(2):
                    sp.dma_start(wbd[64 * h:64 * h + 64, b % 2, :, 64 * h + 32 * half:64 * h + 32 * half + 32],
                                 gen[64 * half:64 * half + 64, b, :, :]).then_inc(S["moved"], 16)
            for b2 in range(2):
                with sp.Fori(0, CPI) as r:
                    sp.wait_ge(S["added"], b2 * CPI + r + 2)
                    for h in range(2):
                        sp.dma_start(d["out"].rearrange("b c y x -> b c (y x)")[2 * h + b2, :, bass.ds(r * CH, CH)],
                                     x[64 * h:64 * h + 64, bass.ds(r * CH + b2 * PIX, CH)]).then_inc(S["stored"], 16)
            sp.wait_ge(S["stored"], 2 * 2 * CPI * 16)

        @block.tensor
        def _(pe):
            pe.wait_ge(S["pooled"], 1)
            for b in range(NB):
                h = b // 2
                mm = pe.matmul(ps[:, 512 * b:512 * b + HID], pw[64 * h:64 * h + 64, b % 2, :],
                               k["w31T"][64 * h:64 * h + 64, :], start=True, stop=True)
            mm.then_inc(S["h_ps"], 1)
            pe.wait_ge(S["moved"], 2 * NB * 16)
            pe.sem_inc(S["added"], 1)
            for b2 in range(2):
                with pe.Fori(0, CPI) as r:
                    n = b2 * CPI + r + 1
                    pe.wait_ge(S["added"], n)
                    for t in range(TAPS):
                        mm = pe.matmul(ps[:, 2048:2048 + CH].rearrange("p (y x) -> p y x", y=ROWS),
                                       wbd[:, b2, t, :], chunk_window(xp, b2, r, t),
                                       start=(t == 0), stop=(t == TAPS - 1))
                    mm.then_inc(S["conv_ps"], 1)

        @block.vector
        def _(v):
            step = Chain(v, S["steps"])
            step(v.tensor_reduce(gm, xn[:, :].rearrange("p (b n) -> p b n", b=2), AX.X, ALU.add))
            step(v.tensor_scalar(gm, gm, 1.0 / PIX, None, ALU.mult))
            v.tensor_copy(pw, gm.unsqueeze(2).to_broadcast([128, 2, 128])).then_inc(S["pooled"], 1)
            v.wait_ge(S["h_ps"], 1)
            hps = ps[:, 0:2048].rearrange("p (b n) -> p b n", b=NB)[:, :, 0:HID]
            step(v.tensor_tensor(hb, hps, k["b1_3"][:, :].unsqueeze(1).to_broadcast([128, NB, HID]), ALU.add))
            step(v.tensor_scalar(hb, hb, 0.0, None, ALU.max))
            v.wait_ge(S["w2"], 64)
            for b in range(NB):
                for u in range(2):
                    step(v.tensor_tensor(prod.rearrange("p (m n) -> p m n", n=HID),
                                         w2[:, n_w * u:n_w * u + n_w].rearrange("p (m n) -> p m n", n=HID),
                                         hb[:, b, :].unsqueeze(1).to_broadcast([128, QO * TAPS, HID]), ALU.mult))
                    step(v.tensor_reduce(gen[:, b, :, QO * u:QO * u + QO],
                                         prod.rearrange("p (o t n) -> p t o n", o=QO, t=TAPS), AX.X, ALU.add))
                v.tensor_tensor(gen[:, b, :, :], gen[:, b, :, :], b2t.rearrange("p (o t) -> p t o", t=TAPS),
                                ALU.add).then_inc(S["gen"], 1)
            for b2 in range(2):
                with v.Fori(0, CPI) as r:
                    v.wait_ge(S["conv_ps"], b2 * CPI + r + 1)
                    xs = x[:, bass.ds(r * CH + b2 * PIX, CH)]
                    v.tensor_tensor(xs, xs, ps[:, 2048:2048 + CH], ALU.add).then_inc(S["added"], 1)


def clear_borders(nc, k):
    cleared = signal(k, "borders_cleared")
    with nc.Block() as block:
        @block.gpsimd
        def _(pool):
            pool.memset(k["xp_flat"], 0.0).then_inc(cleared, 1)
            pool.wait_ge(cleared, 1)


def store_x(nc, k):
    stored = signal(k, "dbg_stored")
    with nc.Block() as block:
        @block.sync
        def _(sp):
            for h in range(2):
                sp.dma_start(k["dram"]["out"][2 * h:2 * h + 2].rearrange("b c y x -> c b (y x)"),
                             k["x"][64 * h:64 * h + 64, :].rearrange("c (b n) -> c b n", b=2)).then_inc(stored, 16)
            sp.wait_ge(stored, 32)


STAGES = 4
WIDE = 1


def program(nc, dram):
    with ExitStack() as ctx:
        k = {"ctx": ctx, "dram": dram, "nc": nc, "signals": []}

        def sb(name, shape, dt=F32):
            k[name] = ctx.enter_context(nc.sbuf_tensor(name + "_sb", shape, dt))
            return k[name]

        sb("x", [128, COLS])
        sb("xn", [128, COLS])
        sb("xp", [128, 2, PH, PH])
        for name, shape in [("vec", [128, len(V64)]), ("dw", [128, TAPS]), ("ident", [128, 128]),
                            ("pairm", [128, 128]), ("halfm", [128, 128]), ("b_om", [128, OM]), 
                            ("b1_3", [128, HID]), ("ba", [128, C]), ("offb", [72, 1]), ("dbs", [128, 1]),
                            ("wg1T", [128, 8]), ("wgb1", [8, 1]), ("wg2T", [8, 2]), ("wgb2", [4, 2]),
                            ("gp1T", [128, 32]), ("gpb1", [32, 1]), ("gp2T", [32, 32]), ("gpb2", [32, 1]),
                            ("gp3T", [32, 128]), ("l2b", [128, 1]), ("stack2", [128, 64]), ("alphas", [128, 2]),
                            ("wom", [128, 2 * OM]), ("win", [128, 128]), ("wout", [128, 128]),
                            ("crT", [128, 128]), ("waT", [128, 128]), ("w31T", [128, 32]),
                            ("offw", [128, TAPS, 72]), ("l2w", [128, 128]), ("dws", [128, TAPS, 128]),
                            ("eps", [128, 1]), ("ones", [128, 1]), ("dwdiag", [128, TAPS, 128]), ("bn", [128, 6]),
                            ("stats", [128, 12]), ("small", [128, 40]), ("wide", [4, 128]),
                            ("mixw", [128, NB, 128]), ("gx", [128, CH])]:
            if name != "dwdiag":
                sb(name, shape)
        sb("identb", [128, 128], mybir.dt.bfloat16)
        sb("flag", [1, 1], mybir.dt.int32)
        sb("sel", [3 * 2 * G * 5, 5, 128], mybir.dt.bfloat16)
        sb("istage", [128, 2, MG], U32)
        for name in ("wom", "win", "wout", "crT", "waT", "l2w"):
            k[name + "_flat"] = k[name][:, :]
        k["offw_flat"] = k["offw"][:, :, :]
        k["dws_flat"] = k["dws"][:, :, :]
        k["mixw_flat"] = k["mixw"][:, :, :]
        k["xp_flat"] = k["xp"][:, :, :, :].rearrange("p b y x -> p (b y x)")
        AR = 31200
        arena = sb("arena", [128, AR])[:, :]
        k["arena"] = arena
        k["dwdiag"] = arena[:, 15000:15000 + TAPS * 128].rearrange("p (t n) -> p t n", t=TAPS)
        k["psum"] = ctx.enter_context(nc.psum_tensor("ps", [128, 4096], F32))[:, :]
        k["xpd"] = nc.dram_tensor("pixel_major", (NB, TPI, PT, C), F32).ap()
        k["tab"] = nc.dram_tensor("quads", (NB * TR, TR * 4 * C), F32).ap()

        load_stage(nc, k)
        vector_setup(nc, k)

        xq0 = AR - 2 * PQ * PQ
        k["xproj"] = arena[:, xq0:AR].rearrange("p (b y x) -> p b y x", b=2, y=PQ)
        group_norm(nc, k, "gn0", True)
        M = 2 * NT
        om0 = arena[:, 0:M * OM].rearrange("p (t n) -> p t n", n=OM)
        k["work0"] = arena[:, M * OM:M * OM + 8 * CH]
        offsets0(nc, k, om0)
        window_counts(nc, k, om0)
        wide = nc.values_load(k["flag"][0:1, 0:1], min_val=0, max_val=1)
        with nc.If(wide < WIDE):
            n = M * 2 * MG
            at = M * OM
            hp, hn = arena[:, at:at + n], arena[:, at + n:at + 2 * n]
            at += 2 * n
            A = arena[:, at:at + M * G * W * W]
            assert at + M * G * W * W <= xq0
            BF = mybir.dt.bfloat16
            n = NT * 3 * 2 * G * W * W // 2
            parts = arena[:, 0:n].bitcast(BF)
            parts = parts.rearrange("p (j u q n v) -> p j u q n v", u=W, q=3, n=2 * G, v=W)
            rest = k["rest0"] = arena[:, n:n + M * G * W * W]
            window_weights(nc, k, om0, hp, hn, A, parts, rest, (k["xn"][:, :], k["xp_flat"]))
            att = arena[:, n:n + W * CH // 2].bitcast(BF)
            n += W * CH // 2
            window_taps(nc, k, parts, att, arena[:, n:n + W * W * CH], arena[:, n + W * W * CH:n + (W * W + 2) * CH])
        with nc.Else():
            xq = k["xproj"]
            pixels_out(nc, k, "pix0", lambda b2, r: xq[:, b2, bass.ds(r * ROWS + 2, ROWS), 2:2 + WW],
                       k["work0"])
            at = AR - M * 2 * MG
            frac0 = arena[:, at:AR].rearrange("p (t n) -> p t n", n=2 * MG)
            at -= M * MG
            mask0 = arena[:, at:at + M * MG].rearrange("p (t n) -> p t n", n=MG)
            at -= (M + 2) * MG
            idx0 = arena[:, at:at + (M + 2) * MG].bitcast(U32).rearrange("p (t n) -> p t n", n=MG)
            yield_places(nc, k, "pl0", om0, idx0, frac0, mask0, MG, True, at, AR)
            quads(nc, k, "quads0", G)
            sample(nc, k, "smp0", idx0, frac0, mask0, MG, True, 4 * C // G, True)
        clear_borders(nc, k)
        end_layer(nc, k)
        if STAGES == 1:
            return store_x(nc, k)

        group_norm(nc, k, "gn1", True)
        NO = 2 * S1
        om1 = arena[:, 0:M * NO].rearrange("p (t n) -> p t n", n=NO)
        k["work1"] = arena[:, M * NO:M * NO + 3 * CH]
        offsets1(nc, k, om1)
        at = AR - M * NO
        frac1 = arena[:, at:AR].rearrange("p (t n) -> p t n", n=NO)
        at -= (M + 2) * S1
        idx1 = arena[:, at:at + (M + 2) * S1].bitcast(U32).rearrange("p (t n) -> p t n", n=S1)
        yield_places(nc, k, "pl1", om1, idx1, frac1, None, S1, False, at, AR)
        quads(nc, k, "quads1", 1)
        k["sc"] = arena[:, 13100:13100 + 2 * COLS].rearrange("p (h n) -> p h n", h=2)
        sample(nc, k, "smp1", idx1, frac1, None, S1, False, 4 * C, False)
        fuse1(nc, k)
        if STAGES == 2:
            return store_x(nc, k)

        group_norm(nc, k, "gn2", False)
        BF = mybir.dt.bfloat16
        stacks = [arena[:, COLS * i:COLS * i + COLS].bitcast(BF) for i in range(4)]
        parts = [k["xn"][:, 0:PIX].bitcast(BF), k["xn"][:, PIX:COLS].bitcast(BF),
                 arena[:, 4 * COLS:4 * COLS + PIX].bitcast(BF)]
        low = 4 * COLS + PIX
        at = arena[:, low:low + NT * 3 * C].rearrange("p (t c) -> p t c", c=3 * C)
        k["work2"] = arena[:, 0:3 * CH]
        project2(nc, k, k["xp_flat"][:, 0:COLS], arena[:, 2 * COLS:3 * COLS], arena[:, 3 * COLS:4 * COLS],
                 parts, at)
        stack2(nc, k, parts, *stacks)
        k["atwork"] = arena[:, low + NT * 3 * C:AR]
        attend2(nc, k, *stacks, at)
        if STAGES == 3:
            return store_x(nc, k)

        group_norm(nc, k, "gn3", True)
        dynamic3(nc, k)


def yield_places(nc, k, tag, om, idx, frac, mask, ns, xfirst, low, AR):
    M = 2 * NT
    base = k[f"base_{tag}"] = k["ctx"].enter_context(nc.sbuf_tensor("base_" + tag, [128, TPI, 2 * ns], F32))
    goff = k["ctx"].enter_context(nc.sbuf_tensor("goff_" + tag, [128, NB, ns], F32))
    loaded = signal(k, tag + "_consts")
    with nc.Block() as block:
        @block.sync
        def _(sp):
            sp.dma_start(base[:, :, :], k["dram"]["base_" + tag]).then_inc(loaded, 16)
            sp.dma_start(goff[:, :, :], k["dram"]["goff_" + tag].partition_broadcast(128)).then_inc(loaded, 16)
            sp.wait_ge(loaded, 32)
    A = k["arena"]
    n = M * 2 * ns
    at = M * om.shape[2]
    assert at + 2 * n <= low
    r1, r2 = A[:, at:at + n], A[:, at + n:at + 2 * n]
    places(nc, k, tag, om, base[:, :, :], goff[:, :, :], idx, frac, ns, xfirst, (r1, r2), mask)


def kernel(**inputs):
    import ml_dtypes
    import numpy as np
    import concourse.bacc as _bacc
    from concourse.bass_utils import run_bass_kernel_spmd as _run

    I = {n: np.asarray(a) for n, a in inputs.items()}
    f = np.float32
    a = {"x": I["x"]}
    L0 = {n[8:]: v for n, v in I.items() if n.startswith("L0_conv_")}
    L1 = {n[8:]: v for n, v in I.items() if n.startswith("L1_conv_")}
    L2 = {n[8:]: v for n, v in I.items() if n.startswith("L2_conv_")}
    L3 = {n[8:]: v for n, v in I.items() if n.startswith("L3_conv_")}
    vecs = dict(L0, gp_b3=L1["gp_b3"], cr_b=L1["cr_b"])
    a["vec64"] = np.stack([vecs[n] for n in V64], 1)
    a["dw_w"] = L0["dw_w"].reshape(C, TAPS)
    a["ident"] = np.eye(128, dtype=f)
    rows = np.arange(3 * 2 * G * 5)
    a["sel"] = ((rows % 5)[:, None, None] == np.arange(5)[None, :, None]) & \
        (((rows // 5) % (2 * G))[:, None, None] == (np.arange(128) // 16)[None, None, :])
    a["sel"] = a["sel"].astype(ml_dtypes.bfloat16)
    a["pairm"] = np.kron(np.eye(64), np.full((2, 2), 1.0 / (2 * PIX))).astype(f)
    a["halfm"] = np.kron(np.eye(2), np.full((64, 64), 1.0 / 64)).astype(f)
    a["stack2"] = np.concatenate([np.eye(64, dtype=f)] * 2, 0)
    a["b_om"] = np.concatenate([L0["b_off"], L0["b_mask"]])
    a["b1_3"] = L3["b1"]
    a["ba"] = L2["ba"]
    a["offb"] = np.concatenate([L1["off_b0"], L1["off_b1"]] * 2)[:, None]
    a["dbs"] = np.concatenate([L1["db0"], L1["db1"]])[:, None]
    a["wg1T"] = L1["wg_w1"].T
    a["wgb1"] = L1["wg_b1"][:, None]
    a["wg2T"] = L1["wg_w2"].T
    a["wgb2"] = L1["wg_b2"]
    a["gp1T"] = np.concatenate([L1["gp_w1"].T] * 2, 0)
    a["gpb1"] = L1["gp_b1"][:, None]
    a["gp2T"] = L1["gp_w2"].T
    a["gpb2"] = L1["gp_b2"][:, None]
    a["gp3T"] = np.concatenate([L1["gp_w3"].T] * 2, 1)
    a["l2b"] = np.concatenate([L2["b1"], L2["b2"]] * 2)[:, None]
    a["alphas"] = np.stack([np.concatenate([np.broadcast_to(L2[n], HID) for n in ("a1", "a2")] * 2),
                            np.broadcast_to(L2["aa"], 128)], 1)
    a["w_om"] = np.concatenate([L0["w_off"], L0["w_mask"]], 1)
    a["w_in"] = L0["w_in"]
    a["w_out"] = L0["w_out"]
    a["crT"] = L1["cr_w"].T
    a["waT"] = L2["wa"].T
    a["w31T"] = L3["W1"].T
    a["offw"] = np.concatenate([L1["off_w0"], L1["off_w1"]], 0).reshape(36, C, TAPS).transpose(1, 2, 0)
    a["l2w"] = np.concatenate([L2["w1"].T, L2["w2"].T], 1)
    a["dws"] = np.stack([L1["dw0"], L1["dw1"]]).reshape(2, C, C, TAPS).transpose(0, 3, 2, 1)
    a["W2"] = L3["W2"]
    a["b2"] = L3["b2"]
    pix = np.arange(PIX).reshape(TPI, PT).T
    y, xx = pix // WW, pix % WW
    tap = np.arange(TAPS)
    b0 = np.stack([xx[..., None] + tap // 3, y[..., None] + tap % 3], -1)
    a["base_pl0"] = np.tile(b0[:, :, None], (1, 1, G, 1, 1)).reshape(128, TPI, 2 * MG).astype(f)
    b1 = np.stack([y[..., None] + tap // 3, xx[..., None] + tap % 3], -1)
    a["base_pl1"] = np.tile(b1[:, :, None], (1, 1, 2, 1, 1)).reshape(128, TPI, 2 * S1).astype(f)
    img = np.arange(NB) * TR * TR
    a["goff_pl0"] = (img[:, None] * G + np.repeat(np.arange(G), TAPS)[None]).astype(f)
    a["goff_pl1"] = np.repeat(img[:, None], S1, 1).astype(f)

    nc = _bacc.Bacc("TRN2", target_bir_lowering=False, num_devices=1)
    arrays, dram = {}, {}
    for n, v in a.items():
        arrays["in_" + n] = np.ascontiguousarray(v)
        dram[n] = nc.dram_tensor("in_" + n, arrays["in_" + n].shape,
                                 mybir.dt.from_np(arrays["in_" + n].dtype), kind="ExternalInput").ap()
    dram["out"] = nc.dram_tensor("out_x", (NB, C, HH, WW), F32, kind="ExternalOutput").ap()
    program(nc, dram)
    r = _run(nc, [arrays], core_ids=[0])
    return r.results[0]["out_x"]
```

```python
import concourse.bass as bass
from concourse import mybir
from contextlib import ExitStack, contextmanager

F32 = mybir.dt.float32
U32 = mybir.dt.uint32
ALU = mybir.AluOpType
ACT = mybir.ActivationFunctionType
AX = mybir.AxisListType

NB, C, HH, WW = 4, 64, 48, 48
PIX = HH * WW
COLS = 2 * PIX
PT = 128
TPI = PIX // PT
NT = 2 * TPI
PH = HH + 2
PQ = HH + 4
PW = HH + 6
IH, IW = 4, 6
WH, WX = IH + 6, IW + 6
KW = WH * WX
TAPS = 9
G = 4
ROWS = 8
CH = ROWS * WW
CPI = HH // ROWS
TPC = CH // PT
TR = PH - 1
ROUND = 12582912.0
MG = G * TAPS
OM = 3 * MG
S1 = 2 * TAPS
HID = 32

V64 = ["b_in", "dw_b", "ln_g", "ln_b", "b_out", "bn_g", "bn_b", "bn_mean", "bn_var", "gp_b3", "cr_b"]
VC = {n: i for i, n in enumerate(V64)}


class Chain:

    def __init__(self, eng, sem):
        self.eng, self.sem, self.off, self.n = eng, sem, 0, 0

    def __call__(self, ins):
        self.n += 1
        ins.then_inc(self.sem, 1)
        self.eng.wait_ge(self.sem, self.off + self.n)

    @contextmanager
    def body(self, i, per, count):
        before, self.off, self.n = self.n, self.n + i * per, 0
        yield
        assert self.n == per, self.n
        self.off, self.n = 0, before + per * count


def signal(k, name):
    k["signals"].append(k["nc"].alloc_semaphore(name))
    return k["signals"][-1]


def end_layer(nc, k):
    nc.all_engine_barrier()
    nc.clear_and_free_semaphores(k["signals"])
    nc.all_engine_barrier()
    k["signals"] = []


def load_stage(nc, k):
    ctx, d = k["ctx"], k["dram"]
    t_x = k["x"]
    loaded = signal(k, "weights_loaded")
    cleared = signal(k, "weights_cleared")
    built = signal(k, "diag_built")
    with nc.Block() as block:
        n = [0]

        @block.sync
        def _(sp):
            def load(dst, src):
                sp.dma_start(dst, src).then_inc(loaded, 16)
                n[0] += 16

            for h in range(2):
                load(t_x[64 * h:64 * h + 64, :].rearrange("c (b n) -> c b n", b=2),
                     d["x"][2 * h:2 * h + 2].rearrange("b c y x -> c b (y x)"))
                load(k["vec"][64 * h:64 * h + 64, :], d["vec64"])
                load(k["dw"][64 * h:64 * h + 64, :], d["dw_w"])
            load(k["ident"][:, :], d["ident"])
            load(k["sel"][:, :, :], d["sel"])
            load(k["pairm"][:, :], d["pairm"])
            load(k["halfm"][:, :], d["halfm"])
            for name in ("b_om", "b1_3", "ba"):
                load(k[name][:, :], d[name].partition_broadcast(128))
            for name in ("offb", "dbs", "wg1T", "wgb1", "wg2T", "gp1T", "gpb1", "gp2T", "gpb2", "gp3T",
                         "l2b", "stack2", "drop"):
                load(k[name][:, :], d[name])
            load(k["wgb2"][:, :], d["wgb2"].partition_broadcast(4))
            load(k["alphas"][:, :], d["alphas"])
            sp.wait_ge(cleared, 1)
            zero = k["arena"][:, 0:3 * PW * C // 4]
            for b in range(NB):
                for lo in (0, PW - 3):
                    load(k["xw"][b, lo:lo + 3].rearrange("y x c -> (y x c)").rearrange("(p n) -> p n", p=6),
                         zero[0:6, 0:PW * C // 2])
            for h in range(2):
                r = slice(64 * h, 64 * h + 64)
                load(k["wom"][r, OM * h:OM * h + OM], d["w_om"])
                load(k["win"][r, r], d["w_in"])
                load(k["wout"][r, r], d["w_out"])
                load(k["crT"][r, r], d["crT"])
                load(k["waT"][r, r], d["waT"])
                load(k["w31T"][r, :], d["w31T"])
                load(k["offw"][r, :, 36 * h:36 * h + 36], d["offw"])
                load(k["l2w"][r, r], d["l2w"])
            sp.wait_ge(loaded, n[0])

        @block.gpsimd
        def _(pool):
            for name in ("wom", "win", "wout", "crT", "waT", "offw", "l2w", "xp"):
                ins = pool.memset(k[name + "_flat"], 0.0)
            pool.memset(k["arena"][:, 0:3 * PW * C // 4], 0.0)
            pool.memset(k["eps"][:, :], 1e-5)
            pool.memset(k["ones"][:, :], 1.0).then_inc(cleared, 1)

        @block.vector
        def _(v):
            v.wait_ge(cleared, 1)


def vector_setup(nc, k):
    ctx = k["ctx"]
    steps = signal(k, "setup_steps")
    rooted = signal(k, "bn_rooted")
    with nc.Block() as block:
        @block.scalar
        def _(act):
            act.activation(k["bn"][:, 0:1], k["vec"][:, VC["bn_var"]:VC["bn_var"] + 1], ACT.Sqrt,
                           bias=k["eps"][:, 0:1]).then_inc(rooted, 1)

        @block.vector
        def _(v):
            step = Chain(v, steps)
            v.tensor_copy(k["identb"][:, :], k["ident"][:, :])
            for t in range(TAPS):
                v.tensor_scalar(k["dwdiag"][:, t, :], k["ident"][:, :], k["dw"][:, t:t + 1], None, ALU.mult)
            bn, vec = k["bn"], k["vec"]

            def col(n):
                return vec[:, VC[n]:VC[n] + 1]
            v.wait_ge(rooted, 1)
            step(v.reciprocal(bn[:, 1:2], bn[:, 0:1]))
            step(v.tensor_tensor(bn[:, 2:3], bn[:, 1:2], col("bn_g"), ALU.mult))
            step(v.tensor_tensor(bn[:, 3:4], col("b_out"), col("bn_mean"), ALU.subtract))
            step(v.tensor_tensor(bn[:, 4:5], bn[:, 3:4], bn[:, 2:3], ALU.mult))
            step(v.tensor_tensor(bn[:, 5:6], bn[:, 4:5], col("bn_b"), ALU.add))


def group_norm(nc, k, tag, padded):
    ctx = k["ctx"]
    x, xn, xp, st = k["x"], k["xn"], k["xp"], k["stats"]
    ps = k["psum"]
    sums = signal(k, tag + "_sums")
    mean_ps = signal(k, tag + "_mean_ps")
    means = signal(k, tag + "_means")
    squares = signal(k, tag + "_squares")
    var_ps = signal(k, tag + "_var_ps")
    rooted = signal(k, tag + "_rooted")
    normed = signal(k, tag + "_normed")
    steps = signal(k, tag + "_steps")
    x3 = x[:, :].rearrange("p (b n) -> p b n", b=2)
    with nc.Block() as block:
        @block.vector
        def _(v):
            step = Chain(v, steps)
            v.tensor_reduce(st[:, 0:2], x3, AX.X, ALU.add).then_inc(sums, 1)
            v.wait_ge(mean_ps, 1)
            step(v.tensor_copy(st[:, 2:4], ps[:, 0:2]))
            v.tensor_scalar(st[:, 4:6], st[:, 2:4], -1.0, None, ALU.mult).then_inc(means, 1)
            v.wait_ge(rooted, 1)
            step(v.reciprocal(st[:, 10:12], st[:, 8:10]))
            for b in range(2):
                v.tensor_scalar(xn[:, PIX * b:PIX * b + PIX], x[:, PIX * b:PIX * b + PIX], st[:, 2 + b:3 + b],
                                st[:, 10 + b:11 + b], ALU.subtract, ALU.mult).then_inc(normed, 1)

        @block.tensor
        def _(pe):
            pe.wait_ge(sums, 1)
            pe.matmul(ps[:, 0:2], k["pairm"][:, :], st[:, 0:2], start=True, stop=True).then_inc(mean_ps, 1)
            pe.wait_ge(squares, 2)
            pe.matmul(ps[:, 512:514], k["pairm"][:, :], st[:, 6:8], start=True, stop=True).then_inc(var_ps, 1)

        @block.scalar
        def _(act):
            act.wait_ge(means, 1)
            for b in range(2):
                act.activation(xn[:, PIX * b:PIX * b + PIX], x[:, PIX * b:PIX * b + PIX], ACT.Square,
                               bias=st[:, 4 + b:5 + b], accum_out=st[:, 6 + b:7 + b]).then_inc(squares, 1)
            act.wait_ge(var_ps, 1)
            act.activation(st[:, 8:10], ps[:, 512:514], ACT.Sqrt, bias=k["eps"][:, 0:1]).then_inc(rooted, 1)
            if padded:
                for b in range(2):
                    act.wait_ge(normed, b + 1)
                    act.activation(xp[:, b, 1:HH + 1, 1:WW + 1],
                                   xn[:, PIX * b:PIX * b + PIX].rearrange("p (y x) -> p y x", y=HH), ACT.Copy)


def chunk_window(xp, b2, r, tap):
    dy, dx = divmod(tap, 3)
    return xp[:, b2, bass.ds(r * ROWS + dy, ROWS), dx:dx + WW]


def offsets0(nc, k, om):
    ctx, ps, xp, xn = k["ctx"], k["psum"], k["xp"], k["xn"]
    big = k["work0"]
    conv, cent, sq, root, inv, z, gel, xs = (big[:, CH * i:CH * i + CH] for i in range(8))
    xq = k["xproj"]
    S = {n: signal(k, "off0_" + n) for n in
         ("conv_ps", "conv", "mean_ps", "cent", "sq", "var_ps", "root", "z", "gelu", "om_ps", "om",
          "proj_ps", "proj", "steps", "cleared")}
    p_conv, p_mean, p_var = ps[:, 0:CH], ps[:, 512:512 + CH], ps[:, 1024:1024 + CH]
    p_om = ps[:, 1536:1536 + TPC * 256].rearrange("p (t n) -> p t n", t=TPC)
    p_proj = ps[:, 2560:2560 + CH]
    vec = k["vec"]

    def turns(eng):
        for b2 in range(2):
            with eng.Fori(0, CPI) as r:
                yield b2, r, b2 * CPI + r + 1

    with nc.Block() as block:
        @block.tensor
        def _(pe):
            pe.sem_inc(S["om"], 1)
            pe.sem_inc(S["proj"], 1)
            for b2, r, n in turns(pe):
                pe.wait_ge(S["om"], n)
                for t in range(TAPS):
                    mm = pe.matmul(p_conv.rearrange("p (y x) -> p y x", y=ROWS), k["dwdiag"][:, t, :],
                                   chunk_window(xp, b2, r, t), start=(t == 0), stop=(t == TAPS - 1))
                mm.then_inc(S["conv_ps"], 1)
                pe.wait_ge(S["conv"], n)
                pe.matmul(p_mean, k["halfm"][:, :], conv, start=True, stop=True).then_inc(S["mean_ps"], 1)
                pe.wait_ge(S["proj"], n)
                pe.matmul(p_proj, k["win"][:, :], xn[:, bass.ds(r * CH + b2 * PIX, CH)], start=True, stop=True)\
                    .then_inc(S["proj_ps"], 1)
                pe.wait_ge(S["sq"], n)
                pe.matmul(p_var, k["halfm"][:, :], sq, start=True, stop=True).then_inc(S["var_ps"], 1)
                pe.wait_ge(S["gelu"], n)
                for t in range(TPC):
                    mm = pe.matmul(p_om[:, t, 0:2 * OM], gel[:, PT * t:PT * t + PT], k["wom"][:, :],
                                   start=True, stop=True)
                mm.then_inc(S["om_ps"], 1)

        @block.scalar
        def _(act):
            for b2, r, n in turns(act):
                act.wait_ge(S["conv_ps"], n)
                act.activation(conv, p_conv, ACT.Identity, bias=vec[:, VC["dw_b"]:VC["dw_b"] + 1])\
                    .then_inc(S["conv"], 1)
                if b2 == 0:
                    act.wait_ge(S["cleared"], 1)
                act.wait_ge(S["proj_ps"], n)
                act.activation(xq[:, b2, bass.ds(r * ROWS + 2, ROWS), 2:2 + WW],
                               p_proj.rearrange("p (y x) -> p y x", y=ROWS), ACT.Identity,
                               bias=vec[:, VC["b_in"]:VC["b_in"] + 1]).then_inc(S["proj"], 1)
                act.wait_ge(S["cent"], n)
                act.activation(sq, cent, ACT.Square).then_inc(S["sq"], 1)
                act.wait_ge(S["var_ps"], n)
                act.activation(root, p_var, ACT.Sqrt, bias=k["eps"][:, 0:1]).then_inc(S["root"], 1)
                act.wait_ge(S["z"], n)
                act.activation(gel, z, ACT.Gelu, scale=vec[:, VC["ln_g"]:VC["ln_g"] + 1],
                               bias=vec[:, VC["ln_b"]:VC["ln_b"] + 1]).then_inc(S["gelu"], 1)

        @block.vector
        def _(v):
            step = Chain(v, S["steps"])
            for b2 in range(2):
                with v.Fori(0, CPI) as r, step.body(r, 1, CPI):
                    n = b2 * CPI + r + 1
                    v.wait_ge(S["mean_ps"], n)
                    v.tensor_tensor(cent, conv, p_mean, ALU.subtract).then_inc(S["cent"], 1)
                    v.wait_ge(S["root"], n)
                    step(v.reciprocal(inv, root))
                    v.tensor_tensor(z, cent, inv, ALU.mult).then_inc(S["z"], 1)
                    v.wait_ge(S["om_ps"], n)
                    v.tensor_tensor(om[:, bass.ds((r + b2 * CPI) * (2 * TPC), 2 * TPC), :]
                                    .rearrange("p (t h) n -> p t h n", h=2),
                                    p_om[:, :, 0:2 * OM].rearrange("p t (h n) -> p t h n", h=2),
                                    k["b_om"][:, :].unsqueeze(1).unsqueeze(1).to_broadcast([128, TPC, 2, OM]),
                                    ALU.add).then_inc(S["om"], 1)

        @block.gpsimd
        def _(pool):
            pool.memset(xq.rearrange("p b y x -> p (b y x)"), 0.0).then_inc(S["cleared"], 1)


def window_counts(nc, k, om):
    ctx, ps, st = k["ctx"], k["psum"], k["small"]
    S = {n: signal(k, "wide_" + n) for n in ("top", "turned", "steps", "flag")}
    with nc.Block() as block:
        @block.vector
        def _(v):
            step = Chain(v, S["steps"])
            v.tensor_reduce(st[:, 0:1], om[:, :, 0:2 * MG], AX.XY, ALU.max, apply_absolute_value=True)\
                .then_inc(S["top"], 1)
            v.wait_ge(S["turned"], 1)
            step(v.tensor_reduce(st[0:1, 1:2], ps[0:1, 0:128], AX.X, ALU.max))
            v.tensor_scalar(k["flag"][:, :], st[0:1, 1:2], 1.0, None, ALU.is_gt).then_inc(S["flag"], 1)

        @block.tensor
        def _(pe):
            pe.wait_ge(S["top"], 1)
            pe.transpose(ps[0:1, 0:128], st[:, 0:1], k["ident"][:, :]).then_inc(S["turned"], 1)


W = 5


def window_weights(nc, k, om, hp, hn, A, parts, rest, tmp):
    ctx = k["ctx"]
    S = {n: signal(k, "ww_" + n) for n in
         ("shifted", "exped", "steps", "hats", "ready", "prod", "used", "a", "part", "cleared")}
    M = 2 * NT
    TG = M * G
    logits = om[:, :, 2 * MG:OM].rearrange("p t (g s) -> p t g s", g=G)
    off = om[:, :, 0:2 * MG]
    hp3, hn3 = hp.rearrange("p (t n) -> p t n", t=M), hn.rearrange("p (t n) -> p t n", t=M)
    top = tmp[0][:, 0:TG].rearrange("p (t g) -> p t g", g=G)
    topb = top.unsqueeze(3).to_broadcast([128, M, G, TAPS])
    hats = [hn3, off, hp3]
    mask = om[:, :, 2 * MG:OM]
    A4 = A.rearrange("p (n u v) -> p n u v", u=W, v=W)
    pr = [t[:, 0:TG * TAPS].rearrange("p (n x y) -> p n x y", x=3, y=3) for t in tmp]

    def axis(h, a):
        return h.rearrange("p t (s a) -> p t s a", a=2)[:, :, :, a]

    def by_row(a, u):
        return a.rearrange("p (j n u v) -> p j n u v", n=2 * G, u=W, v=W)[:, :, :, u, :]

    POOLED = (1, 4, 7)
    with nc.Block() as block:
        @block.scalar
        def _(act):
            act.activation(hp3, off, ACT.Relu).then_inc(S["hats"], 1)
            act.activation(hn3, off, ACT.Relu, scale=-1.0).then_inc(S["hats"], 1)
            act.wait_ge(S["shifted"], 1)
            act.activation(mask, mask, ACT.Exp).then_inc(S["exped"], 1)
            for q in range(3):
                act.wait_ge(S["a"], q + 1)
                for u in range(W):
                    last = act.activation(parts[:, :, u, q, :, :], by_row((A, rest, A)[q], u), ACT.Copy)
                last.then_inc(S["part"], 1)

        @block.gpsimd
        def _(pool):
            pool.memset(A, 0.0).then_inc(S["cleared"], 1)
            pool.wait_ge(S["ready"], 1)
            for n, q in enumerate(POOLED):
                dy, dx = divmod(q, 3)
                if n:
                    pool.wait_ge(S["used"], n)
                pool.tensor_tensor(tmp[1][:, 0:TG * TAPS].rearrange("p (t s) -> p t s", s=MG),
                                   axis(hats[dy], 1), axis(hats[dx], 0), ALU.mult).then_inc(S["prod"], 1)

        @block.vector
        def _(v):
            step = Chain(v, S["steps"])
            step(v.tensor_reduce(top, logits, AX.X, ALU.max))
            v.tensor_tensor(logits, logits, topb, ALU.subtract).then_inc(S["shifted"], 1)
            v.wait_ge(S["hats"], 2)
            step(v.scalar_tensor_tensor(off, hp3, 1.0, hn3, ALU.subtract, ALU.add))
            step(v.tensor_scalar(off, off, -1.0, None, ALU.mult))
            v.wait_ge(S["exped"], 1)
            step(v.tensor_reduce(top, logits, AX.X, ALU.add))
            step(v.reciprocal(top, top))
            step(v.tensor_tensor(logits, logits, topb, ALU.mult))
            for n, h in enumerate(hats):
                ins = v.tensor_tensor(axis(h, 1), axis(h, 1), mask, ALU.mult)
            ins.then_inc(S["ready"], 1)
            v.wait_ge(S["ready"], 1)
            v.wait_ge(S["cleared"], 1)
            own = [q for q in range(9) if q not in POOLED]
            for n in range(9):
                q = own[n - (n + 1) // 3] if n % 3 != 2 else POOLED[n // 3]
                dy, dx = divmod(q, 3)
                if n % 3 == 2:
                    v.wait_ge(S["prod"], n // 3 + 1)
                    src = pr[1]
                else:
                    step(v.tensor_tensor(tmp[0][:, 0:TG * TAPS].rearrange("p (t s) -> p t s", s=MG),
                                         axis(hats[dy], 1), axis(hats[dx], 0), ALU.mult))
                    src = pr[0]
                dst = A4[:, :, dy:dy + 3, dx:dx + 3]
                add = v.tensor_tensor(dst, dst, src.rearrange("p n x y -> p n y x"), ALU.add)
                if n == 8:
                    add.then_inc(S["a"], 1)
                elif n % 3 == 2:
                    add.then_inc(S["used"], 1)
                    v.wait_ge(S["used"], n // 3 + 1)
                else:
                    step(add)
            for q in range(2):
                v.wait_ge(S["part"], q + 1)
                dst, src = ((rest, A), (A, rest))[q]
                for u in range(W):
                    last = v.tensor_tensor(by_row(dst, u), by_row(src, u), parts[:, :, u, q, :, :], ALU.subtract)
                last.then_inc(S["a"], 1)


def window_taps(nc, k, parts, att, pr, tail):
    ctx, ps, xq, x = k["ctx"], k["psum"], k["xproj"], k["x"]
    BF = mybir.dt.bfloat16
    S = {n: signal(k, "wt_" + n) for n in
         ("turned", "at", "spread", "prod", "sum1", "sum2", "acc", "gated", "added", "steps")}
    sel = k["sel"]
    R = 3 * 8 * W
    p_t = ps[0:R, 3072:4096].bitcast(BF).rearrange("p (n c) -> p n c", c=PT)
    p_b = [ps[:, 512 * v:512 * v + CH] for v in range(W)]
    p_y = ps[:, 2560:2560 + CH]
    prod = [[pr[:, (W * u + v) * CH:(W * u + v + 1) * CH] for v in range(W)] for u in range(W)]
    yb = [tail[:, CH * i:CH * i + CH] for i in range(2)]

    def turns(eng):
        for b2 in range(2):
            with eng.Fori(0, CPI) as r:
                yield b2, r, b2 * CPI + r + 1

    flat = parts.rearrange("p j u q n v -> p (j u q n v)")
    with nc.Block() as block:
        @block.gpsimd
        def _(pool):
            for b2, r, n in turns(pool):
                for u in range(W):
                    m = (n - 1) * W + (u + 1)
                    pool.wait_ge(S["prod"], (n - 1) * (W * W) + (W * u + 4 + W))
                    a = pr[:, W * u * CH:(W * u + 2) * CH]
                    pool.tensor_tensor(a, a, pr[:, (W * u + 2) * CH:(W * u + 4) * CH], ALU.add).then_inc(S["sum1"], 1)
                    pool.wait_ge(S["sum1"], m)
                    pool.tensor_tensor(prod[u][0], prod[u][0], prod[u][1], ALU.add).then_inc(S["sum2"], 1)

        @block.scalar
        def _(act):
            for b2, r, n in turns(act):
                act.wait_ge(S["turned"], n)
                act.wait_ge(S["spread"], (n - 1) * (W * W) + 1)
                act.activation(att[0:R, :].rearrange("p (n c) -> p n c", c=PT)[:, 0:15, :], p_t[:, 0:15, :],
                               ACT.Copy).then_inc(S["at"], 1)
                act.wait_ge(S["acc"], n * W + W)
                act.wait_ge(S["added"], n)
                act.activation(yb[0], p_y, ACT.Identity, scale=k["bn"][:, 2:3], bias=k["bn"][:, 5:6])
                act.activation(yb[1], p_y, ACT.Sigmoid, scale=k["bn"][:, 2:3], bias=k["bn"][:, 5:6])\
                    .then_inc(S["gated"], 1)

        @block.tensor
        def _(pe):
            pe.sem_inc(S["spread"], 1)
            pe.sem_inc(S["added"], 1)
            pe.sem_inc(S["prod"], W)
            pe.sem_inc(S["at"], 1)
            pe.sem_inc(S["gated"], 1)
            for b2, r, n in turns(pe):
                pe.wait_ge(S["at"], n)
                for t in range(TPC):
                    for u in range(W):
                        mm = pe.transpose(p_t[:, u * TPC + t, :], flat[:, bass.ds(r * (TPC * W * R) + (b2 * TPI + t) * (W * R) + u * R, R)],
                                          k["identb"][:, :])
                mm.then_inc(S["turned"], 1)
                pe.wait_ge(S["at"], n + 1)

                def gather_sums(u):
                    pe.wait_ge(S["sum2"], (n - 1) * W + (u + 1))
                    if u == 0:
                        pe.wait_ge(S["gated"], n)
                    pe.matmul(p_y, k["wout"][:, :], prod[u][0], start=(u == 0), stop=False)
                    pe.wait_ge(S["prod"], (n - 1) * (W * W) + (W * u + 5 + W))
                    mm = pe.matmul(p_y, k["wout"][:, :], prod[u][4], start=False, stop=(u == W - 1))
                    mm.then_inc(S["acc"], 1)

                for u in range(W):
                    for v in range(W):
                        c = (n - 1) * (W * W) + (W * u + v + 1)
                        pe.wait_ge(S["prod"], c)
                        pe.matmul(p_b[v], sel[0:R, v, :], att[0:R, CH * u:CH * u + CH], start=True, stop=True)\
                            .then_inc(S["spread"], 1)
                    if u >= 1:
                        gather_sums(u - 1)
                gather_sums(W - 1)

        @block.vector
        def _(v_):
            step = Chain(v_, S["steps"])
            v_.sem_inc(S["acc"], W)
            for b2 in range(2):
                with v_.Fori(0, CPI) as r, step.body(r, 1, CPI):
                    n = b2 * CPI + r + 1
                    for u in range(W):
                        v_.wait_ge(S["acc"], (n - 1) * W + (u + 1))
                        for v in range(W):
                            v_.wait_ge(S["spread"], (n - 1) * (W * W) + (W * u + v + 2))
                            v_.tensor_tensor(prod[u][v].rearrange("p (y x) -> p y x", y=ROWS),
                                             p_b[v].rearrange("p (y x) -> p y x", y=ROWS),
                                             xq[:, b2, bass.ds(r * ROWS + u, ROWS), v:v + WW], ALU.mult)\
                                .then_inc(S["prod"], 1)
                    v_.wait_ge(S["gated"], n + 1)
                    step(v_.tensor_tensor(yb[0], yb[0], yb[1], ALU.mult))
                    xs = x[:, bass.ds(r * CH + b2 * PIX, CH)]
                    v_.tensor_tensor(xs, xs, yb[0], ALU.add).then_inc(S["added"], 1)


def pixels_out(nc, k, tag, window, buf, loads=()):
    ps = k["psum"]
    TP, NTP = 2 * PW, ROWS // 2
    xs, pp = buf[:, 0:ROWS * PW], buf[0:TP, ROWS * PW:ROWS * PW + NTP * 128]
    x4 = xs.rearrange("p (y j t) -> p y j t", y=ROWS, j=IW)
    S = {n: signal(k, tag + "_" + n) for n in ("xs", "turned", "pp", "stored", "loaded", "xs0")}

    def turns(eng):
        for b2 in range(2):
            with eng.Fori(0, CPI) as r:
                yield b2, r, b2 * CPI + r + 1

    with nc.Block() as block:
        @block.vector
        def _(v):
            v.memset(xs, 0.0).then_inc(S["xs0"], 1)
            v.wait_ge(S["xs0"], 1)
            v.sem_inc(S["turned"], 1)
            for b2, r, n in turns(v):
                v.wait_ge(S["turned"], n)
                src = window(b2, r).rearrange("p y (t q) -> p y q t", q=IW)
                for j, t in ((0, 1), (3, 0)):
                    cp = v.tensor_copy(x4[:, :, j:j + 3, t:t + WW // IW], src[:, :, 3 - j:6 - j, :])
                cp.then_inc(S["xs"], 1)

        @block.tensor
        def _(pe):
            pe.sem_inc(S["pp"], 1)
            for b2, r, n in turns(pe):
                pe.wait_ge(S["xs"], n)
                pe.wait_ge(S["pp"], n)
                for t in range(NTP):
                    mm = pe.transpose(ps[0:TP, 128 * t:128 * t + 128], xs[:, TP * t:TP * t + TP],
                                      k["ident"][:, :])
                mm.then_inc(S["turned"], 1)

        @block.scalar
        def _(act):
            for b2, r, n in turns(act):
                act.wait_ge(S["turned"], n + 1)
                act.wait_ge(S["stored"], 32 * n)
                act.activation(pp, ps[0:TP, 0:NTP * 128], ACT.Copy).then_inc(S["pp"], 1)

        @block.sync
        def _(sp):
            for dst, src in loads:
                sp.dma_start(dst, src).then_inc(S["loaded"], 16)
            sp.sem_inc(S["stored"], 32)
            p4 = pp.rearrange("p (t h c) -> p t h c", h=2, c=C)
            rows = k["xw"][:, 3:3 + HH, :, :].rearrange("b (y u) x c -> b (u x) y c", u=2)
            for b2 in range(2):
                with sp.Fori(0, CPI) as r:
                    sp.wait_ge(S["pp"], b2 * CPI + r + 2)
                    for h in range(2):
                        sp.dma_start(rows[2 * h + b2, :, bass.ds(r * (ROWS // 2), ROWS // 2), :], p4[:, :, h, :])\
                            .then_inc(S["stored"], 16)
            sp.wait_ge(S["stored"], 32 * (2 * CPI + 1))
            if loads:
                sp.wait_ge(S["loaded"], 16 * len(loads))


def quads(nc, k, tag, groups):
    ctx = k["ctx"]
    A = k["arena"]
    n = C // groups
    rows = [A[0:2 * TR, 3200 * i:3200 * i + 3200].rearrange("p (x c) -> p x c", c=C) for i in range(2)]
    T = A[0:2 * TR, 6400:6400 + TR * 4 * C]
    T6 = T.rearrange("p (x g q n) -> p x g q n", g=groups, q=4, n=n)
    cleared = signal(k, tag + "_cleared")
    loaded = signal(k, tag + "_loaded")
    spread = signal(k, tag + "_spread")
    stored = signal(k, tag + "_stored")
    img = k["xw"][:, 3:3 + HH, :, :].rearrange("b y (j t) c -> b y j t c", j=IW)
    NL = 4 * IW * 16
    tab = k["tab"]

    def copy(eng, run, q):
        dy, dx = divmod(q, 2)
        return run(T6[:, :, :, q, :], rows[dy][:, dx:dx + TR, :].rearrange("p x (g n) -> p x g n", g=groups))

    with nc.Block() as block:
        @block.gpsimd
        def _(pool):
            pool.memset(A[0:2 * TR, 0:6400], 0.0).then_inc(cleared, 1)
            for bb in range(2):
                pool.wait_ge(loaded, NL * (bb + 1))
                if bb:
                    pool.wait_ge(stored, 16 * bb)
                copy(pool, pool.tensor_copy, 0).then_inc(spread, 1)

        @block.scalar
        def _(act):
            for bb in range(2):
                act.wait_ge(loaded, NL * (bb + 1))
                if bb:
                    act.wait_ge(stored, 16 * bb)
                copy(act, lambda o, i: act.activation(o, i, ACT.Copy), 1).then_inc(spread, 1)

        @block.vector
        def _(v):
            for bb in range(2):
                v.wait_ge(loaded, NL * (bb + 1))
                if bb:
                    v.wait_ge(stored, 16 * bb)
                for q in (2, 3):
                    copy(v, v.tensor_copy, q).then_inc(spread, 1)

        @block.sync
        def _(sp):
            sp.wait_ge(cleared, 1)
            for bb in range(2):
                if bb:
                    sp.wait_ge(spread, 4 * bb)
                for dy in range(2):
                    for u in range(2):
                        dst = rows[dy][TR * u + 1 - dy:TR * u + 1 - dy + HH, 1:WW + 1, :]\
                            .rearrange("p (t q) c -> p q t c", q=IW)
                        for j in range(IW):
                            t = 1 if j < 3 else 0
                            sp.dma_start(dst[:, (j + 3) % IW, :, :], img[2 * bb + u, :, j, t:t + WW // IW, :])\
                                .then_inc(loaded, 16)
                sp.wait_ge(spread, 4 * (bb + 1))
                sp.dma_start(tab[2 * TR * bb:2 * TR * bb + 2 * TR, :], T).then_inc(stored, 16)
            sp.wait_ge(stored, 32)


def places(nc, k, tag, om, base, goff, idx, frac, ns, xfirst, tmp, mask):
    ctx = k["ctx"]
    steps = signal(k, tag + "_steps")
    shifted = signal(k, tag + "_shifted")
    exped = signal(k, tag + "_exped")
    M = 2 * NT
    cf = frac[:, :, :]
    r1, r2 = tmp
    with nc.Block() as block:
        @block.vector
        def _(v):
            step = Chain(v, steps)
            if mask is not None:
                logits = om[:, :, 2 * MG:OM].rearrange("p t (g k) -> p t g k", g=G)
                m4 = mask[:, 0:M, :].rearrange("p t (g k) -> p t g k", g=G)
                top = r1[:, 0:M * G].rearrange("p (t g) -> p t g", g=G)
                topb = top.unsqueeze(3).to_broadcast([128, M, G, TAPS])
                step(v.tensor_reduce(top, logits, AX.X, ALU.max))
                v.tensor_tensor(m4, logits, topb, ALU.subtract).then_inc(shifted, 1)
                v.wait_ge(exped, 1)
                step(v.tensor_reduce(top, m4, AX.X, ALU.add))
                step(v.reciprocal(top, top))
                step(v.tensor_tensor(m4, m4, topb, ALU.mult))
            for b2 in range(2):
                for h in range(2):
                    o = om[:, :, 0:2 * ns].rearrange("p (b t h) n -> p b t h n", b=2, h=2)[:, b2, :, h, :]
                    f = cf.rearrange("p (b t h) n -> p b t h n", b=2, h=2)[:, b2, :, h, :]
                    last = v.tensor_tensor(f, o, base, ALU.add)
            step(last)
            flat = cf.rearrange("p t n -> p (t n)")
            a, b = r1[:, 0:M * 2 * ns], r2[:, 0:M * 2 * ns]
            step(v.tensor_scalar(flat, flat, float(PH - 1), 0.0, ALU.min, ALU.max))
            step(v.tensor_scalar(a, flat, ROUND, ROUND, ALU.add, ALU.subtract))
            step(v.tensor_tensor(b, a, flat, ALU.is_gt))
            step(v.tensor_tensor(a, a, b, ALU.subtract))
            step(v.tensor_scalar(a, a, float(PH - 2), None, ALU.min))
            step(v.tensor_tensor(flat, flat, a, ALU.subtract))
            ax = a.rearrange("p (t n a) -> p t n a", n=ns, a=2)
            y0, x0 = (ax[:, :, :, 1], ax[:, :, :, 0]) if xfirst else (ax[:, :, :, 0], ax[:, :, :, 1])
            lin = b[:, 0:M * ns].rearrange("p (t n) -> p t n", n=ns)
            step(v.scalar_tensor_tensor(lin, y0, float(TR), x0, ALU.mult, ALU.add))
            for b2 in range(2):
                for h in range(2):
                    src = lin.rearrange("p (b t h) n -> p b t h n", b=2, h=2)[:, b2, :, h, :]
                    dst = idx[:, 0:M, :].rearrange("p (b t h) n -> p b t h n", b=2, h=2)[:, b2, :, h, :]
                    gb = goff[:, 2 * h + b2, :].unsqueeze(1).to_broadcast([128, TPI, ns])
                    v.scalar_tensor_tensor(dst, src, float(G if mask is not None else 1), gb, ALU.mult, ALU.add)
            v.memset(idx[:, M:M + 2, :], 0)

        if mask is not None:
            @block.scalar
            def _(act):
                act.wait_ge(shifted, 1)
                fl = mask[:, 0:M, :].rearrange("p t n -> p (t n)")
                act.activation(fl, fl, ACT.Exp).then_inc(exped, 1)


def sample(nc, k, tag, idx, frac, mask, ns, xfirst, row, first):
    ctx, ps = k["ctx"], k["psum"]
    A = k["arena"]
    gat = [A[:, ns * row * i:ns * row * (i + 1)].rearrange("p (s n) -> p s n", s=ns) for i in range(2)]
    at = 2 * ns * row
    w4 = A[:, at:at + 2 * ns * 4].rearrange("p (h s q) -> p h s q", h=2, q=4)
    at += 8 * ns
    S = {n: signal(k, f"{tag}_{n}") for n in
         ("idx0", "idx1", "got0", "got1", "turn", "summed0", "summed1", "turned", "turned_sb",
          "taken", "prod", "act", "add", "steps", "steps_act")}
    stage = k["istage"]
    table = k["tab"].rearrange("r (i n) -> (r i) n", n=row)
    sumw = 128 if first else ns * C
    n_sum = 1 if first else 2
    acc = A[:, at:at + n_sum * sumw].rearrange("p (u n) -> p u n", u=n_sum)
    at += n_sum * sumw
    turned = A[:, at:at + (128 if first else TAPS * 128)]
    at += 128 if first else TAPS * 128
    yb = A[:, at:at + 256]

    def tile(i, h):
        return bass.ds(i * 2 + h, 1)

    with nc.Block() as block:
        @block.gpsimd
        def _(pool):
            with pool.Fori(0, NT) as i:
                for h in range(2):
                    pool.wait_ge(S[f"summed{h}"], i + 1)
                    pool.wait_ge(S[f"idx{h}"], i + 1)
                    pool.sem_inc(S["turn"], 1)
                    for s in range(ns):
                        pool.indirect_dma_start(
                            out=gat[h][:, s, :], out_offset=None, in_=table,
                            in_offset=bass.IndirectOffsetOnAxis(ap=stage[:, h, s:s + 1], axis=0)
                        ).then_inc(S[f"got{h}"], 16)

        @block.vector
        def _(v):
            step = Chain(v, S["steps"])
            for h in range(2):
                v.sem_inc(S[f"summed{h}"], 1)
                v.tensor_copy(stage[:, h, 0:ns], idx[:, h, :]).then_inc(S[f"idx{h}"], 1)
            per = 6 + 2
            with v.Fori(0, NT) as i, step.body(i, per, NT):
                f4 = frac[:, bass.ds(i * 2, 2), :].rearrange("p t (s a) -> p t s a", a=2)
                wy, wx = (f4[:, :, :, 1], f4[:, :, :, 0]) if xfirst else (f4[:, :, :, 0], f4[:, :, :, 1])
                m = mask[:, bass.ds(i * 2, 2), :] if first else k["ones"][:, 0:1].unsqueeze(2).to_broadcast([128, 2, ns])
                w = [w4[:, :, :, q] for q in range(4)]
                step(v.tensor_tensor(w[2], m, wy, ALU.mult))
                step(v.tensor_tensor(w[0], m, w[2], ALU.subtract))
                step(v.tensor_tensor(w[3], w[2], wx, ALU.mult))
                step(v.tensor_tensor(w[1], w[0], wx, ALU.mult))
                step(v.tensor_tensor(w[2], w[2], w[3], ALU.subtract))
                step(v.tensor_tensor(w[0], w[0], w[1], ALU.subtract))
                for h in range(2):
                    v.wait_ge(S[f"got{h}"], (i + 1) * (16 * ns))
                    v.tensor_copy(stage[:, h, 0:ns], idx[:, tile(i + 1, h), :].rearrange("p a s -> p (a s)"))\
                        .then_inc(S[f"idx{h}"], 1)
                    n = row // 4
                    g4 = gat[h].rearrange("p s (q n) -> p (s q) n", n=n)
                    wb = w4[:, h, :, :].rearrange("p s q -> p (s q)").unsqueeze(2).to_broadcast([128, 4 * ns, n])
                    step(v.tensor_tensor(g4, g4, wb, ALU.mult))
                    if first:
                        if h == 0:
                            v.wait_ge(S["taken"], i + 1)
                        v.tensor_reduce(
                            acc[:, 0, 64 * h:64 * h + 64].rearrange("p (g n) -> p g n", g=G),
                            gat[h].rearrange("p (g s) (q n) -> p g n (s q)", g=G, n=n), AX.X, ALU.add)\
                            .then_inc(S[f"summed{h}"], 1)
                    else:
                        v.wait_ge(S["taken"], i * 2 + h + 1)
                        v.tensor_reduce(acc[:, h, :].rearrange("p (s n) -> p s n", n=C),
                                        gat[h].rearrange("p s (q n) -> p s n q", n=n), AX.X, ALU.add)\
                            .then_inc(S[f"summed{h}"], 1)
                if first:
                    v.wait_ge(S["act"], i + 1)
                    xs = k["x"][:, bass.ds(i * PT, PT)]
                    v.tensor_tensor(yb[:, 0:128], yb[:, 0:128], yb[:, 128:256], ALU.mult).then_inc(S["prod"], 1)
                    v.wait_ge(S["prod"], i + 1)
                    v.tensor_tensor(xs, xs, yb[:, 0:128], ALU.add).then_inc(S["add"], 1)

        if first:
            @block.tensor
            def _(pe):
                pe.sem_inc(S["taken"], 1)
                with pe.Fori(0, NT) as i:
                    pe.wait_ge(S["summed0"], i + 2)
                    pe.wait_ge(S["summed1"], i + 2)
                    pe.transpose(ps[:, 0:128], acc[:, 0, :], k["ident"][:, :]).then_inc(S["taken"], 1)
                    pe.wait_ge(S["turned_sb"], i + 1)
                    pe.matmul(ps[:, 512:640], k["wout"][:, :], turned, start=True, stop=True)\
                        .then_inc(S["turned"], 1)

            @block.scalar
            def _(act):
                act.sem_inc(S["add"], 1)
                with act.Fori(0, NT) as i:
                    act.wait_ge(S["taken"], i + 2)
                    act.activation(turned, ps[:, 0:128], ACT.Copy).then_inc(S["turned_sb"], 1)
                    act.wait_ge(S["turned"], i + 1)
                    act.wait_ge(S["add"], i + 1)
                    act.activation(yb[:, 0:128], ps[:, 512:640], ACT.Identity, scale=k["bn"][:, 2:3],
                                   bias=k["bn"][:, 5:6])
                    act.activation(yb[:, 128:256], ps[:, 512:640], ACT.Sigmoid, scale=k["bn"][:, 2:3],
                                   bias=k["bn"][:, 5:6]).then_inc(S["act"], 1)
        else:
            sc = k["sc"]

            @block.tensor
            def _(pe):
                pe.sem_inc(S["taken"], 2)
                with pe.Fori(0, NT) as i:
                    for h in range(2):
                        n = i * 2 + h + 1
                        pe.wait_ge(S[f"summed{h}"], i + 2)
                        for m in range(TAPS):
                            mm = pe.transpose(ps[:, 128 * m:128 * m + 128], acc[:, h, 128 * m:128 * m + 128],
                                              k["ident"][:, :])
                        mm.then_inc(S["taken"], 1)
                        pe.wait_ge(S["turned_sb"], n)
                        for m in range(TAPS):
                            mm = pe.matmul(ps[:, 2048:2176], k["dws2"][:, m, :], turned[:, 128 * m:128 * m + 128],
                                           start=(m == 0), stop=(m == TAPS - 1))
                        mm.then_inc(S["prod"], 1)

            @block.scalar
            def _(act):
                with act.Fori(0, NT) as i:
                    for h in range(2):
                        n = i * 2 + h + 1
                        act.wait_ge(S["taken"], n + 2)
                        act.activation(turned, ps[:, 0:TAPS * 128], ACT.Copy).then_inc(S["turned_sb"], 1)
                        act.wait_ge(S["prod"], n)
                        act.activation(sc[:, h, bass.ds(i * PT, PT)], ps[:, 2048:2176], ACT.Identity,
                                       bias=k["dbs"][:, 0:1])


NO1 = 2 * S1
R3 = 3 * NO1
K3 = R3 + 1


def offsets1(nc, k, raw, o3, w):
    ps, xp = k["psum"], k["xp"]
    y = [w[0:R3, CH * h:CH * h + CH] for h in range(2)]
    hi = [w[0:R3, CH * 2 + CH // 2 * h:CH * 2 + CH // 2 * (h + 1)].bitcast(mybir.dt.bfloat16) for h in range(2)]
    S = {n: signal(k, "off1_" + n) for n in ("conv_ps", "raw", "rep_ps", "y", "hi", "dropped", "o3", "ones")}
    p_c = ps[0:2 * NO1, 0:CH]
    p_y = [ps[0:R3, 512 * (1 + h):512 * (1 + h) + CH] for h in range(2)]

    def turns(eng):
        for b2 in range(2):
            with eng.Fori(0, CPI) as r:
                yield b2, r, b2 * CPI + r + 1

    with nc.Block() as block:
        @block.gpsimd
        def _(pool):
            pool.memset(o3, 1.0).then_inc(S["ones"], 1)

        @block.tensor
        def _(pe):
            pe.sem_inc(S["raw"], 1)
            pe.sem_inc(S["y"], 2)
            for b2, r, n in turns(pe):
                pe.wait_ge(S["raw"], n)
                for t in range(TAPS):
                    mm = pe.matmul(p_c.rearrange("p (y x) -> p y x", y=ROWS), k["offw"][:, t, :],
                                   chunk_window(xp, b2, r, t), start=(t == 0), stop=(t == TAPS - 1))
                mm.then_inc(S["conv_ps"], 1)
                pe.wait_ge(S["raw"], n + 1)
                pe.wait_ge(S["y"], n * 2)
                for h in range(2):
                    mm = pe.matmul(p_y[h], k["rep1"][:, h, :], raw[:, bass.ds(r * CH + b2 * PIX, CH)],
                                   start=True, stop=True)
                mm.then_inc(S["rep_ps"], 1)

        @block.scalar
        def _(act):
            act.wait_ge(S["ones"], 1)
            for b2, r, n in turns(act):
                for q in range(2):
                    for h in range(2):
                        if q == 0:
                            act.wait_ge(S["y"], (n - 1) * 2 + (h + 3))
                        else:
                            act.wait_ge(S["dropped"], (n - 1) * 4 + (h + 1))
                        act.activation(hi[h], y[h], ACT.Copy).then_inc(S["hi"], 1)
                for h in range(2):
                    act.wait_ge(S["dropped"], (n - 1) * 4 + (h + 3))
                    act.activation(o3[0:R3, bass.ds(r * CH + (2 * h + b2) * PIX, CH)], y[h], ACT.Copy)\
                        .then_inc(S["o3"], 1)

        @block.vector
        def _(v):
            v.sem_inc(S["o3"], 2)
            for b2, r, n in turns(v):
                v.wait_ge(S["conv_ps"], n)
                v.tensor_scalar(raw[:, bass.ds(r * CH + b2 * PIX, CH)], p_c, k["offb"][:, 0:1], None, ALU.add)\
                    .then_inc(S["raw"], 1)
                v.wait_ge(S["rep_ps"], n)
                for h in range(2):
                    v.wait_ge(S["o3"], (n - 1) * 2 + (h + 1))
                    v.tensor_tensor(y[h], p_y[h], k["rel1"][0:R3, :], ALU.add).then_inc(S["y"], 1)
                for q in range(2):
                    for h in range(2):
                        v.wait_ge(S["hi"], (n - 1) * 4 + (2 * q + h + 1))
                        v.scalar_tensor_tensor(y[h], hi[h], k["drop"][0:R3, q:q + 1], y[h], ALU.mult, ALU.add)\
                            .then_inc(S["dropped"], 1)


def widest1(nc, k, raw):
    ps, st, n = k["psum"], k["small"], 2 * NO1
    S = {n_: signal(k, "wide1_" + n_) for n_ in ("top", "turned", "steps", "flag")}
    with nc.Block() as block:
        @block.vector
        def _(v):
            step = Chain(v, S["steps"])
            v.tensor_reduce(st[0:n, 0:1], raw, AX.X, ALU.max, apply_absolute_value=True).then_inc(S["top"], 1)
            v.wait_ge(S["turned"], 1)
            step(v.tensor_reduce(st[0:1, 1:2], ps[0:1, 0:n], AX.X, ALU.max))
            v.tensor_scalar(k["flag"][:, :], st[0:1, 1:2], 2.0, None, ALU.is_gt).then_inc(S["flag"], 1)

        @block.tensor
        def _(pe):
            pe.wait_ge(S["top"], 1)
            pe.transpose(ps[0:1, 0:n], st[0:n, 0:1], k["ident"][0:n, 0:n]).then_inc(S["turned"], 1)


def turn_offsets1(nc, k, raw, om, w):
    ps, d = k["psum"], k["dram"]
    NO = 2 * NO1
    xs = w[0:NO, 0:CH]
    S = {n: signal(k, "to1_" + n) for n in ("xs", "turned", "om", "cleared", "loaded")}

    def turns(eng):
        for b2 in range(2):
            with eng.Fori(0, CPI) as r:
                yield b2, r, b2 * CPI + r + 1

    with nc.Block() as block:
        @block.scalar
        def _(act):
            act.sem_inc(S["turned"], 1)
            for b2, r, n in turns(act):
                act.wait_ge(S["turned"], n)
                act.activation(xs, raw[:, bass.ds(r * CH + b2 * PIX, CH)], ACT.Copy).then_inc(S["xs"], 1)

        @block.tensor
        def _(pe):
            pe.sem_inc(S["om"], 1)
            for b2, r, n in turns(pe):
                pe.wait_ge(S["xs"], n)
                pe.wait_ge(S["om"], n)
                for t in range(TPC):
                    mm = pe.transpose(ps[:, NO * t:NO * t + NO], xs[:, PT * t:PT * t + PT], k["ident"][0:NO, 0:NO])
                mm.then_inc(S["turned"], 1)

        @block.vector
        def _(v):
            for b2, r, n in turns(v):
                v.wait_ge(S["turned"], n + 1)
                v.tensor_copy(om[:, bass.ds((r + b2 * CPI) * (2 * TPC), 2 * TPC), :]
                              .rearrange("p t n -> p (t n)"), ps[:, 0:TPC * NO]).then_inc(S["om"], 1)

        @block.gpsimd
        def _(pool):
            pool.memset(k["dws2_flat"], 0.0).then_inc(S["cleared"], 1)

        @block.sync
        def _(sp):
            sp.wait_ge(S["cleared"], 1)
            for m in range(TAPS):
                for u in range(2):
                    s = 2 * m + u
                    v, tap = s // TAPS, s % TAPS
                    sp.dma_start(k["dws2"][64 * u:64 * u + 64, m, 64 * v:64 * v + 64], d["dws"][v, tap])\
                        .then_inc(S["loaded"], 16)
            sp.wait_ge(S["loaded"], 16 * S1)


def windows1(nc, k, o3, bmat, win, sc, smp, tmp):
    ps = k["psum"]
    S = {n: signal(k, "win_" + n) for n in
         ("loaded0", "loaded1", "spread", "abs", "hat_x", "z", "b", "pe_turn", "pool_turn", "clamped", "sampled", "kept", "conv", "sc")}
    NQ = NB * CPI
    NTX = WW // IW
    PAIRS = 2 * (NTX // 2)
    ROWP = 3
    p_d = [ps[0:KW, 1024 * i:1024 * i + 1024].rearrange("p (a n) -> p a n", a=2)[:, :, 0:CH] for i in range(2)]
    mag = [tmp[0:KW, 2 * CH * i:2 * CH * i + 2 * CH].rearrange("p (a n) -> p a n", a=2) for i in range(2)]
    pq = [ps[:, 512 * (4 + i):512 * (4 + i) + TAPS * IH * 2 * IW] for i in range(2)]
    pc = [ps[64 * v:64 * v + 64, 512 * (6 + v):512 * (6 + v) + CH] for v in range(2)]
    S4 = smp.rearrange("p (s y x) -> p s y x", s=TAPS, y=ROWS)

    def walk(eng, gen, mul):
        gen(eng, 0, 0, None)
        with eng.Fori(0, NQ // 2 - 1) as i:
            for par in range(2):
                gen(eng, i * 2 + (par + 1), 1 - par, lambda part, n=i * 2 + par, p=par: mul(eng, n, p, part))
        gen(eng, NQ - 1, 1, lambda part: mul(eng, NQ - 2, 0, part))
        for part in range(S1):
            mul(eng, NQ - 1, 1, part)

    POOLED = 5
    assert 1 + PAIRS + TAPS == S1

    with nc.Block() as block:
        @block.sync
        def _(sp):
            phased = k["xw"].rearrange("b y (j t) c -> b (y j) t c", j=IW)
            for b in range(NB):
                with sp.Fori(0, CPI // 2) as i:
                    for par in range(2):
                        sp.wait_ge(S["sampled"], (i * 2 + (par + b * CPI + 1)) * PAIRS)
                        for band in range(2):
                            for a in range(2):
                                src = phased[b, bass.ds(i * (2 * ROWS * IW) + (par * ROWS + band * IH) * IW, WH * IW),
                                             a:a + WW // IW, :]
                                sp.dma_start(win[par][KW // 2 * a:KW // 2 * (a + 1), band, :, :], src)\
                                    .then_inc(S[f"loaded{par}"], 16)

        @block.tensor
        def _(pe):
            def gen(pe, n, par, mul):
                for s in range(S1):
                    c = n * S1 + (s + 1)
                    pe.wait_ge(S["abs"], c)
                    for a in range(2):
                        mm = pe.matmul(p_d[s % 2][:, a, :], k["sel1"][:, 2 * s + a, :], o3[:, chunk_cols(n)],
                                       start=True, stop=True)
                    mm.then_inc(S["spread"], 1)
                    if mul is not None:
                        mul(s)

            def mul(pe, n, par, part):
                if part == 1:
                    pe.wait_ge(S["b"], n * POOLED + POOLED)
                    pe.wait_ge(S["clamped"], n + 1)
                    pe.wait_ge(S[f"loaded{par}"], (n - par) * 32 + 64)
                if 1 <= part <= PAIRS:
                    band, pair = divmod(part - 1, NTX // 2)
                    pe.wait_ge(S["kept"], n * PAIRS + part)
                    out = pq[part % 2].rearrange("p (s y x) -> p s y x", s=TAPS, y=IH)
                    for t in range(2):
                        tile = 2 * pair + t
                        for v in range(2):
                            rhs = bmat[par].rearrange("p (s y x) -> p s y x", s=S1, y=ROWS)[
                                :, TAPS * v:TAPS * v + TAPS, IH * band:IH * band + IH, IW * tile:IW * tile + IW]
                            mm = pe.matmul(out[64 * v:64 * v + 64, :, :, IW * t:IW * t + IW],
                                           win[par][0:KW, band, tile, :], rhs, start=True, stop=True,
                                           skip_group_check=True)
                    mm.then_inc(S["sampled"], 1)
                elif part > PAIRS:
                    t = part - PAIRS - 1
                    if t == 0:
                        pe.wait_ge(S["kept"], n * PAIRS + (PAIRS + 2))
                        pe.wait_ge(S["sc"], n + 1)
                        pe.sem_inc(S["pe_turn"], 1)
                    for v in range(2):
                        mm = pe.matmul(pc[v], k["dws"][64 * v:64 * v + 64, t, :],
                                       smp[64 * v:64 * v + 64, CH * t:CH * t + CH],
                                       start=(t == 0), stop=(t == TAPS - 1))
                    if t == TAPS - 1:
                        mm.then_inc(S["conv"], 1)

            pe.sem_inc(S["abs"], 2)
            pe.sem_inc(S["kept"], 2)
            pe.sem_inc(S["sc"], 1)
            pe.sem_inc(S["sampled"], 2 * PAIRS)
            walk(pe, gen, mul)

        @block.scalar
        def _(act):
            def gen(act, n, par, mul):
                for s in range(S1):
                    c = n * S1 + (s + 1)
                    act.wait_ge(S["z"], c)
                    act.wait_ge(S["spread"], c)
                    act.activation(mag[s % 2], p_d[s % 2], ACT.Abs).then_inc(S["abs"], 1)
                    if mul is not None:
                        mul(s)

            def mul(act, n, par, part):
                if part == 0:
                    act.wait_ge(S["z"], n * S1 + (S1 + 2))
                    last = bmat[par][:, CH * ROWP * POOLED:]
                    act.activation(last, last, ACT.Relu).then_inc(S["clamped"], 1)
                elif part <= PAIRS:
                    band, pair = divmod(part - 1, NTX // 2)
                    act.wait_ge(S["sampled"], n * PAIRS + (part + 2 * PAIRS))
                    if part == 1:
                        act.wait_ge(S["conv"], n + 1)
                    act.activation(S4[:, :, IH * band:IH * band + IH, 2 * IW * pair:2 * IW * pair + 2 * IW],
                                   pq[part % 2].rearrange("p (s y x) -> p s y x", s=TAPS, y=IH), ACT.Copy)\
                        .then_inc(S["kept"], 1)

            act.sem_inc(S["z"], 2)
            act.sem_inc(S["conv"], 1)
            walk(act, gen, mul)

        @block.vector
        def _(v_):
            def gen(v_, n, par, mul):
                for s in range(S1):
                    c = n * S1 + (s + 1)
                    v_.wait_ge(S["abs"], c + 2)
                    v_.tensor_scalar(mag[s % 2][:, 1, :], mag[s % 2][:, 1, :], 1.0, 1.0, ALU.min, ALU.subtract)\
                        .then_inc(S["hat_x"], 1)
                    v_.wait_ge(S["hat_x"], c)
                    if s == 0:
                        v_.wait_ge(S["sampled"], (n + 1) * PAIRS)
                    v_.scalar_tensor_tensor(bmat[par][:, CH * s:CH * s + CH], mag[s % 2][:, 0, :], 1.0,
                                            mag[s % 2][:, 1, :],
                                            ALU.subtract, ALU.mult).then_inc(S["z"], 1)
                    if mul is not None:
                        mul(s)

            def mul(v_, n, par, part):
                if part == S1 - 1:
                    v_.wait_ge(S["conv"], n + 2)
                    for v in range(2):
                        last = v_.tensor_scalar(sc_cols(sc, n)[64 * v:64 * v + 64, :], pc[v],
                                                k["dbs"][64 * v:64 * v + 64, 0:1], None, ALU.add)
                    last.then_inc(S["sc"], 1)

            walk(v_, gen, mul)

        @block.gpsimd
        def _(pool):
            def gen(pool, n, par, mul):
                for g in range(POOLED):
                    pool.wait_ge(S["z"], n * S1 + (ROWP * (g + 1) + 2))
                    pool.sem_inc(S["pool_turn"], 1)
                    part = bmat[par][:, CH * ROWP * g:CH * ROWP * (g + 1)]
                    pool.tensor_scalar(part, part, 0.0, None, ALU.max).then_inc(S["b"], 1)

            walk(pool, gen, lambda *a: None)


def chunk_cols(n):
    return bass.ds(n * CH, CH)


def sc_cols(sc, n):
    return sc.rearrange("p h n -> p (h n)")[:, chunk_cols(n)]


def fuse1(nc, k):
    ctx, ps = k["ctx"], k["psum"]
    sc, xn, x, st = k["sc"], k["xn"], k["x"], k["small"]
    S = {n: signal(k, "fuse_" + n) for n in
         ("v", "pe", "act", "steps", "mix_ps", "mixed", "gated", "cleared", "gsteps")}
    pool4, gm = st[:, 0:4], st[:, 4:6]
    h8, lg, wts = st[0:8, 8:12], st[0:4, 12:14], st[0:4, 16:18]
    wide = k["wide"]
    g1, g2, gate = st[0:32, 20:24], st[0:32, 24:28], st[:, 28:32]
    mixw = k["mixw"]
    with nc.Block() as block:
        @block.vector
        def _(v):
            step = Chain(v, S["steps"])
            v.memset(k["mixw_flat"], 0.0)
            step(v.tensor_reduce(pool4, sc.rearrange("p h (b n) -> p (h b) n", b=2), AX.X, ALU.add))
            step(v.tensor_reduce(gm, xn[:, :].rearrange("p (b n) -> p b n", b=2), AX.X, ALU.add))
            v.tensor_scalar(st[:, 0:6], st[:, 0:6], 1.0 / PIX, None, ALU.mult).then_inc(S["v"], 1)
            v.wait_ge(S["pe"], 2)
            step(v.tensor_tensor(lg, ps[0:4, 2048:2050], k["wgb2"][:, :], ALU.add))
            step(v.tensor_reduce(st[0:4, 14:15], lg, AX.X, ALU.max, negate=True))
            v.tensor_scalar(lg, lg, st[0:4, 14:15], None, ALU.add).then_inc(S["v"], 1)
            v.wait_ge(S["act"], 2)
            step(v.tensor_reduce(st[0:4, 14:15], wts, AX.X, ALU.add))
            step(v.reciprocal(st[0:4, 15:16], st[0:4, 14:15]))
            step(v.tensor_scalar(wts, wts, st[0:4, 15:16], None, ALU.mult))
            v.tensor_copy(wide[:, :].rearrange("b (v c) -> b v c", v=2),
                          wts.unsqueeze(2).to_broadcast([4, 2, C])).then_inc(S["v"], 1)
            v.wait_ge(S["pe"], 3)
            step(v.tensor_copy(st[:, 32:36], ps[:, 2560:2564]))
            for b in range(NB):
                h = b // 2
                last = v.tensor_scalar(mixw[:, b, 64 * h:64 * h + 64], k["stack2"][:, :], st[:, 32 + b:33 + b],
                                       None, ALU.mult)
            last.then_inc(S["v"], 1)
            v.wait_ge(S["act"], 5)
            for b2 in range(2):
                with v.Fori(0, CPI) as r, step.body(r, 1, CPI):
                    n = b2 * CPI + r + 1
                    v.wait_ge(S["gated"], n)
                    v.wait_ge(S["mix_ps"], n)
                    xs = x[:, bass.ds(r * CH + b2 * PIX, CH)]
                    step(v.tensor_tensor(xs, xs, ps[:, 512:512 + CH], ALU.add))
                    v.tensor_tensor(xs, xs, k["gx"][:, :], ALU.add).then_inc(S["mixed"], 1)

        @block.tensor
        def _(pe):
            pe.wait_ge(S["v"], 1)
            pe.matmul(ps[0:8, 0:4], k["wg1T"][:, :], pool4, start=True, stop=True)
            for h in range(2):
                mm = pe.matmul(ps[0:32, 512 * (2 + h):512 * (2 + h) + 2], k["gp1T"][64 * h:64 * h + 64, :],
                               gm[64 * h:64 * h + 64, :], start=True, stop=True)
            mm.then_inc(S["pe"], 1)
            pe.wait_ge(S["act"], 1)
            pe.matmul(ps[0:4, 2048:2050], h8, k["wg2T"][:, :], start=True, stop=True).then_inc(S["pe"], 1)
            pe.wait_ge(S["v"], 3)
            pe.matmul(ps[:, 2560:2564], wide[:, :], k["ident"][0:4, 0:4], start=True, stop=True).then_inc(S["pe"], 1)
            pe.wait_ge(S["act"], 3)
            pe.matmul(ps[0:32, 3072:3076], k["gp2T"][:, :], g1, start=True, stop=True).then_inc(S["pe"], 1)
            pe.wait_ge(S["act"], 4)
            pe.matmul(ps[:, 3584:3588], k["gp3T"][:, :], g2, start=True, stop=True).then_inc(S["pe"], 1)
            pe.wait_ge(S["v"], 4)
            pe.sem_inc(S["mixed"], 1)
            for b2 in range(2):
                with pe.Fori(0, CPI) as r:
                    n = b2 * CPI + r + 1
                    pe.wait_ge(S["mixed"], n)
                    for h in range(2):
                        pe.matmul(ps[:, 512:512 + CH], mixw[:, 2 * h + b2, :],
                                  sc[:, h, bass.ds(r * CH + b2 * PIX, CH)], start=(h == 0), stop=(h == 1))
                    pe.matmul(ps[:, 1024:1024 + CH], k["crT"][:, :], xn[:, bass.ds(r * CH + b2 * PIX, CH)],
                              start=True, stop=True).then_inc(S["mix_ps"], 1)

        @block.scalar
        def _(act):
            act.wait_ge(S["pe"], 1)
            act.activation(g1[:, 0:2], ps[0:32, 1024:1026], ACT.Relu, bias=k["gpb1"][:, 0:1])
            act.activation(g1[:, 2:4], ps[0:32, 1536:1538], ACT.Relu, bias=k["gpb1"][:, 0:1])
            act.activation(h8, ps[0:8, 0:4], ACT.Relu, bias=k["wgb1"][:, 0:1]).then_inc(S["act"], 1)
            act.wait_ge(S["v"], 2)
            act.activation(wts, lg, ACT.Exp).then_inc(S["act"], 1)
            act.wait_ge(S["pe"], 3)
            act.sem_inc(S["act"], 1)
            act.wait_ge(S["pe"], 4)
            act.activation(g2, ps[0:32, 3072:3076], ACT.Relu, bias=k["gpb2"][:, 0:1]).then_inc(S["act"], 1)
            act.wait_ge(S["pe"], 5)
            act.activation(gate, ps[:, 3584:3588], ACT.Sigmoid,
                           bias=k["vec"][:, VC["gp_b3"]:VC["gp_b3"] + 1]).then_inc(S["act"], 1)
            act.wait_ge(S["act"], 5)
            for b2 in range(2):
                for h in range(2):
                    r = slice(64 * h, 64 * h + 64)
                    act.activation(st[r, 36 + b2:37 + b2], gate[r, 2 * h + b2:2 * h + b2 + 1], ACT.Copy)\
                        .then_inc(S["gsteps"], 1)
            act.wait_ge(S["gsteps"], 4)
            act.activation(st[:, 38:40], st[:, 36:38], ACT.Copy,
                           scale=k["vec"][:, VC["cr_b"]:VC["cr_b"] + 1]).then_inc(S["gsteps"], 1)
            act.wait_ge(S["gsteps"], 5)
            for b2 in range(2):
                with act.Fori(0, CPI) as r:
                    n = b2 * CPI + r + 1
                    act.wait_ge(S["mix_ps"], n)
                    act.activation(k["gx"][:, :], ps[:, 1024:1024 + CH], ACT.Identity,
                                   scale=st[:, 36 + b2:37 + b2], bias=st[:, 38 + b2:39 + b2])\
                        .then_inc(S["gated"], 1)


def project2(nc, k, y, t1, t2, parts, at):
    ctx, ps, xn = k["ctx"], k["psum"], k["xn"]
    xs, ya, ta = (k["work2"][:, CH * i:CH * i + CH] for i in range(3))
    S = {n: signal(k, "proj2_" + n) for n in
         ("xs", "ps", "done", "biased", "steps", "part", "rest", "ones")}
    al = k["alphas"]
    with nc.Block() as block:
        @block.gpsimd
        def _(pool):
            pool.memset(at[:, :, C:2 * C], 1.0)
            pool.sem_inc(S["done"], 1)
            for b2 in range(2):
                with pool.Fori(0, CPI) as r:
                    n = b2 * CPI + r + 1
                    pool.wait_ge(S["done"], n)
                    pool.tensor_copy(xs, xn[:, bass.ds(r * CH + b2 * PIX, CH)]).then_inc(S["xs"], 1)

        @block.tensor
        def _(pe):
            for b2 in range(2):
                with pe.Fori(0, CPI) as r:
                    n = b2 * CPI + r + 1
                    pe.wait_ge(S["xs"], n)
                    pe.matmul(ps[:, 0:CH], k["l2w"][:, :], xs, start=True, stop=True)
                    for t in range(TPC):
                        mm = pe.matmul(ps[:, 512 + PT * t:512 + PT * t + PT], xs[:, PT * t:PT * t + PT],
                                       k["waT"][:, :], start=True, stop=True)
                    mm.then_inc(S["ps"], 1)

        @block.scalar
        def _(act):
            for b2 in range(2):
                with act.Fori(0, CPI) as r:
                    n = b2 * CPI + r + 1
                    act.wait_ge(S["ps"], n)
                    act.activation(y[:, bass.ds(r * CH + b2 * PIX, CH)], ps[:, 0:CH], ACT.Identity,
                                   bias=k["l2b"][:, 0:1]).then_inc(S["biased"], 1)
            for q in range(3):
                act.wait_ge(S["rest"], q + 1)
                act.activation(parts[q], (y, t1, t2)[q], ACT.Copy).then_inc(S["part"], 1)

        @block.vector
        def _(v):
            step = Chain(v, S["steps"])
            for b2 in range(2):
                with v.Fori(0, CPI) as r, step.body(r, 2, CPI):
                    n = b2 * CPI + r + 1
                    v.wait_ge(S["ps"], n)
                    step(v.tensor_tensor(ya.rearrange("p (t c) -> p t c", c=C),
                                         ps[:, 512:512 + CH].rearrange("p (t c) -> p t c", c=C),
                                         k["ba"][:, :].unsqueeze(1).to_broadcast([128, 2 * TPC, C]), ALU.add))
                    step(v.tensor_scalar(ta, ya, 0.0, al[:, 1:2], ALU.min, ALU.mult))
                    v.wait_ge(S["biased"], n)
                    for h in range(2):
                        y3 = ya.rearrange("p (t h c) -> p t h c", h=2, c=C)[:, :, h, :]
                        t3 = ta.rearrange("p (t h c) -> p t h c", h=2, c=C)[:, :, h, :]
                        last = v.scalar_tensor_tensor(at[:, bass.ds((r + b2 * CPI) * TPC, TPC), 2 * C * h:2 * C * h + C],
                                                      y3, 0.0, t3, ALU.max, ALU.add)
                    last.then_inc(S["done"], 1)
            step(v.tensor_scalar(t1, y, 0.0, al[:, 0:1], ALU.min, ALU.mult))
            v.scalar_tensor_tensor(y, y, 0.0, t1, ALU.max, ALU.add).then_inc(S["rest"], 1)
            v.wait_ge(S["part"], 1)
            v.tensor_tensor(t1, y, parts[0], ALU.subtract).then_inc(S["rest"], 1)
            v.wait_ge(S["part"], 2)
            v.tensor_tensor(t2, t1, parts[1], ALU.subtract).then_inc(S["rest"], 1)


def stack2(nc, k, parts, qa, ka, qb, kb):
    ctx = k["ctx"]
    stacked = signal(k, "stacked")
    H_, M_, L_ = 0, 1, 2
    plan = [(qa, 0, (H_, H_, M_)), (ka, 1, (H_, M_, H_)), (qb, 0, (M_, L_, H_)), (kb, 1, (M_, H_, L_))]
    with nc.Block() as block:
        def moves(eng, b2):
            for dst, e, order in plan:
                for pos, q in enumerate(order):
                    for h in range(2):
                        u = 2 * b2 + h
                        eng.dma_start(dst[HID * pos:HID * pos + HID, PIX * u:PIX * u + PIX],
                                      parts[q][64 * h + HID * e:64 * h + HID * e + HID, PIX * b2:PIX * b2 + PIX])\
                            .then_inc(stacked, 16)

        @block.sync
        def _(sp):
            moves(sp, 0)
            sp.wait_ge(stacked, 16 * 48)

        @block.scalar
        def _(act):
            moves(act, 1)

        @block.gpsimd
        def _(pool):
            pool.memset(ka[96:99, :], 1.0)


def attend2(nc, k, qa, ka, qb, kb, at):
    ctx, ps, x = k["ctx"], k["psum"], k["x"]
    A = k["atwork"]
    BF = mybir.dt.bfloat16
    SLOTS = 3
    pt = [A[:, CH * i:CH * i + CH] for i in range(SLOTS)]
    recs = [A[:, (SLOTS + i) * CH:(SLOTS + i + 1) * CH] for i in range(2)]
    at0 = (SLOTS + 2) * CH
    part = A[:, at0:at0 + 18]
    mx = A[:, at0 + 18:at0 + 36]
    rest = A[:, at0 + 36:at0 + 72]
    mparts = A[:, at0 + 72:at0 + 99].bitcast(BF)
    mrow = A[:, at0 + 100:at0 + 164].bitcast(BF)
    S = {n: signal(k, "att_" + n) for n in
         ("scores", "probs", "pv", "maxmm", "maxred", "steps", "mparts", "mrow_ps", "mrow", "mset", "added")}
    KA, KB = 3 * HID + 3, 3 * HID
    NJ = TPI
    NS, NM = 3, 3
    p_s = [ps[:, 512 * i:512 * i + CH] for i in range(NS)]
    p_m = [ps[:, 512 * (NS + i):512 * (NS + i) + CH] for i in range(NM)]
    p_o = [ps[:, 3072 + 512 * i:3072 + 512 * i + CH] for i in range(2)]
    p_r = ps[0:3 * NJ, 512 * NS:512 * NS + 64].bitcast(BF)

    def blocks(eng):
        with eng.Fori(0, CPI // 2) as i:
            for par in range(2):
                yield i * 2 + par, par

    def last_step(u, ib):
        return ib * NJ + (u * CPI + 1) * NJ

    with nc.Block() as block:
        @block.gpsimd
        def _(pool):
            pool.memset(k["xp_flat"], 0.0)

        @block.sync
        def _(sp):
            for u in range(NB):
                sp.wait_ge(S["mrow"], u + 1)
                for q in range(3):
                    sp.dma_start(qa[96 + q:97 + q, PIX * u:PIX * u + PIX], mrow[NJ * q:NJ * q + NJ, :])\
                        .then_inc(S["mset"], 16)

        @block.tensor
        def _(pe):
            def maxima(u, ib, j):
                n = ib * NJ + (u * CPI * NJ + j + 1)
                pe.wait_ge(S["maxred"], n)
                pe.matmul(p_m[j % NM], qa[0:KB, bass.ds(ib * CH + (u * PIX + PT * (j // 6)), PT)],
                          ka[0:KB, u * PIX + CH * (j % 6):u * PIX + CH * (j % 6) + CH],
                          start=True, stop=True).then_inc(S["maxmm"], 1)

            def maxrow(u):
                pe.wait_ge(S["mparts"], u + 1)
                pe.transpose(p_r, mparts, k["identb"][:, :]).then_inc(S["mrow_ps"], 1)

            def scores(u, ib, j):
                n = ib * NJ + (u * CPI * NJ + j + 1)
                pe.wait_ge(S["probs"], n)
                q = bass.ds(ib * CH + u * PIX, CH)
                kk = slice(u * PIX + PT * j, u * PIX + PT * j + PT)
                pe.matmul(p_s[j % NS], ka[0:KA, kk], qa[0:KA, q], start=True, stop=False)
                pe.matmul(p_s[j % NS], kb[0:KB, kk], qb[0:KB, q], start=False, stop=True)\
                    .then_inc(S["scores"], 1)

            def values(u, ib, par, j):
                n = ib * NJ + (u * CPI * NJ + j + 1)
                pe.wait_ge(S["probs"], n + NS)
                h, b2 = u % 2, u // 2
                pe.matmul(p_o[par], at[:, b2 * TPI + j, C * h:C * h + 2 * C], pt[j % SLOTS],
                          start=(j == 0), stop=(j == NJ - 1)).then_inc(S["pv"], 1)

            pe.sem_inc(S["maxred"], NM)
            pe.sem_inc(S["probs"], NS)
            pe.sem_inc(S["pv"], SLOTS)
            pe.sem_inc(S["added"], 2)
            with pe.Fori(0, CPI) as ib:
                for j in range(NJ):
                    maxima(0, ib, j)
            maxrow(0)
            for u in range(NB):
                pe.wait_ge(S["mset"], 48 * (u + 1))
                for ib, par in blocks(pe):
                    scores(u, ib, 0)
                    for j in range(NJ):
                        if j + 1 < NJ:
                            scores(u, ib, j + 1)
                        if u + 1 < NB:
                            maxima(u + 1, ib, j)
                        if j == 1:
                            pe.wait_ge(S["added"], ib + (u * CPI + 1))
                        if j >= 1:
                            values(u, ib, par, j - 1)
                    values(u, ib, par, NJ - 1)
                if u + 1 < NB:
                    maxrow(u + 1)

        @block.scalar
        def _(act):
            for u in range(NB):
                with act.Fori(0, CPI) as ib:
                    for j in range(NJ):
                        n = ib * NJ + (u * CPI * NJ + j + 1)
                        act.wait_ge(S["scores"], n)
                        act.wait_ge(S["pv"], n)
                        act.activation(pt[j % SLOTS], p_s[j % NS], ACT.Exp).then_inc(S["probs"], 1)

        @block.vector
        def _(v):
            step = Chain(v, S["steps"])

            def maxima(u, ib):
                for j in range(NJ):
                    v.wait_ge(S["maxmm"], ib * NJ + (u * CPI * NJ + j + 1))
                    v.tensor_reduce(part[:, j:j + 1], p_m[j % NM], AX.X, ALU.max).then_inc(S["maxred"], 1)
                v.wait_ge(S["maxred"], last_step(u, ib) + NM)
                step(v.tensor_reduce(mx[:, bass.ds(ib * 3, 3)], part.rearrange("p (i c) -> p i c", c=6), AX.X,
                                     ALU.max, negate=True))

            def split_maxima(u):
                m = [mparts[:, NJ * q:NJ * q + NJ] for q in range(3)]
                step(v.tensor_copy(m[0], mx))
                step(v.tensor_tensor(rest[:, 0:NJ], mx, m[0], ALU.subtract))
                step(v.tensor_copy(m[1], rest[:, 0:NJ]))
                step(v.tensor_tensor(rest[:, NJ:2 * NJ], rest[:, 0:NJ], m[1], ALU.subtract))
                v.tensor_copy(m[2], rest[:, NJ:2 * NJ]).then_inc(S["mparts"], 1)
                v.wait_ge(S["mrow_ps"], u + 1)
                if u:
                    v.wait_ge(S["mset"], 48 * u)
                v.tensor_copy(mrow[0:3 * NJ, :], p_r).then_inc(S["mrow"], 1)

            with v.Fori(0, CPI) as ib, step.body(ib, 1, CPI):
                maxima(0, ib)
            split_maxima(0)
            for u in range(NB):
                h, b2 = u % 2, u // 2
                more = u + 1 < NB
                per = 3 if more else 2
                start = step.n
                for ib, par in blocks(v):
                    step.off, step.n = ib * per + start, 0
                    if more:
                        maxima(u + 1, ib)
                    v.wait_ge(S["pv"], last_step(u, ib) + SLOTS)
                    own, other = slice(64 * h, 64 * h + 64), slice(64 - 64 * h, 128 - 64 * h)
                    rec = recs[par]
                    v.wait_ge(S["added"], ib + (u * CPI + 1))
                    step(v.reciprocal(rec[own, :], p_o[par][other, :]))
                    step(v.tensor_tensor(rec[own, :], rec[own, :], p_o[par][own, :], ALU.mult))
                    xs = x[own, bass.ds(ib * CH + b2 * PIX, CH)]
                    v.tensor_tensor(xs, xs, rec[own, :], ALU.add).then_inc(S["added"], 1)
                step.off, step.n = 0, start + per * CPI
                if more:
                    split_maxima(u + 1)


def dynamic3(nc, k):
    ctx, ps, x, xn, xp, d = k["ctx"], k["psum"], k["x"], k["xn"], k["xp"], k["dram"]
    A = k["arena"]
    QO = C // 4
    n_w = QO * TAPS * HID
    w2, prod = A[:, 0:2 * n_w], A[:, 2 * n_w:3 * n_w]
    at = 3 * n_w
    gen = A[:, at:at + NB * TAPS * 32].rearrange("p (b t o) -> p b t o", b=NB, t=TAPS)
    at += NB * TAPS * 32
    b2t = A[:, at:at + 32 * TAPS]
    at += 32 * TAPS
    wbd = A[:, at:at + 2 * TAPS * 128].rearrange("p (b t o) -> p b t o", b=2, t=TAPS)
    at += 2 * TAPS * 128
    hb = A[:, at:at + NB * HID].rearrange("p (b n) -> p b n", b=NB)
    at += NB * HID
    pw = A[:, at:at + 2 * 128].rearrange("p (b n) -> p b n", b=2)
    at += 256
    gm = k["small"][:, 4:6]
    S = {n: signal(k, "dyn_" + n) for n in
         ("w2", "steps", "pooled", "h_ps", "gen", "cleared", "moved", "conv_ps", "added", "stored")}
    with nc.Block() as block:
        @block.gpsimd
        def _(pool):
            pool.memset(wbd.rearrange("p b t o -> p (b t o)"), 0.0).then_inc(S["cleared"], 1)

        @block.sync
        def _(sp):
            for half in range(2):
                sp.dma_start(w2[64 * half:64 * half + 64, :].rearrange("c (o n) -> c o n", o=32),
                             d["W2"].rearrange("(a o c t) n -> a c o (t n)", a=2, c=C, t=TAPS)[half])\
                    .then_inc(S["w2"], 16)
                sp.dma_start(b2t[64 * half:64 * half + 64, :].rearrange("c (o n) -> c o n", o=32),
                             d["b2"].rearrange("(a o c t) -> a c o t", a=2, c=C, t=TAPS)[half])\
                    .then_inc(S["w2"], 16)
            sp.wait_ge(S["cleared"], 1)
            for b in range(NB):
                sp.wait_ge(S["gen"], b + 1)
                h = b // 2
                for half in range(2):
                    sp.dma_start(wbd[64 * h:64 * h + 64, b % 2, :, 64 * h + 32 * half:64 * h + 32 * half + 32],
                                 gen[64 * half:64 * half + 64, b, :, :]).then_inc(S["moved"], 16)
            for b2 in range(2):
                with sp.Fori(0, CPI) as r:
                    sp.wait_ge(S["added"], b2 * CPI + r + 2)
                    for h in range(2):
                        sp.dma_start(d["out"].rearrange("b c y x -> b c (y x)")[2 * h + b2, :, bass.ds(r * CH, CH)],
                                     x[64 * h:64 * h + 64, bass.ds(r * CH + b2 * PIX, CH)]).then_inc(S["stored"], 16)
            sp.wait_ge(S["stored"], 2 * 2 * CPI * 16)

        @block.tensor
        def _(pe):
            pe.wait_ge(S["pooled"], 1)
            for b in range(NB):
                h = b // 2
                mm = pe.matmul(ps[:, 512 * b:512 * b + HID], pw[64 * h:64 * h + 64, b % 2, :],
                               k["w31T"][64 * h:64 * h + 64, :], start=True, stop=True)
            mm.then_inc(S["h_ps"], 1)
            pe.wait_ge(S["moved"], 2 * NB * 16)
            pe.sem_inc(S["added"], 1)
            for b2 in range(2):
                with pe.Fori(0, CPI) as r:
                    n = b2 * CPI + r + 1
                    pe.wait_ge(S["added"], n)
                    for t in range(TAPS):
                        mm = pe.matmul(ps[:, 2048:2048 + CH].rearrange("p (y x) -> p y x", y=ROWS),
                                       wbd[:, b2, t, :], chunk_window(xp, b2, r, t),
                                       start=(t == 0), stop=(t == TAPS - 1))
                    mm.then_inc(S["conv_ps"], 1)

        @block.vector
        def _(v):
            step = Chain(v, S["steps"])
            step(v.tensor_reduce(gm, xn[:, :].rearrange("p (b n) -> p b n", b=2), AX.X, ALU.add))
            step(v.tensor_scalar(gm, gm, 1.0 / PIX, None, ALU.mult))
            v.tensor_copy(pw, gm.unsqueeze(2).to_broadcast([128, 2, 128])).then_inc(S["pooled"], 1)
            v.wait_ge(S["h_ps"], 1)
            hps = ps[:, 0:2048].rearrange("p (b n) -> p b n", b=NB)[:, :, 0:HID]
            step(v.tensor_tensor(hb, hps, k["b1_3"][:, :].unsqueeze(1).to_broadcast([128, NB, HID]), ALU.add))
            step(v.tensor_scalar(hb, hb, 0.0, None, ALU.max))
            v.wait_ge(S["w2"], 64)
            for b in range(NB):
                for u in range(2):
                    step(v.tensor_tensor(prod.rearrange("p (m n) -> p m n", n=HID),
                                         w2[:, n_w * u:n_w * u + n_w].rearrange("p (m n) -> p m n", n=HID),
                                         hb[:, b, :].unsqueeze(1).to_broadcast([128, QO * TAPS, HID]), ALU.mult))
                    step(v.tensor_reduce(gen[:, b, :, QO * u:QO * u + QO],
                                         prod.rearrange("p (o t n) -> p t o n", o=QO, t=TAPS), AX.X, ALU.add))
                v.tensor_tensor(gen[:, b, :, :], gen[:, b, :, :], b2t.rearrange("p (o t) -> p t o", t=TAPS),
                                ALU.add).then_inc(S["gen"], 1)
            for b2 in range(2):
                with v.Fori(0, CPI) as r:
                    v.wait_ge(S["conv_ps"], b2 * CPI + r + 1)
                    xs = x[:, bass.ds(r * CH + b2 * PIX, CH)]
                    v.tensor_tensor(xs, xs, ps[:, 2048:2048 + CH], ALU.add).then_inc(S["added"], 1)


def clear_borders(nc, k):
    cleared = signal(k, "borders_cleared")
    with nc.Block() as block:
        @block.gpsimd
        def _(pool):
            pool.memset(k["xp_flat"], 0.0).then_inc(cleared, 1)
            pool.wait_ge(cleared, 1)


def store_x(nc, k):
    stored = signal(k, "dbg_stored")
    with nc.Block() as block:
        @block.sync
        def _(sp):
            for h in range(2):
                sp.dma_start(k["dram"]["out"][2 * h:2 * h + 2].rearrange("b c y x -> c b (y x)"),
                             k["x"][64 * h:64 * h + 64, :].rearrange("c (b n) -> c b n", b=2)).then_inc(stored, 16)
            sp.wait_ge(stored, 32)


STAGES = 4
WIDE = 1


def program(nc, dram):
    with ExitStack() as ctx:
        k = {"ctx": ctx, "dram": dram, "nc": nc, "signals": []}

        def sb(name, shape, dt=F32):
            k[name] = ctx.enter_context(nc.sbuf_tensor(name + "_sb", shape, dt))
            return k[name]

        sb("x", [128, COLS])
        sb("xn", [128, COLS])
        sb("xp", [128, 2, PH, PH])
        for name, shape in [("vec", [128, len(V64)]), ("dw", [128, TAPS]), ("ident", [128, 128]),
                            ("pairm", [128, 128]), ("halfm", [128, 128]), ("b_om", [128, OM]), 
                            ("b1_3", [128, HID]), ("ba", [128, C]), ("offb", [72, 1]), ("dbs", [128, 1]),
                            ("wg1T", [128, 8]), ("wgb1", [8, 1]), ("wg2T", [8, 2]), ("wgb2", [4, 2]),
                            ("gp1T", [128, 32]), ("gpb1", [32, 1]), ("gp2T", [32, 32]), ("gpb2", [32, 1]),
                            ("gp3T", [32, 128]), ("l2b", [128, 1]), ("stack2", [128, 64]), ("alphas", [128, 2]),
                            ("wom", [128, 2 * OM]), ("win", [128, 128]), ("wout", [128, 128]),
                            ("crT", [128, 128]), ("waT", [128, 128]), ("w31T", [128, 32]),
                            ("offw", [128, TAPS, 72]), ("l2w", [128, 128]), ("drop", [R3, 2]),
                            ("eps", [128, 1]), ("ones", [128, 1]), ("dwdiag", [128, TAPS, 128]), ("bn", [128, 6]),
                            ("stats", [128, 12]), ("small", [128, 40]), ("wide", [4, 128]),
                            ("mixw", [128, NB, 128]), ("gx", [128, CH])]:
            if name != "dwdiag":
                sb(name, shape)
        sb("identb", [128, 128], mybir.dt.bfloat16)
        sb("flag", [1, 1], mybir.dt.int32)
        sb("sel", [3 * 2 * G * 5, 5, 128], mybir.dt.bfloat16)
        sb("istage", [128, 2, MG], U32)
        for name in ("wom", "win", "wout", "crT", "waT", "l2w"):
            k[name + "_flat"] = k[name][:, :]
        k["offw_flat"] = k["offw"][:, :, :]
        k["mixw_flat"] = k["mixw"][:, :, :]
        k["xp_flat"] = k["xp"][:, :, :, :].rearrange("p b y x -> p (b y x)")
        AR = 32500
        arena = sb("arena", [128, AR])[:, :]
        k["arena"] = arena
        k["dwdiag"] = arena[:, 15000:15000 + TAPS * 128].rearrange("p (t n) -> p t n", t=TAPS)
        k["psum"] = ctx.enter_context(nc.psum_tensor("ps", [128, 4096], F32))[:, :]
        k["xw"] = nc.dram_tensor("pixel_major", (NB, PW, PW, C), F32).ap()
        k["tab"] = nc.dram_tensor("quads", (NB * TR, TR * 4 * C), F32).ap()

        load_stage(nc, k)
        vector_setup(nc, k)

        xq0 = AR - 2 * PQ * PQ
        k["xproj"] = arena[:, xq0:AR].rearrange("p (b y x) -> p b y x", b=2, y=PQ)
        group_norm(nc, k, "gn0", True)
        M = 2 * NT
        om0 = arena[:, 0:M * OM].rearrange("p (t n) -> p t n", n=OM)
        k["work0"] = arena[:, M * OM:M * OM + 8 * CH]
        offsets0(nc, k, om0)
        window_counts(nc, k, om0)
        wide = nc.values_load(k["flag"][0:1, 0:1], min_val=0, max_val=1)
        with nc.If(wide < WIDE):
            n = M * 2 * MG
            at = M * OM
            hp, hn = arena[:, at:at + n], arena[:, at + n:at + 2 * n]
            at += 2 * n
            A = arena[:, at:at + M * G * W * W]
            assert at + M * G * W * W <= xq0
            BF = mybir.dt.bfloat16
            n = NT * 3 * 2 * G * W * W // 2
            parts = arena[:, 0:n].bitcast(BF)
            parts = parts.rearrange("p (j u q n v) -> p j u q n v", u=W, q=3, n=2 * G, v=W)
            rest = k["rest0"] = arena[:, n:n + M * G * W * W]
            window_weights(nc, k, om0, hp, hn, A, parts, rest, (k["xn"][:, :], k["xp_flat"]))
            att = arena[:, n:n + W * CH // 2].bitcast(BF)
            n += W * CH // 2
            window_taps(nc, k, parts, att, arena[:, n:n + W * W * CH], arena[:, n + W * W * CH:n + (W * W + 2) * CH])
        with nc.Else():
            xq = k["xproj"]
            pixels_out(nc, k, "pix0", lambda b2, r: xq[:, b2, bass.ds(r * ROWS + 2, ROWS), 2:2 + WW],
                       k["work0"])
            at = AR - M * 2 * MG
            frac0 = arena[:, at:AR].rearrange("p (t n) -> p t n", n=2 * MG)
            at -= M * MG
            mask0 = arena[:, at:at + M * MG].rearrange("p (t n) -> p t n", n=MG)
            at -= (M + 2) * MG
            idx0 = arena[:, at:at + (M + 2) * MG].bitcast(U32).rearrange("p (t n) -> p t n", n=MG)
            yield_places(nc, k, "pl0", om0, idx0, frac0, mask0, MG, True, at, AR)
            quads(nc, k, "quads0", G)
            sample(nc, k, "smp0", idx0, frac0, mask0, MG, True, 4 * C // G, True)
        clear_borders(nc, k)
        end_layer(nc, k)
        if STAGES == 1:
            return store_x(nc, k)

        group_norm(nc, k, "gn1", True)
        BF = mybir.dt.bfloat16
        om1 = arena[:, 0:M * NO1].rearrange("p (t n) -> p t n", n=NO1)
        size = S1 * CH
        work1 = arena[:, M * NO1:M * NO1 + 3 * CH]
        at = M * NO1 + 3 * CH
        k["rel1"] = arena[0:R3, at:at + CH]
        k["rep1"] = arena[0:2 * NO1, at + CH:at + CH + 2 * R3].rearrange("p (h n) -> p h n", h=2)
        assert at + CH + 2 * R3 <= size
        bmat = [arena[0:KW, 0:size]]
        o3 = arena[0:K3, size:size + 2 * PIX].bitcast(BF)
        at = size + 2 * PIX

        def window_slot(at):
            return arena[0:KW, at:at + 2 * (WW // IW) * C].rearrange("p (u t c) -> p u t c", u=2, c=C)

        win = [window_slot(at)]
        at += 2 * (WW // IW) * C
        k["dws"] = arena[:, at:at + TAPS * C].rearrange("p (t o) -> p t o", o=C)
        at += TAPS * C
        k["sc"] = arena[:, at:at + 2 * COLS].rearrange("p (h n) -> p h n", h=2)
        raw = arena[0:2 * NO1, at:at + COLS]
        at += 2 * COLS
        k["dws2_flat"] = arena[:, at:at + TAPS * 128]
        k["dws2"] = k["dws2_flat"].rearrange("p (t o) -> p t o", o=128)
        out1 = arena[:, at:at + ROWS * PW + ROWS // 2 * 128]
        low1 = at + TAPS * 128
        bmat.append(arena[0:KW, at:at + size])
        at += size
        win.append(window_slot(at))
        at += 2 * (WW // IW) * C
        k["sel1"] = arena[0:K3, at:at + NO1 * KW // 2].bitcast(BF).rearrange("p (s n) -> p s n", s=NO1)
        assert at + NO1 * KW // 2 <= AR
        loads = [(k["rel1"], dram["rel1"]), (k["rep1"], dram["rep1"]), (k["sel1"], dram["sel1"])] + \
            [(k["dws"][64 * v:64 * v + 64, :, :], dram["dws"][v].rearrange("t c o -> c t o")) for v in range(2)]
        xn = k["xn"]
        pixels_out(nc, k, "pix1", lambda b2, r: xn[:, bass.ds(r * CH + b2 * PIX, CH)]
                   .rearrange("p (y x) -> p y x", y=ROWS), out1, loads)
        offsets1(nc, k, raw, o3, work1)
        widest1(nc, k, raw)
        wide = nc.values_load(k["flag"][0:1, 0:1], min_val=0, max_val=1)
        with nc.If(wide < WIDE):
            smp = k["xp_flat"][:, 0:TAPS * CH]
            windows1(nc, k, o3, bmat, win, k["sc"], smp, k["xp_flat"][:, TAPS * CH:TAPS * CH + 4 * CH])
        with nc.Else():
            turn_offsets1(nc, k, raw, om1, work1)
            at = AR - M * NO1
            frac1 = arena[:, at:AR].rearrange("p (t n) -> p t n", n=NO1)
            at -= (M + 2) * S1
            idx1 = arena[:, at:at + (M + 2) * S1].bitcast(U32).rearrange("p (t n) -> p t n", n=S1)
            assert low1 <= at
            yield_places(nc, k, "pl1", om1, idx1, frac1, None, S1, False, at, AR)
            quads(nc, k, "quads1", 1)
            sample(nc, k, "smp1", idx1, frac1, None, S1, False, 4 * C, False)
        fuse1(nc, k)
        if STAGES == 2:
            return store_x(nc, k)

        group_norm(nc, k, "gn2", False)
        BF = mybir.dt.bfloat16
        stacks = [arena[:, COLS * i:COLS * i + COLS].bitcast(BF) for i in range(4)]
        parts = [k["xn"][:, 0:PIX].bitcast(BF), k["xn"][:, PIX:COLS].bitcast(BF),
                 arena[:, 4 * COLS:4 * COLS + PIX].bitcast(BF)]
        low = 4 * COLS + PIX
        at = arena[:, low:low + NT * 3 * C].rearrange("p (t c) -> p t c", c=3 * C)
        k["work2"] = arena[:, 0:3 * CH]
        project2(nc, k, k["xp_flat"][:, 0:COLS], arena[:, 2 * COLS:3 * COLS], arena[:, 3 * COLS:4 * COLS],
                 parts, at)
        stack2(nc, k, parts, *stacks)
        k["atwork"] = arena[:, low + NT * 3 * C:AR]
        attend2(nc, k, *stacks, at)
        if STAGES == 3:
            return store_x(nc, k)

        group_norm(nc, k, "gn3", True)
        dynamic3(nc, k)


def yield_places(nc, k, tag, om, idx, frac, mask, ns, xfirst, low, AR):
    M = 2 * NT
    base = k[f"base_{tag}"] = k["ctx"].enter_context(nc.sbuf_tensor("base_" + tag, [128, TPI, 2 * ns], F32))
    goff = k["ctx"].enter_context(nc.sbuf_tensor("goff_" + tag, [128, NB, ns], F32))
    loaded = signal(k, tag + "_consts")
    with nc.Block() as block:
        @block.sync
        def _(sp):
            sp.dma_start(base[:, :, :], k["dram"]["base_" + tag]).then_inc(loaded, 16)
            sp.dma_start(goff[:, :, :], k["dram"]["goff_" + tag].partition_broadcast(128)).then_inc(loaded, 16)
            sp.wait_ge(loaded, 32)
    A = k["arena"]
    n = M * 2 * ns
    at = M * om.shape[2]
    assert at + 2 * n <= low
    r1, r2 = A[:, at:at + n], A[:, at + n:at + 2 * n]
    places(nc, k, tag, om, base[:, :, :], goff[:, :, :], idx, frac, ns, xfirst, (r1, r2), mask)


def kernel(**inputs):
    import ml_dtypes
    import numpy as np
    import concourse.bacc as _bacc
    from concourse.bass_utils import run_bass_kernel_spmd as _run

    I = {n: np.asarray(a) for n, a in inputs.items()}
    f = np.float32
    a = {"x": I["x"]}
    L0 = {n[8:]: v for n, v in I.items() if n.startswith("L0_conv_")}
    L1 = {n[8:]: v for n, v in I.items() if n.startswith("L1_conv_")}
    L2 = {n[8:]: v for n, v in I.items() if n.startswith("L2_conv_")}
    L3 = {n[8:]: v for n, v in I.items() if n.startswith("L3_conv_")}
    vecs = dict(L0, gp_b3=L1["gp_b3"], cr_b=L1["cr_b"])
    a["vec64"] = np.stack([vecs[n] for n in V64], 1)
    a["dw_w"] = L0["dw_w"].reshape(C, TAPS)
    a["ident"] = np.eye(128, dtype=f)
    rows = np.arange(3 * 2 * G * 5)
    a["sel"] = ((rows % 5)[:, None, None] == np.arange(5)[None, :, None]) & \
        (((rows // 5) % (2 * G))[:, None, None] == (np.arange(128) // 16)[None, None, :])
    a["sel"] = a["sel"].astype(ml_dtypes.bfloat16)
    a["pairm"] = np.kron(np.eye(64), np.full((2, 2), 1.0 / (2 * PIX))).astype(f)
    a["halfm"] = np.kron(np.eye(2), np.full((64, 64), 1.0 / 64)).astype(f)
    a["stack2"] = np.concatenate([np.eye(64, dtype=f)] * 2, 0)
    a["b_om"] = np.concatenate([L0["b_off"], L0["b_mask"]])
    a["b1_3"] = L3["b1"]
    a["ba"] = L2["ba"]
    a["offb"] = np.concatenate([L1["off_b0"], L1["off_b1"]] * 2)[:, None]
    a["dbs"] = np.concatenate([L1["db0"], L1["db1"]])[:, None]
    a["wg1T"] = L1["wg_w1"].T
    a["wgb1"] = L1["wg_b1"][:, None]
    a["wg2T"] = L1["wg_w2"].T
    a["wgb2"] = L1["wg_b2"]
    a["gp1T"] = np.concatenate([L1["gp_w1"].T] * 2, 0)
    a["gpb1"] = L1["gp_b1"][:, None]
    a["gp2T"] = L1["gp_w2"].T
    a["gpb2"] = L1["gp_b2"][:, None]
    a["gp3T"] = np.concatenate([L1["gp_w3"].T] * 2, 1)
    a["l2b"] = np.concatenate([L2["b1"], L2["b2"]] * 2)[:, None]
    a["alphas"] = np.stack([np.concatenate([np.broadcast_to(L2[n], HID) for n in ("a1", "a2")] * 2),
                            np.broadcast_to(L2["aa"], 128)], 1)
    a["w_om"] = np.concatenate([L0["w_off"], L0["w_mask"]], 1)
    a["w_in"] = L0["w_in"]
    a["w_out"] = L0["w_out"]
    a["crT"] = L1["cr_w"].T
    a["waT"] = L2["wa"].T
    a["w31T"] = L3["W1"].T
    a["offw"] = np.concatenate([L1["off_w0"], L1["off_w1"]], 0).reshape(36, C, TAPS).transpose(1, 2, 0)
    a["l2w"] = np.concatenate([L2["w1"].T, L2["w2"].T], 1)
    a["dws"] = np.stack([L1["dw0"], L1["dw1"]]).reshape(2, C, C, TAPS).transpose(0, 3, 2, 1)
    row = np.arange(R3) % NO1
    tap, axis = row // 2 % TAPS, row % 2
    y, xx = np.divmod(np.arange(CH), WW)
    a["rel1"] = np.where(axis[:, None] == 0, y % IH + tap[:, None] // 3 + 2,
                         xx % IW + tap[:, None] % 3 + 2).astype(f)
    a["drop"] = np.stack([np.arange(R3) >= NO1, np.arange(R3) >= 2 * NO1], 1).astype(f) * f(-1)
    half, i, j = (v.ravel() for v in np.meshgrid(range(2), range(WH), range(IW), indexing="ij"))
    own = -np.stack([i, IW * half + j])[np.arange(NO1) % 2][None]
    spread = np.repeat((row[:, None] == np.arange(NO1))[:, :, None], KW, 2)
    a["sel1"] = np.concatenate([spread, own]).astype(ml_dtypes.bfloat16)
    a["rep1"] = (np.arange(2 * NO1)[:, None, None] == NO1 * np.arange(2)[:, None] + row).astype(f)
    a["W2"] = L3["W2"]
    a["b2"] = L3["b2"]
    pix = np.arange(PIX).reshape(TPI, PT).T
    y, xx = pix // WW, pix % WW
    tap = np.arange(TAPS)
    b0 = np.stack([xx[..., None] + tap // 3, y[..., None] + tap % 3], -1)
    a["base_pl0"] = np.tile(b0[:, :, None], (1, 1, G, 1, 1)).reshape(128, TPI, 2 * MG).astype(f)
    b1 = np.stack([y[..., None] + tap // 3, xx[..., None] + tap % 3], -1)
    a["base_pl1"] = np.tile(b1[:, :, None], (1, 1, 2, 1, 1)).reshape(128, TPI, 2 * S1).astype(f)
    img = np.arange(NB) * TR * TR
    a["goff_pl0"] = (img[:, None] * G + np.repeat(np.arange(G), TAPS)[None]).astype(f)
    a["goff_pl1"] = np.repeat(img[:, None], S1, 1).astype(f)

    nc = _bacc.Bacc("TRN2", target_bir_lowering=False, num_devices=1)
    arrays, dram = {}, {}
    for n, v in a.items():
        arrays["in_" + n] = np.ascontiguousarray(v)
        dram[n] = nc.dram_tensor("in_" + n, arrays["in_" + n].shape,
                                 mybir.dt.from_np(arrays["in_" + n].dtype), kind="ExternalInput").ap()
    dram["out"] = nc.dram_tensor("out_x", (NB, C, HH, WW), F32, kind="ExternalOutput").ap()
    program(nc, dram)
    r = _run(nc, [arrays], core_ids=[0])
    return r.results[0]["out_x"]
```

```python
import concourse.bass as bass
from concourse import mybir
from contextlib import ExitStack, contextmanager

F32 = mybir.dt.float32
U32 = mybir.dt.uint32
ALU = mybir.AluOpType
ACT = mybir.ActivationFunctionType
AX = mybir.AxisListType

NB, C, HH, WW = 4, 64, 48, 48
PIX = HH * WW
COLS = 2 * PIX
PT = 128
TPI = PIX // PT
NT = 2 * TPI
PH = HH + 2
PQ = HH + 4
PW = HH + 6
IH, IW = 4, 6
WH, WX = IH + 6, IW + 6
KW = WH * WX
TAPS = 9
G = 4
ROWS = 8
CH = ROWS * WW
CPI = HH // ROWS
TPC = CH // PT
TR = PH - 1
ROUND = 12582912.0
MG = G * TAPS
OM = 3 * MG
S1 = 2 * TAPS
HID = 32

V64 = ["b_in", "dw_b", "ln_g", "ln_b", "b_out", "bn_g", "bn_b", "bn_mean", "bn_var", "gp_b3", "cr_b"]
VC = {n: i for i, n in enumerate(V64)}


class Chain:

    def __init__(self, eng, sem):
        self.eng, self.sem, self.off, self.n = eng, sem, 0, 0

    def __call__(self, ins):
        self.n += 1
        ins.then_inc(self.sem, 1)
        self.eng.wait_ge(self.sem, self.off + self.n)

    @contextmanager
    def body(self, i, per, count):
        before, self.off, self.n = self.n, self.n + i * per, 0
        yield
        assert self.n == per, self.n
        self.off, self.n = 0, before + per * count


def signal(k, name):
    k["signals"].append(k["nc"].alloc_semaphore(name))
    return k["signals"][-1]


def end_layer(nc, k):
    nc.all_engine_barrier()
    nc.clear_and_free_semaphores(k["signals"])
    nc.all_engine_barrier()
    k["signals"] = []


def load_stage(nc, k):
    d = k["dram"]
    t_x = k["x"]
    x_loaded = signal(k, "x_loaded")
    cleared = signal(k, "weights_cleared")
    loads = []

    def load(dst, src):
        loads.append((dst, src))

    for h in range(2):
        load(k["vec"][64 * h:64 * h + 64, :], d["vec64"])
        load(k["dw"][64 * h:64 * h + 64, :], d["dw_w"])
    load(k["ident"][:, :], d["ident"])
    load(k["sel"][:, :, :], d["sel"])
    load(k["halfm"][:, :], d["halfm"])
    for name in ("b_om", "ba"):
        load(k[name][:, :], d[name].partition_broadcast(128))
    for name in ("offb", "dbs", "wg1T", "wgb1", "wg2T", "gp1T", "gpb1", "gp2T", "gpb2", "gp3T",
                 "l2b", "stack2", "drop", "b1_3"):
        load(k[name][:, :], d[name])
    load(k["wgb2"][:, :], d["wgb2"].partition_broadcast(4))
    load(k["alphas"][:, :], d["alphas"])
    zero = k["arena"][:, 0:3 * PW * C // 4]
    for b in range(NB):
        for lo in (0, PW - 3):
            load(k["xw"][b, lo:lo + 3].rearrange("y x c -> (y x c)").rearrange("(p n) -> p n", p=6),
                 zero[0:6, 0:PW * C // 2])
    for h in range(2):
        r = slice(64 * h, 64 * h + 64)
        load(k["wom"][r, OM * h:OM * h + OM], d["w_om"])
        load(k["win"][r, r], d["w_in"])
        load(k["wout"][r, r], d["w_out"])
        load(k["crT"][r, r], d["crT"])
        load(k["waT"][r, r], d["waT"])
        load(k["w31T"][r, :], d["w31T"])
        load(k["offw"][r, :, 36 * h:36 * h + 36], d["offw"])
        load(k["l2w"][r, r], d["l2w"])

    with nc.Block() as block:
        @block.sync
        def _(sp):
            for h in range(2):
                for b2 in range(2):
                    sp.dma_start(t_x[64 * h:64 * h + 64, PIX * b2:PIX * b2 + PIX],
                                 d["x"][2 * h + b2].rearrange("c y x -> c (y x)")).then_inc(x_loaded, 16)
            sp.dma_start(k["pairm"][:, :], d["pairm"]).then_inc(x_loaded, 16)
            sp.wait_ge(x_loaded, 16 * 5)

        @block.gpsimd
        def _(pool):
            for name in ("wom", "win", "wout", "crT", "waT", "offw", "l2w", "xp"):
                ins = pool.memset(k[name + "_flat"], 0.0)
            pool.memset(k["arena"][:, 0:3 * PW * C // 4], 0.0)
            pool.memset(k["eps"][:, :], 1e-5)
            pool.memset(k["ones"][:, :], 1.0).then_inc(cleared, 1)
            pool.wait_ge(cleared, 1)
    return loads


def vector_setup(nc, k):
    ctx = k["ctx"]
    steps = signal(k, "setup_steps")
    rooted = signal(k, "bn_rooted")
    with nc.Block() as block:
        @block.scalar
        def _(act):
            act.activation(k["bn"][:, 0:1], k["vec"][:, VC["bn_var"]:VC["bn_var"] + 1], ACT.Sqrt,
                           bias=k["eps"][:, 0:1]).then_inc(rooted, 1)

        @block.vector
        def _(v):
            step = Chain(v, steps)
            v.tensor_copy(k["identb"][:, :], k["ident"][:, :])
            for t in range(TAPS):
                v.tensor_scalar(k["dwdiag"][:, t, :], k["ident"][:, :], k["dw"][:, t:t + 1], None, ALU.mult)
            bn, vec = k["bn"], k["vec"]

            def col(n):
                return vec[:, VC[n]:VC[n] + 1]
            v.wait_ge(rooted, 1)
            step(v.reciprocal(bn[:, 1:2], bn[:, 0:1]))
            step(v.tensor_tensor(bn[:, 2:3], bn[:, 1:2], col("bn_g"), ALU.mult))
            step(v.tensor_tensor(bn[:, 3:4], col("b_out"), col("bn_mean"), ALU.subtract))
            step(v.tensor_tensor(bn[:, 4:5], bn[:, 3:4], bn[:, 2:3], ALU.mult))
            step(v.tensor_tensor(bn[:, 5:6], bn[:, 4:5], col("bn_b"), ALU.add))


def group_norm(nc, k, tag, padded, loads=()):
    ctx = k["ctx"]
    x, xn, xp, st = k["x"], k["xn"], k["xp"], k["stats"]
    ps = k["psum"]
    sums = signal(k, tag + "_sums")
    mean_ps = signal(k, tag + "_mean_ps")
    means = signal(k, tag + "_means")
    squares = signal(k, tag + "_squares")
    var_ps = signal(k, tag + "_var_ps")
    rooted = signal(k, tag + "_rooted")
    normed = signal(k, tag + "_normed")
    steps = signal(k, tag + "_steps")
    loaded = signal(k, tag + "_loaded")
    x3 = x[:, :].rearrange("p (b n) -> p b n", b=2)
    with nc.Block() as block:
        @block.vector
        def _(v):
            step = Chain(v, steps)
            v.tensor_reduce(st[:, 0:2], x3, AX.X, ALU.add).then_inc(sums, 1)
            v.wait_ge(mean_ps, 1)
            step(v.tensor_copy(st[:, 2:4], ps[:, 0:2]))
            v.tensor_scalar(st[:, 4:6], st[:, 2:4], -1.0, None, ALU.mult).then_inc(means, 1)
            v.wait_ge(rooted, 1)
            step(v.reciprocal(st[:, 10:12], st[:, 8:10]))
            for b in range(2):
                v.tensor_scalar(xn[:, PIX * b:PIX * b + PIX], x[:, PIX * b:PIX * b + PIX], st[:, 2 + b:3 + b],
                                st[:, 10 + b:11 + b], ALU.subtract, ALU.mult).then_inc(normed, 1)

        @block.tensor
        def _(pe):
            pe.wait_ge(sums, 1)
            pe.matmul(ps[:, 0:2], k["pairm"][:, :], st[:, 0:2], start=True, stop=True).then_inc(mean_ps, 1)
            pe.wait_ge(squares, 2)
            pe.matmul(ps[:, 512:514], k["pairm"][:, :], st[:, 6:8], start=True, stop=True).then_inc(var_ps, 1)

        @block.scalar
        def _(act):
            act.wait_ge(means, 1)
            for b in range(2):
                act.activation(xn[:, PIX * b:PIX * b + PIX], x[:, PIX * b:PIX * b + PIX], ACT.Square,
                               bias=st[:, 4 + b:5 + b], accum_out=st[:, 6 + b:7 + b]).then_inc(squares, 1)
            act.wait_ge(var_ps, 1)
            act.activation(st[:, 8:10], ps[:, 512:514], ACT.Sqrt, bias=k["eps"][:, 0:1]).then_inc(rooted, 1)
            if padded:
                for b in range(2):
                    act.wait_ge(normed, b + 1)
                    act.activation(xp[:, b, 1:HH + 1, 1:WW + 1],
                                   xn[:, PIX * b:PIX * b + PIX].rearrange("p (y x) -> p y x", y=HH), ACT.Copy)

        if loads:
            @block.sync
            def _(sp):
                for dst, src in loads:
                    sp.dma_start(dst, src).then_inc(loaded, 16)
                sp.wait_ge(loaded, 16 * len(loads))


def chunk_window(xp, b2, r, tap):
    dy, dx = divmod(tap, 3)
    return xp[:, b2, bass.ds(r * ROWS + dy, ROWS), dx:dx + WW]


def offsets0(nc, k, om):
    ctx, ps, xp, xn = k["ctx"], k["psum"], k["xp"], k["xn"]
    big = k["work0"]
    conv, cent, sq, root, inv, z, gel, xs = (big[:, CH * i:CH * i + CH] for i in range(8))
    xq = k["xproj"]
    S = {n: signal(k, "off0_" + n) for n in
         ("conv_ps", "conv", "mean_ps", "cent", "sq", "var_ps", "root", "z", "gelu", "om_ps", "om",
          "proj_ps", "proj", "steps", "cleared")}
    p_conv, p_mean, p_var = ps[:, 0:CH], ps[:, 512:512 + CH], ps[:, 1024:1024 + CH]
    p_om = ps[:, 1536:1536 + TPC * 256].rearrange("p (t n) -> p t n", t=TPC)
    p_proj = ps[:, 2560:2560 + CH]
    vec = k["vec"]

    def turns(eng):
        for b2 in range(2):
            with eng.Fori(0, CPI) as r:
                yield b2, r, b2 * CPI + r + 1

    with nc.Block() as block:
        @block.tensor
        def _(pe):
            def taps(b2, r, which):
                for t in which:
                    mm = pe.matmul(p_conv.rearrange("p (y x) -> p y x", y=ROWS), k["dwdiag"][:, t, :],
                                   chunk_window(xp, b2, r, t), start=(t == 0), stop=(t == TAPS - 1))
                if t == TAPS - 1:
                    mm.then_inc(S["conv_ps"], 1)

            def chunk(b2, r, after):
                n = b2 * CPI + r + 1
                pe.wait_ge(S["conv"], n)
                pe.matmul(p_mean, k["halfm"][:, :], conv, start=True, stop=True).then_inc(S["mean_ps"], 1)
                if after:
                    taps(*after, range(3))
                pe.wait_ge(S["sq"], n)
                pe.matmul(p_var, k["halfm"][:, :], sq, start=True, stop=True).then_inc(S["var_ps"], 1)
                if after:
                    taps(*after, range(3, TAPS))
                pe.wait_ge(S["proj"], n)
                pe.matmul(p_proj, k["win"][:, :], xn[:, bass.ds(r * CH + b2 * PIX, CH)], start=True, stop=True)\
                    .then_inc(S["proj_ps"], 1)
                pe.wait_ge(S["gelu"], n)
                pe.wait_ge(S["om"], n)
                for t in range(TPC):
                    mm = pe.matmul(p_om[:, t, 0:2 * OM], gel[:, PT * t:PT * t + PT], k["wom"][:, :],
                                   start=True, stop=True)
                mm.then_inc(S["om_ps"], 1)

            pe.sem_inc(S["om"], 1)
            pe.sem_inc(S["proj"], 1)
            taps(0, 0, range(TAPS))
            for b2 in range(2):
                with pe.Fori(0, CPI - 1) as r:
                    chunk(b2, r, (b2, r + 1))
                chunk(b2, CPI - 1, None if b2 else (1, 0))

        @block.scalar
        def _(act):
            for b2, r, n in turns(act):
                act.wait_ge(S["conv_ps"], n)
                act.activation(conv, p_conv, ACT.Identity, bias=vec[:, VC["dw_b"]:VC["dw_b"] + 1])\
                    .then_inc(S["conv"], 1)
                act.wait_ge(S["cent"], n)
                act.activation(sq, cent, ACT.Square).then_inc(S["sq"], 1)
                act.wait_ge(S["var_ps"], n)
                act.activation(root, p_var, ACT.Sqrt, bias=k["eps"][:, 0:1]).then_inc(S["root"], 1)
                act.wait_ge(S["z"], n)
                act.activation(gel, z, ACT.Gelu, scale=vec[:, VC["ln_g"]:VC["ln_g"] + 1],
                               bias=vec[:, VC["ln_b"]:VC["ln_b"] + 1]).then_inc(S["gelu"], 1)
                if b2 == 0:
                    act.wait_ge(S["cleared"], 1)
                act.wait_ge(S["proj_ps"], n)
                act.activation(xq[:, b2, bass.ds(r * ROWS + 2, ROWS), 2:2 + WW],
                               p_proj.rearrange("p (y x) -> p y x", y=ROWS), ACT.Identity,
                               bias=vec[:, VC["b_in"]:VC["b_in"] + 1]).then_inc(S["proj"], 1)

        @block.vector
        def _(v):
            step = Chain(v, S["steps"])
            for b2 in range(2):
                with v.Fori(0, CPI) as r, step.body(r, 1, CPI):
                    n = b2 * CPI + r + 1
                    v.wait_ge(S["mean_ps"], n)
                    v.tensor_tensor(cent, conv, p_mean, ALU.subtract).then_inc(S["cent"], 1)
                    v.wait_ge(S["root"], n)
                    step(v.reciprocal(inv, root))
                    v.tensor_tensor(z, cent, inv, ALU.mult).then_inc(S["z"], 1)
                    v.wait_ge(S["om_ps"], n)
                    v.tensor_tensor(om[:, bass.ds((r + b2 * CPI) * (2 * TPC), 2 * TPC), :]
                                    .rearrange("p (t h) n -> p t h n", h=2),
                                    p_om[:, :, 0:2 * OM].rearrange("p t (h n) -> p t h n", h=2),
                                    k["b_om"][:, :].unsqueeze(1).unsqueeze(1).to_broadcast([128, TPC, 2, OM]),
                                    ALU.add).then_inc(S["om"], 1)

        @block.gpsimd
        def _(pool):
            pool.memset(xq.rearrange("p b y x -> p (b y x)"), 0.0).then_inc(S["cleared"], 1)


def window_counts(nc, k, om):
    ctx, ps, st = k["ctx"], k["psum"], k["small"]
    S = {n: signal(k, "wide_" + n) for n in ("top", "turned", "steps", "flag")}
    with nc.Block() as block:
        @block.vector
        def _(v):
            step = Chain(v, S["steps"])
            v.tensor_reduce(st[:, 0:1], om[:, :, 0:2 * MG], AX.XY, ALU.max, apply_absolute_value=True)\
                .then_inc(S["top"], 1)
            v.wait_ge(S["turned"], 1)
            step(v.tensor_reduce(st[0:1, 1:2], ps[0:1, 0:128], AX.X, ALU.max))
            v.tensor_scalar(k["flag"][:, :], st[0:1, 1:2], 1.0, None, ALU.is_gt).then_inc(S["flag"], 1)

        @block.tensor
        def _(pe):
            pe.wait_ge(S["top"], 1)
            pe.transpose(ps[0:1, 0:128], st[:, 0:1], k["ident"][:, :]).then_inc(S["turned"], 1)


W = 5


def window_weights(nc, k, om, hp, hn, A, parts, rest, tmp):
    ctx = k["ctx"]
    S = {n: signal(k, "ww_" + n) for n in
         ("shifted", "exped", "steps", "hats", "ready", "prod", "used", "a", "part", "cleared")}
    M = 2 * NT
    TG = M * G
    logits = om[:, :, 2 * MG:OM].rearrange("p t (g s) -> p t g s", g=G)
    off = om[:, :, 0:2 * MG]
    hp3, hn3 = hp.rearrange("p (t n) -> p t n", t=M), hn.rearrange("p (t n) -> p t n", t=M)
    top = tmp[0][:, 0:TG].rearrange("p (t g) -> p t g", g=G)
    topb = top.unsqueeze(3).to_broadcast([128, M, G, TAPS])
    hats = [hn3, off, hp3]
    mask = om[:, :, 2 * MG:OM]
    A4 = A.rearrange("p (n u v) -> p n u v", u=W, v=W)
    pr = [t[:, 0:TG * TAPS].rearrange("p (n x y) -> p n x y", x=3, y=3) for t in tmp]

    def axis(h, a):
        return h.rearrange("p t (s a) -> p t s a", a=2)[:, :, :, a]

    def by_row(a, u):
        return a.rearrange("p (j n u v) -> p j n u v", n=2 * G, u=W, v=W)[:, :, :, u, :]

    POOLED = (1, 4, 7)
    with nc.Block() as block:
        @block.scalar
        def _(act):
            act.activation(hp3, off, ACT.Relu).then_inc(S["hats"], 1)
            act.activation(hn3, off, ACT.Relu, scale=-1.0).then_inc(S["hats"], 1)
            act.wait_ge(S["shifted"], 1)
            act.activation(mask, mask, ACT.Exp).then_inc(S["exped"], 1)
            for q in range(3):
                for u in range(W):
                    act.wait_ge(S["a"], 1 + (W * (q - 1) + u + 1 if q else 0))
                    act.activation(parts[:, :, u, q, :, :], by_row((A, rest, A)[q], u), ACT.Copy)\
                        .then_inc(S["part"], 1)

        @block.gpsimd
        def _(pool):
            pool.memset(A, 0.0).then_inc(S["cleared"], 1)
            pool.wait_ge(S["ready"], 1)
            for n, q in enumerate(POOLED):
                dy, dx = divmod(q, 3)
                if n:
                    pool.wait_ge(S["used"], n)
                pool.tensor_tensor(tmp[1][:, 0:TG * TAPS].rearrange("p (t s) -> p t s", s=MG),
                                   axis(hats[dy], 1), axis(hats[dx], 0), ALU.mult).then_inc(S["prod"], 1)

        @block.vector
        def _(v):
            step = Chain(v, S["steps"])
            step(v.tensor_reduce(top, logits, AX.X, ALU.max))
            v.tensor_tensor(logits, logits, topb, ALU.subtract).then_inc(S["shifted"], 1)
            v.wait_ge(S["hats"], 2)
            step(v.scalar_tensor_tensor(off, hp3, 1.0, hn3, ALU.subtract, ALU.add))
            step(v.tensor_scalar(off, off, -1.0, None, ALU.mult))
            v.wait_ge(S["exped"], 1)
            step(v.tensor_reduce(top, logits, AX.X, ALU.add))
            step(v.reciprocal(top, top))
            step(v.tensor_tensor(logits, logits, topb, ALU.mult))
            for n, h in enumerate(hats):
                ins = v.tensor_tensor(axis(h, 1), axis(h, 1), mask, ALU.mult)
            ins.then_inc(S["ready"], 1)
            v.wait_ge(S["ready"], 1)
            v.wait_ge(S["cleared"], 1)
            own = [q for q in range(9) if q not in POOLED]
            for n in range(9):
                q = own[n - (n + 1) // 3] if n % 3 != 2 else POOLED[n // 3]
                dy, dx = divmod(q, 3)
                if n % 3 == 2:
                    v.wait_ge(S["prod"], n // 3 + 1)
                    src = pr[1]
                else:
                    step(v.tensor_tensor(tmp[0][:, 0:TG * TAPS].rearrange("p (t s) -> p t s", s=MG),
                                         axis(hats[dy], 1), axis(hats[dx], 0), ALU.mult))
                    src = pr[0]
                dst = A4[:, :, dy:dy + 3, dx:dx + 3]
                add = v.tensor_tensor(dst, dst, src.rearrange("p n x y -> p n y x"), ALU.add)
                if n == 8:
                    add.then_inc(S["a"], 1)
                elif n % 3 == 2:
                    add.then_inc(S["used"], 1)
                    v.wait_ge(S["used"], n // 3 + 1)
                else:
                    step(add)
            for q in range(2):
                dst, src = ((rest, A), (A, rest))[q]
                for u in range(W):
                    v.wait_ge(S["part"], W * q + u + 1)
                    v.tensor_tensor(by_row(dst, u), by_row(src, u), parts[:, :, u, q, :, :], ALU.subtract)\
                        .then_inc(S["a"], 1)


def window_taps(nc, k, parts, att, pr, tail):
    ps, xq, x = k["psum"], k["xproj"], k["x"]
    BF = mybir.dt.bfloat16
    S = {n: signal(k, "wt_" + n) for n in
         ("turned", "at", "spread", "prod", "sum1", "sum2", "acc", "gated", "gate", "added")}
    sel = k["sel"]
    R = 3 * 8 * W
    WW2 = W * W
    p_t = [ps[0:R, 3072 + 512 * i:3072 + 512 * i + CH // 2].bitcast(BF) for i in range(2)]
    p_b = [ps[:, 512 * v:512 * v + CH] for v in range(W)]
    p_y = ps[:, 2560:2560 + CH]
    prod = [[pr[:, (W * u + v) * CH:(W * u + v + 1) * CH] for v in range(W)] for u in range(W)]
    yb = [tail[:, CH * i:CH * i + CH] for i in range(2)]

    def walk(eng, chunk):
        chunk(0, 0, 0, True, False)
        with eng.Fori(0, CPI - 1) as i:
            chunk(0, i + 1, i + 1, False, False)
        with eng.Fori(0, CPI - 1) as i:
            chunk(1, i, i + CPI, False, False)
        chunk(1, CPI - 1, 2 * CPI - 1, False, True)

    flat = parts.rearrange("p j u q n v -> p (j u q n v)")
    with nc.Block() as block:
        @block.gpsimd
        def _(pool):
            def chunk(b2, r, n, first, last):
                for u in range(W):
                    pool.wait_ge(S["prod"], n * WW2 + (W * u + 4 + W))
                    a = pr[:, W * u * CH:(W * u + 2) * CH]
                    pool.tensor_tensor(a, a, pr[:, (W * u + 2) * CH:(W * u + 4) * CH], ALU.add).then_inc(S["sum1"], 1)
                    pool.wait_ge(S["sum1"], n * W + (u + 1))
                    pool.tensor_tensor(prod[u][0], prod[u][0], prod[u][1], ALU.add).then_inc(S["sum2"], 1)

            walk(pool, chunk)

        @block.scalar
        def _(act):
            def keep(n, u):
                act.wait_ge(S["turned"], n * W + (u + 1))
                act.activation(att[0:R, CH * u:CH * u + CH], p_t[u % 2], ACT.Copy).then_inc(S["at"], 1)

            def gate(n):
                act.wait_ge(S["acc"], n * W + 2 * W)
                act.wait_ge(S["added"], n + 1)
                act.activation(yb[0], p_y, ACT.Identity, scale=k["bn"][:, 2:3], bias=k["bn"][:, 5:6])
                act.activation(yb[1], p_y, ACT.Sigmoid, scale=k["bn"][:, 2:3], bias=k["bn"][:, 5:6])\
                    .then_inc(S["gated"], 1)

            def chunk(b2, r, n, first, last):
                for u in range(W):
                    if not last:
                        act.wait_ge(S["spread"], n * WW2 + (W * u + W))
                        keep(n + 1, u)
                    if u == 1 and not first:
                        gate(n - 1)

            for u in range(W):
                keep(0, u)
            walk(act, chunk)
            gate(2 * CPI - 1)

        @block.tensor
        def _(pe):
            def turn(n, u):
                pe.wait_ge(S["at"], n * W + (u if u else 1))
                for t in range(TPC):
                    mm = pe.transpose(p_t[u % 2][:, PT * t:PT * t + PT],
                                      flat[:, bass.ds(n * (TPC * W * R) + (t * W * R + u * R), R)], k["identb"][:, :])
                mm.then_inc(S["turned"], 1)

            def gather_sums(n, u):
                pe.wait_ge(S["sum2"], n * W + (u + 1))
                if u == 0:
                    pe.wait_ge(S["gated"], n + 1)
                pe.matmul(p_y, k["wout"][:, :], prod[u][0], start=(u == 0), stop=False)
                pe.wait_ge(S["prod"], n * WW2 + (W * u + 5 + W))
                pe.matmul(p_y, k["wout"][:, :], prod[u][4], start=False, stop=(u == W - 1)).then_inc(S["acc"], 1)

            def chunk(b2, r, n, first, last):
                for u in range(W):
                    pe.wait_ge(S["at"], n * W + (u + 2))
                    for v in range(W):
                        pe.wait_ge(S["prod"], n * WW2 + (W * u + v + 1))
                        pe.matmul(p_b[v], sel[0:R, v, :], att[0:R, CH * u:CH * u + CH], start=True, stop=True)\
                            .then_inc(S["spread"], 1)
                    if not last:
                        turn(n + 1, u)
                    if u >= 2:
                        gather_sums(n, u - 2)
                    elif not first:
                        gather_sums(n - 1, u + 3)

            pe.sem_inc(S["added"], 1)
            pe.sem_inc(S["prod"], W)
            pe.sem_inc(S["at"], 1)
            pe.sem_inc(S["gated"], 1)
            for u in range(W):
                turn(0, u)
            walk(pe, chunk)
            gather_sums(2 * CPI - 1, 3)
            gather_sums(2 * CPI - 1, 4)

        @block.vector
        def _(v_):
            def finish(n):
                v_.wait_ge(S["gated"], n + 2)
                v_.tensor_tensor(yb[0], yb[0], yb[1], ALU.mult).then_inc(S["gate"], 1)
                v_.wait_ge(S["gate"], n + 1)
                xs = x[:, bass.ds(n * CH, CH)]
                v_.tensor_tensor(xs, xs, yb[0], ALU.add).then_inc(S["added"], 1)

            def chunk(b2, r, n, first, last):
                for u in range(W):
                    v_.wait_ge(S["acc"], n * W + (u + 1))
                    for v in range(W):
                        v_.wait_ge(S["spread"], n * WW2 + (W * u + v + 1))
                        v_.tensor_tensor(prod[u][v].rearrange("p (y x) -> p y x", y=ROWS),
                                         p_b[v].rearrange("p (y x) -> p y x", y=ROWS),
                                         xq[:, b2, bass.ds(r * ROWS + u, ROWS), v:v + WW], ALU.mult)\
                            .then_inc(S["prod"], 1)
                    if u == 2 and not first:
                        finish(n - 1)

            v_.sem_inc(S["acc"], W)
            walk(v_, chunk)
            finish(2 * CPI - 1)


def pixels_out(nc, k, tag, window, buf, loads=()):
    ps = k["psum"]
    TP, NTP = 2 * PW, ROWS // 2
    xs = [buf[:, ROWS * PW * i:ROWS * PW * i + ROWS * PW] for i in range(2)]
    at = 2 * ROWS * PW
    pp = [buf[0:TP, at + NTP * 128 * i:at + NTP * 128 * (i + 1)] for i in range(2)]
    p_x = [ps[0:TP, 512 * i:512 * i + NTP * 128] for i in range(2)]
    S = {n: signal(k, tag + "_" + n) for n in ("xs", "turned", "pp", "stored0", "stored1", "loaded", "xs0")}

    def turns(eng):
        for b2 in range(2):
            with eng.Fori(0, CPI // 2) as i:
                for par in range(2):
                    yield b2, i * 2 + par, i * 2 + (par + b2 * CPI + 1), par

    with nc.Block() as block:
        @block.vector
        def _(v):
            for par in range(2):
                v.memset(xs[par], 0.0).then_inc(S["xs0"], 1)
            v.wait_ge(S["xs0"], 2)
            v.sem_inc(S["turned"], 2)
            for b2, r, n, par in turns(v):
                v.wait_ge(S["turned"], n)
                src = window(b2, r).rearrange("p y (t q) -> p y q t", q=IW)
                x4 = xs[par].rearrange("p (y j t) -> p y j t", y=ROWS, j=IW)
                for j, t in ((0, 1), (3, 0)):
                    cp = v.tensor_copy(x4[:, :, j:j + 3, t:t + WW // IW], src[:, :, 3 - j:6 - j, :])
                cp.then_inc(S["xs"], 1)

        @block.tensor
        def _(pe):
            pe.sem_inc(S["pp"], 2)
            for b2, r, n, par in turns(pe):
                pe.wait_ge(S["xs"], n)
                pe.wait_ge(S["pp"], n)
                for t in range(NTP):
                    mm = pe.transpose(p_x[par][:, 128 * t:128 * t + 128], xs[par][:, TP * t:TP * t + TP],
                                      k["ident"][:, :])
                mm.then_inc(S["turned"], 1)

        @block.scalar
        def _(act):
            for b2, r, n, par in turns(act):
                act.wait_ge(S["turned"], n + 2)
                act.wait_ge(S[f"stored{par}"], (n + (1 - par)) * 16)
                act.activation(pp[par], p_x[par], ACT.Copy).then_inc(S["pp"], 1)

        @block.sync
        def _(sp):
            for dst, src in loads:
                sp.dma_start(dst, src).then_inc(S["loaded"], 16)
            for par in range(2):
                sp.sem_inc(S[f"stored{par}"], 32)
            rows = k["xw"][:, 3:3 + HH, :, :].rearrange("b (y u) x c -> b (u x) y c", u=2)
            for b2, r, n, par in turns(sp):
                sp.wait_ge(S["pp"], n + 2)
                p4 = pp[par].rearrange("p (t h c) -> p t h c", h=2, c=C)
                for h in range(2):
                    sp.dma_start(rows[2 * h + b2, :, bass.ds(r * (ROWS // 2), ROWS // 2), :], p4[:, :, h, :])\
                        .then_inc(S[f"stored{par}"], 16)
            for par in range(2):
                sp.wait_ge(S[f"stored{par}"], 32 * (CPI + 1))
            if loads:
                sp.wait_ge(S["loaded"], 16 * len(loads))


def quads(nc, k, tag, groups):
    ctx = k["ctx"]
    A = k["arena"]
    n = C // groups
    rows = [A[0:2 * TR, 3200 * i:3200 * i + 3200].rearrange("p (x c) -> p x c", c=C) for i in range(2)]
    T = A[0:2 * TR, 6400:6400 + TR * 4 * C]
    T6 = T.rearrange("p (x g q n) -> p x g q n", g=groups, q=4, n=n)
    cleared = signal(k, tag + "_cleared")
    loaded = signal(k, tag + "_loaded")
    spread = signal(k, tag + "_spread")
    stored = signal(k, tag + "_stored")
    img = k["xw"][:, 3:3 + HH, :, :].rearrange("b y (j t) c -> b y j t c", j=IW)
    NL = 4 * IW * 16
    tab = k["tab"]

    def copy(eng, run, q):
        dy, dx = divmod(q, 2)
        return run(T6[:, :, :, q, :], rows[dy][:, dx:dx + TR, :].rearrange("p x (g n) -> p x g n", g=groups))

    with nc.Block() as block:
        @block.gpsimd
        def _(pool):
            pool.memset(A[0:2 * TR, 0:6400], 0.0).then_inc(cleared, 1)
            for bb in range(2):
                pool.wait_ge(loaded, NL * (bb + 1))
                if bb:
                    pool.wait_ge(stored, 16 * bb)
                copy(pool, pool.tensor_copy, 0).then_inc(spread, 1)

        @block.scalar
        def _(act):
            for bb in range(2):
                act.wait_ge(loaded, NL * (bb + 1))
                if bb:
                    act.wait_ge(stored, 16 * bb)
                copy(act, lambda o, i: act.activation(o, i, ACT.Copy), 1).then_inc(spread, 1)

        @block.vector
        def _(v):
            for bb in range(2):
                v.wait_ge(loaded, NL * (bb + 1))
                if bb:
                    v.wait_ge(stored, 16 * bb)
                for q in (2, 3):
                    copy(v, v.tensor_copy, q).then_inc(spread, 1)

        @block.sync
        def _(sp):
            sp.wait_ge(cleared, 1)
            for bb in range(2):
                if bb:
                    sp.wait_ge(spread, 4 * bb)
                for dy in range(2):
                    for u in range(2):
                        dst = rows[dy][TR * u + 1 - dy:TR * u + 1 - dy + HH, 1:WW + 1, :]\
                            .rearrange("p (t q) c -> p q t c", q=IW)
                        for j in range(IW):
                            t = 1 if j < 3 else 0
                            sp.dma_start(dst[:, (j + 3) % IW, :, :], img[2 * bb + u, :, j, t:t + WW // IW, :])\
                                .then_inc(loaded, 16)
                sp.wait_ge(spread, 4 * (bb + 1))
                sp.dma_start(tab[2 * TR * bb:2 * TR * bb + 2 * TR, :], T).then_inc(stored, 16)
            sp.wait_ge(stored, 32)


def places(nc, k, tag, om, base, goff, idx, frac, ns, xfirst, tmp, mask):
    ctx = k["ctx"]
    steps = signal(k, tag + "_steps")
    shifted = signal(k, tag + "_shifted")
    exped = signal(k, tag + "_exped")
    M = 2 * NT
    cf = frac[:, :, :]
    r1, r2 = tmp
    with nc.Block() as block:
        @block.vector
        def _(v):
            step = Chain(v, steps)
            if mask is not None:
                logits = om[:, :, 2 * MG:OM].rearrange("p t (g k) -> p t g k", g=G)
                m4 = mask[:, 0:M, :].rearrange("p t (g k) -> p t g k", g=G)
                top = r1[:, 0:M * G].rearrange("p (t g) -> p t g", g=G)
                topb = top.unsqueeze(3).to_broadcast([128, M, G, TAPS])
                step(v.tensor_reduce(top, logits, AX.X, ALU.max))
                v.tensor_tensor(m4, logits, topb, ALU.subtract).then_inc(shifted, 1)
                v.wait_ge(exped, 1)
                step(v.tensor_reduce(top, m4, AX.X, ALU.add))
                step(v.reciprocal(top, top))
                step(v.tensor_tensor(m4, m4, topb, ALU.mult))
            for b2 in range(2):
                for h in range(2):
                    o = om[:, :, 0:2 * ns].rearrange("p (b t h) n -> p b t h n", b=2, h=2)[:, b2, :, h, :]
                    f = cf.rearrange("p (b t h) n -> p b t h n", b=2, h=2)[:, b2, :, h, :]
                    last = v.tensor_tensor(f, o, base, ALU.add)
            step(last)
            flat = cf.rearrange("p t n -> p (t n)")
            a, b = r1[:, 0:M * 2 * ns], r2[:, 0:M * 2 * ns]
            step(v.tensor_scalar(flat, flat, float(PH - 1), 0.0, ALU.min, ALU.max))
            step(v.tensor_scalar(a, flat, ROUND, ROUND, ALU.add, ALU.subtract))
            step(v.tensor_tensor(b, a, flat, ALU.is_gt))
            step(v.tensor_tensor(a, a, b, ALU.subtract))
            step(v.tensor_scalar(a, a, float(PH - 2), None, ALU.min))
            step(v.tensor_tensor(flat, flat, a, ALU.subtract))
            ax = a.rearrange("p (t n a) -> p t n a", n=ns, a=2)
            y0, x0 = (ax[:, :, :, 1], ax[:, :, :, 0]) if xfirst else (ax[:, :, :, 0], ax[:, :, :, 1])
            lin = b[:, 0:M * ns].rearrange("p (t n) -> p t n", n=ns)
            step(v.scalar_tensor_tensor(lin, y0, float(TR), x0, ALU.mult, ALU.add))
            for b2 in range(2):
                for h in range(2):
                    src = lin.rearrange("p (b t h) n -> p b t h n", b=2, h=2)[:, b2, :, h, :]
                    dst = idx[:, 0:M, :].rearrange("p (b t h) n -> p b t h n", b=2, h=2)[:, b2, :, h, :]
                    gb = goff[:, 2 * h + b2, :].unsqueeze(1).to_broadcast([128, TPI, ns])
                    v.scalar_tensor_tensor(dst, src, float(G if mask is not None else 1), gb, ALU.mult, ALU.add)
            v.memset(idx[:, M:M + 2, :], 0)

        if mask is not None:
            @block.scalar
            def _(act):
                act.wait_ge(shifted, 1)
                fl = mask[:, 0:M, :].rearrange("p t n -> p (t n)")
                act.activation(fl, fl, ACT.Exp).then_inc(exped, 1)


def sample(nc, k, tag, idx, frac, mask, ns, xfirst, row, first):
    ctx, ps = k["ctx"], k["psum"]
    A = k["arena"]
    gat = [A[:, ns * row * i:ns * row * (i + 1)].rearrange("p (s n) -> p s n", s=ns) for i in range(2)]
    at = 2 * ns * row
    w4 = A[:, at:at + 2 * ns * 4].rearrange("p (h s q) -> p h s q", h=2, q=4)
    at += 8 * ns
    S = {n: signal(k, f"{tag}_{n}") for n in
         ("idx0", "idx1", "got0", "got1", "turn", "summed0", "summed1", "turned", "turned_sb",
          "taken", "prod", "act", "add", "steps", "steps_act")}
    stage = k["istage"]
    table = k["tab"].rearrange("r (i n) -> (r i) n", n=row)
    sumw = 128 if first else ns * C
    n_sum = 1 if first else 2
    acc = A[:, at:at + n_sum * sumw].rearrange("p (u n) -> p u n", u=n_sum)
    at += n_sum * sumw
    turned = A[:, at:at + (128 if first else TAPS * 128)]
    at += 128 if first else TAPS * 128
    yb = A[:, at:at + 256]

    def tile(i, h):
        return bass.ds(i * 2 + h, 1)

    with nc.Block() as block:
        @block.gpsimd
        def _(pool):
            with pool.Fori(0, NT) as i:
                for h in range(2):
                    pool.wait_ge(S[f"summed{h}"], i + 1)
                    pool.wait_ge(S[f"idx{h}"], i + 1)
                    pool.sem_inc(S["turn"], 1)
                    for s in range(ns):
                        pool.indirect_dma_start(
                            out=gat[h][:, s, :], out_offset=None, in_=table,
                            in_offset=bass.IndirectOffsetOnAxis(ap=stage[:, h, s:s + 1], axis=0)
                        ).then_inc(S[f"got{h}"], 16)

        @block.vector
        def _(v):
            step = Chain(v, S["steps"])
            for h in range(2):
                v.sem_inc(S[f"summed{h}"], 1)
                v.tensor_copy(stage[:, h, 0:ns], idx[:, h, :]).then_inc(S[f"idx{h}"], 1)
            per = 6 + 2
            with v.Fori(0, NT) as i, step.body(i, per, NT):
                f4 = frac[:, bass.ds(i * 2, 2), :].rearrange("p t (s a) -> p t s a", a=2)
                wy, wx = (f4[:, :, :, 1], f4[:, :, :, 0]) if xfirst else (f4[:, :, :, 0], f4[:, :, :, 1])
                m = mask[:, bass.ds(i * 2, 2), :] if first else k["ones"][:, 0:1].unsqueeze(2).to_broadcast([128, 2, ns])
                w = [w4[:, :, :, q] for q in range(4)]
                step(v.tensor_tensor(w[2], m, wy, ALU.mult))
                step(v.tensor_tensor(w[0], m, w[2], ALU.subtract))
                step(v.tensor_tensor(w[3], w[2], wx, ALU.mult))
                step(v.tensor_tensor(w[1], w[0], wx, ALU.mult))
                step(v.tensor_tensor(w[2], w[2], w[3], ALU.subtract))
                step(v.tensor_tensor(w[0], w[0], w[1], ALU.subtract))
                for h in range(2):
                    v.wait_ge(S[f"got{h}"], (i + 1) * (16 * ns))
                    v.tensor_copy(stage[:, h, 0:ns], idx[:, tile(i + 1, h), :].rearrange("p a s -> p (a s)"))\
                        .then_inc(S[f"idx{h}"], 1)
                    n = row // 4
                    g4 = gat[h].rearrange("p s (q n) -> p (s q) n", n=n)
                    wb = w4[:, h, :, :].rearrange("p s q -> p (s q)").unsqueeze(2).to_broadcast([128, 4 * ns, n])
                    step(v.tensor_tensor(g4, g4, wb, ALU.mult))
                    if first:
                        if h == 0:
                            v.wait_ge(S["taken"], i + 1)
                        v.tensor_reduce(
                            acc[:, 0, 64 * h:64 * h + 64].rearrange("p (g n) -> p g n", g=G),
                            gat[h].rearrange("p (g s) (q n) -> p g n (s q)", g=G, n=n), AX.X, ALU.add)\
                            .then_inc(S[f"summed{h}"], 1)
                    else:
                        v.wait_ge(S["taken"], i * 2 + h + 1)
                        v.tensor_reduce(acc[:, h, :].rearrange("p (s n) -> p s n", n=C),
                                        gat[h].rearrange("p s (q n) -> p s n q", n=n), AX.X, ALU.add)\
                            .then_inc(S[f"summed{h}"], 1)
                if first:
                    v.wait_ge(S["act"], i + 1)
                    xs = k["x"][:, bass.ds(i * PT, PT)]
                    v.tensor_tensor(yb[:, 0:128], yb[:, 0:128], yb[:, 128:256], ALU.mult).then_inc(S["prod"], 1)
                    v.wait_ge(S["prod"], i + 1)
                    v.tensor_tensor(xs, xs, yb[:, 0:128], ALU.add).then_inc(S["add"], 1)

        if first:
            @block.tensor
            def _(pe):
                pe.sem_inc(S["taken"], 1)
                with pe.Fori(0, NT) as i:
                    pe.wait_ge(S["summed0"], i + 2)
                    pe.wait_ge(S["summed1"], i + 2)
                    pe.transpose(ps[:, 0:128], acc[:, 0, :], k["ident"][:, :]).then_inc(S["taken"], 1)
                    pe.wait_ge(S["turned_sb"], i + 1)
                    pe.matmul(ps[:, 512:640], k["wout"][:, :], turned, start=True, stop=True)\
                        .then_inc(S["turned"], 1)

            @block.scalar
            def _(act):
                act.sem_inc(S["add"], 1)
                with act.Fori(0, NT) as i:
                    act.wait_ge(S["taken"], i + 2)
                    act.activation(turned, ps[:, 0:128], ACT.Copy).then_inc(S["turned_sb"], 1)
                    act.wait_ge(S["turned"], i + 1)
                    act.wait_ge(S["add"], i + 1)
                    act.activation(yb[:, 0:128], ps[:, 512:640], ACT.Identity, scale=k["bn"][:, 2:3],
                                   bias=k["bn"][:, 5:6])
                    act.activation(yb[:, 128:256], ps[:, 512:640], ACT.Sigmoid, scale=k["bn"][:, 2:3],
                                   bias=k["bn"][:, 5:6]).then_inc(S["act"], 1)
        else:
            sc = k["sc"]

            @block.tensor
            def _(pe):
                pe.sem_inc(S["taken"], 2)
                with pe.Fori(0, NT) as i:
                    for h in range(2):
                        n = i * 2 + h + 1
                        pe.wait_ge(S[f"summed{h}"], i + 2)
                        for m in range(TAPS):
                            mm = pe.transpose(ps[:, 128 * m:128 * m + 128], acc[:, h, 128 * m:128 * m + 128],
                                              k["ident"][:, :])
                        mm.then_inc(S["taken"], 1)
                        pe.wait_ge(S["turned_sb"], n)
                        for m in range(TAPS):
                            mm = pe.matmul(ps[:, 2048:2176], k["dws2"][:, m, :], turned[:, 128 * m:128 * m + 128],
                                           start=(m == 0), stop=(m == TAPS - 1))
                        mm.then_inc(S["prod"], 1)

            @block.scalar
            def _(act):
                with act.Fori(0, NT) as i:
                    for h in range(2):
                        n = i * 2 + h + 1
                        act.wait_ge(S["taken"], n + 2)
                        act.activation(turned, ps[:, 0:TAPS * 128], ACT.Copy).then_inc(S["turned_sb"], 1)
                        act.wait_ge(S["prod"], n)
                        act.activation(sc[:, h, bass.ds(i * PT, PT)], ps[:, 2048:2176], ACT.Identity,
                                       bias=k["dbs"][:, 0:1])


NO1 = 2 * S1
R3 = 3 * NO1
K3 = R3 + 1


def offsets1(nc, k, raw, o3, w):
    ps, xp = k["psum"], k["xp"]
    y = [w[0:R3, CH * h:CH * h + CH] for h in range(2)]
    hi = [w[0:R3, CH * 2 + CH // 2 * h:CH * 2 + CH // 2 * (h + 1)].bitcast(mybir.dt.bfloat16) for h in range(2)]
    S = {n: signal(k, "off1_" + n) for n in ("conv_ps", "raw", "rep_ps", "y", "hi", "dropped", "o3", "ones")}
    p_c = ps[0:2 * NO1, 0:CH]
    p_y = [ps[0:R3, 512 * (1 + h):512 * (1 + h) + CH] for h in range(2)]

    def turns(eng):
        for b2 in range(2):
            with eng.Fori(0, CPI) as r:
                yield b2, r, b2 * CPI + r + 1

    with nc.Block() as block:
        @block.gpsimd
        def _(pool):
            pool.memset(o3, 1.0).then_inc(S["ones"], 1)

        @block.tensor
        def _(pe):
            pe.sem_inc(S["raw"], 1)
            pe.sem_inc(S["y"], 2)
            for b2, r, n in turns(pe):
                pe.wait_ge(S["raw"], n)
                for t in range(TAPS):
                    mm = pe.matmul(p_c.rearrange("p (y x) -> p y x", y=ROWS), k["offw"][:, t, :],
                                   chunk_window(xp, b2, r, t), start=(t == 0), stop=(t == TAPS - 1))
                mm.then_inc(S["conv_ps"], 1)
                pe.wait_ge(S["raw"], n + 1)
                pe.wait_ge(S["y"], n * 2)
                for h in range(2):
                    mm = pe.matmul(p_y[h], k["rep1"][:, h, :], raw[:, bass.ds(r * CH + b2 * PIX, CH)],
                                   start=True, stop=True)
                mm.then_inc(S["rep_ps"], 1)

        @block.scalar
        def _(act):
            act.wait_ge(S["ones"], 1)
            for b2, r, n in turns(act):
                for q in range(2):
                    for h in range(2):
                        if q == 0:
                            act.wait_ge(S["y"], (n - 1) * 2 + (h + 3))
                        else:
                            act.wait_ge(S["dropped"], (n - 1) * 4 + (h + 1))
                        act.activation(hi[h], y[h], ACT.Copy).then_inc(S["hi"], 1)
                for h in range(2):
                    act.wait_ge(S["dropped"], (n - 1) * 4 + (h + 3))
                    act.activation(o3[0:R3, bass.ds(r * CH + (2 * h + b2) * PIX, CH)], y[h], ACT.Copy)\
                        .then_inc(S["o3"], 1)

        @block.vector
        def _(v):
            v.sem_inc(S["o3"], 2)
            for b2, r, n in turns(v):
                v.wait_ge(S["conv_ps"], n)
                v.tensor_scalar(raw[:, bass.ds(r * CH + b2 * PIX, CH)], p_c, k["offb"][:, 0:1], None, ALU.add)\
                    .then_inc(S["raw"], 1)
                v.wait_ge(S["rep_ps"], n)
                for h in range(2):
                    v.wait_ge(S["o3"], (n - 1) * 2 + (h + 1))
                    v.tensor_tensor(y[h], p_y[h], k["rel1"][0:R3, :], ALU.add).then_inc(S["y"], 1)
                for q in range(2):
                    for h in range(2):
                        v.wait_ge(S["hi"], (n - 1) * 4 + (2 * q + h + 1))
                        v.scalar_tensor_tensor(y[h], hi[h], k["drop"][0:R3, q:q + 1], y[h], ALU.mult, ALU.add)\
                            .then_inc(S["dropped"], 1)


def widest1(nc, k, raw):
    ps, st, n = k["psum"], k["small"], 2 * NO1
    S = {n_: signal(k, "wide1_" + n_) for n_ in ("top", "turned", "steps", "flag")}
    with nc.Block() as block:
        @block.vector
        def _(v):
            step = Chain(v, S["steps"])
            v.tensor_reduce(st[0:n, 0:1], raw, AX.X, ALU.max, apply_absolute_value=True).then_inc(S["top"], 1)
            v.wait_ge(S["turned"], 1)
            step(v.tensor_reduce(st[0:1, 1:2], ps[0:1, 0:n], AX.X, ALU.max))
            v.tensor_scalar(k["flag"][:, :], st[0:1, 1:2], 2.0, None, ALU.is_gt).then_inc(S["flag"], 1)

        @block.tensor
        def _(pe):
            pe.wait_ge(S["top"], 1)
            pe.transpose(ps[0:1, 0:n], st[0:n, 0:1], k["ident"][0:n, 0:n]).then_inc(S["turned"], 1)


def turn_offsets1(nc, k, raw, om, w):
    ps, d = k["psum"], k["dram"]
    NO = 2 * NO1
    xs = w[0:NO, 0:CH]
    S = {n: signal(k, "to1_" + n) for n in ("xs", "turned", "om", "cleared", "loaded")}

    def turns(eng):
        for b2 in range(2):
            with eng.Fori(0, CPI) as r:
                yield b2, r, b2 * CPI + r + 1

    with nc.Block() as block:
        @block.scalar
        def _(act):
            act.sem_inc(S["turned"], 1)
            for b2, r, n in turns(act):
                act.wait_ge(S["turned"], n)
                act.activation(xs, raw[:, bass.ds(r * CH + b2 * PIX, CH)], ACT.Copy).then_inc(S["xs"], 1)

        @block.tensor
        def _(pe):
            pe.sem_inc(S["om"], 1)
            for b2, r, n in turns(pe):
                pe.wait_ge(S["xs"], n)
                pe.wait_ge(S["om"], n)
                for t in range(TPC):
                    mm = pe.transpose(ps[:, NO * t:NO * t + NO], xs[:, PT * t:PT * t + PT], k["ident"][0:NO, 0:NO])
                mm.then_inc(S["turned"], 1)

        @block.vector
        def _(v):
            for b2, r, n in turns(v):
                v.wait_ge(S["turned"], n + 1)
                v.tensor_copy(om[:, bass.ds((r + b2 * CPI) * (2 * TPC), 2 * TPC), :]
                              .rearrange("p t n -> p (t n)"), ps[:, 0:TPC * NO]).then_inc(S["om"], 1)

        @block.gpsimd
        def _(pool):
            pool.memset(k["dws2_flat"], 0.0).then_inc(S["cleared"], 1)

        @block.sync
        def _(sp):
            sp.wait_ge(S["cleared"], 1)
            for m in range(TAPS):
                for u in range(2):
                    s = 2 * m + u
                    v, tap = s // TAPS, s % TAPS
                    sp.dma_start(k["dws2"][64 * u:64 * u + 64, m, 64 * v:64 * v + 64], d["dws"][v, tap])\
                        .then_inc(S["loaded"], 16)
            sp.wait_ge(S["loaded"], 16 * S1)


def windows1(nc, k, o3, bmat, win, sc, smp, tmp):
    ps = k["psum"]
    S = {n: signal(k, "win_" + n) for n in
         ("loaded0", "loaded1", "spread", "abs", "hat_x", "z", "b", "pe_turn", "pool_turn", "clamped", "clamped_v", "sampled", "kept", "conv", "sc")}
    NQ = NB * CPI
    NTX = WW // IW
    PAIRS = 2 * (NTX // 2)
    p_d = [ps[0:KW, 1024 * i:1024 * i + 1024].rearrange("p (a n) -> p a n", a=2)[:, :, 0:CH] for i in range(2)]
    mag = [tmp[0:KW, 2 * CH * i:2 * CH * i + 2 * CH].rearrange("p (a n) -> p a n", a=2) for i in range(2)]
    pq = [ps[:, 512 * (4 + i):512 * (4 + i) + TAPS * IH * 2 * IW] for i in range(2)]
    pc = [ps[64 * v:64 * v + 64, 512 * (6 + v):512 * (6 + v) + CH] for v in range(2)]
    S4 = smp.rearrange("p (s y x) -> p s y x", s=TAPS, y=ROWS)

    def walk(eng, gen, mul):
        gen(eng, 0, 0, None)
        with eng.Fori(0, NQ // 2 - 1) as i:
            for par in range(2):
                gen(eng, i * 2 + (par + 1), 1 - par, lambda part, n=i * 2 + par, p=par: mul(eng, n, p, part))
        gen(eng, NQ - 1, 1, lambda part: mul(eng, NQ - 2, 0, part))
        for part in range(S1):
            mul(eng, NQ - 1, 1, part)

    FIRST = 1
    POOLED = [(0, 3), (3, 6), (6, 9), (10, 11), (12, 13), (14, 15), (15, 16), (16, 17)]
    CLAMPED = {12: 9, 14: 11, 16: 13}
    assert FIRST + PAIRS + TAPS == S1

    with nc.Block() as block:
        @block.sync
        def _(sp):
            phased = k["xw"].rearrange("b y (j t) c -> b (y j) t c", j=IW)
            for b in range(NB):
                with sp.Fori(0, CPI // 2) as i:
                    for par in range(2):
                        sp.wait_ge(S["sampled"], (i * 2 + (par + b * CPI + 1)) * PAIRS)
                        for band in range(2):
                            for a in range(2):
                                src = phased[b, bass.ds(i * (2 * ROWS * IW) + (par * ROWS + band * IH) * IW, WH * IW),
                                             a:a + WW // IW, :]
                                sp.dma_start(win[par][KW // 2 * a:KW // 2 * (a + 1), band, :, :], src)\
                                    .then_inc(S[f"loaded{par}"], 16)

        @block.tensor
        def _(pe):
            def gen(pe, n, par, mul):
                for s in range(S1):
                    c = n * S1 + (s + 1)
                    pe.wait_ge(S["abs"], c)
                    for a in range(2):
                        mm = pe.matmul(p_d[s % 2][:, a, :], k["sel1"][:, 2 * s + a, :], o3[:, chunk_cols(n)],
                                       start=True, stop=True)
                    mm.then_inc(S["spread"], 1)
                    if mul is not None:
                        mul(s)

            def mul(pe, n, par, part):
                part -= FIRST
                if part == 0:
                    pe.wait_ge(S["b"], (n + 1) * len(POOLED))
                    pe.wait_ge(S["clamped"], (n + 1) * len(CLAMPED))
                    pe.wait_ge(S["clamped_v"], n + 1)
                    pe.wait_ge(S[f"loaded{par}"], (n - par) * 32 + 64)
                if 0 <= part < PAIRS:
                    band, pair = divmod(part, NTX // 2)
                    pe.wait_ge(S["kept"], n * PAIRS + (part + 1))
                    out = pq[part % 2].rearrange("p (s y x) -> p s y x", s=TAPS, y=IH)
                    for t in range(2):
                        tile = 2 * pair + t
                        for v in range(2):
                            rhs = bmat[par].rearrange("p (s y x) -> p s y x", s=S1, y=ROWS)[
                                :, TAPS * v:TAPS * v + TAPS, IH * band:IH * band + IH, IW * tile:IW * tile + IW]
                            mm = pe.matmul(out[64 * v:64 * v + 64, :, :, IW * t:IW * t + IW],
                                           win[par][0:KW, band, tile, :], rhs, start=True, stop=True,
                                           skip_group_check=True)
                    mm.then_inc(S["sampled"], 1)
                elif part >= PAIRS:
                    if part == PAIRS:
                        pe.wait_ge(S["kept"], n * PAIRS + (PAIRS + 2))
                        pe.wait_ge(S["sc"], n + 1)
                        pe.sem_inc(S["pe_turn"], 1)
                    t = part - PAIRS
                    for v in range(2):
                        mm = pe.matmul(pc[v], k["dws"][64 * v:64 * v + 64, t, :],
                                       smp[64 * v:64 * v + 64, CH * t:CH * t + CH],
                                       start=(t == 0), stop=(t == TAPS - 1))
                    if t == TAPS - 1:
                        mm.then_inc(S["conv"], 1)

            pe.sem_inc(S["abs"], 2)
            pe.sem_inc(S["kept"], 2)
            pe.sem_inc(S["sc"], 1)
            pe.sem_inc(S["sampled"], 2 * PAIRS)
            walk(pe, gen, mul)

        @block.scalar
        def _(act):
            def gen(act, n, par, mul):
                for s in range(S1):
                    c = n * S1 + (s + 1)
                    act.wait_ge(S["z"], c)
                    act.wait_ge(S["spread"], c)
                    act.activation(mag[s % 2], p_d[s % 2], ACT.Abs).then_inc(S["abs"], 1)
                    if s in CLAMPED:
                        own = bmat[par][:, CH * CLAMPED[s]:CH * CLAMPED[s] + CH]
                        act.activation(own, own, ACT.Relu).then_inc(S["clamped"], 1)
                    if mul is not None:
                        mul(s)

            def mul(act, n, par, part):
                part -= FIRST
                if 0 <= part < PAIRS:
                    band, pair = divmod(part, NTX // 2)
                    act.wait_ge(S["sampled"], n * PAIRS + (part + 1 + 2 * PAIRS))
                    if part == 0:
                        act.wait_ge(S["conv"], n + 1)
                    act.activation(S4[:, :, IH * band:IH * band + IH, 2 * IW * pair:2 * IW * pair + 2 * IW],
                                   pq[part % 2].rearrange("p (s y x) -> p s y x", s=TAPS, y=IH), ACT.Copy)\
                        .then_inc(S["kept"], 1)

            act.sem_inc(S["z"], 2)
            act.sem_inc(S["conv"], 1)
            walk(act, gen, mul)

        @block.vector
        def _(v_):
            def gen(v_, n, par, mul):
                for s in range(S1):
                    c = n * S1 + (s + 1)
                    v_.wait_ge(S["abs"], c + 2)
                    v_.tensor_scalar(mag[s % 2][:, 1, :], mag[s % 2][:, 1, :], 1.0, 1.0, ALU.min, ALU.subtract)\
                        .then_inc(S["hat_x"], 1)
                    v_.wait_ge(S["hat_x"], c)
                    if s == 0:
                        v_.wait_ge(S["sampled"], (n + 1) * PAIRS)
                    v_.scalar_tensor_tensor(bmat[par][:, CH * s:CH * s + CH], mag[s % 2][:, 0, :], 1.0,
                                            mag[s % 2][:, 1, :],
                                            ALU.subtract, ALU.mult).then_inc(S["z"], 1)
                    if s == S1 - 1:
                        v_.wait_ge(S["z"], c + 2)
                        own = bmat[par][:, CH * s:CH * s + CH]
                        v_.tensor_scalar(own, own, 0.0, None, ALU.max).then_inc(S["clamped_v"], 1)
                    if mul is not None:
                        mul(s)

            def mul(v_, n, par, part):
                if part == S1 - 1:
                    v_.wait_ge(S["conv"], n + 2)
                    for v in range(2):
                        last = v_.tensor_scalar(sc_cols(sc, n)[64 * v:64 * v + 64, :], pc[v],
                                                k["dbs"][64 * v:64 * v + 64, 0:1], None, ALU.add)
                    last.then_inc(S["sc"], 1)

            walk(v_, gen, mul)

        @block.gpsimd
        def _(pool):
            def gen(pool, n, par, mul):
                for lo, hi in POOLED:
                    pool.wait_ge(S["z"], n * S1 + (hi + 2))
                    pool.sem_inc(S["pool_turn"], 1)
                    part = bmat[par][:, CH * lo:CH * hi]
                    pool.tensor_scalar(part, part, 0.0, None, ALU.max).then_inc(S["b"], 1)

            walk(pool, gen, lambda *a: None)


def chunk_cols(n):
    return bass.ds(n * CH, CH)


def sc_cols(sc, n):
    return sc.rearrange("p h n -> p (h n)")[:, chunk_cols(n)]


def fuse1(nc, k):
    ctx, ps = k["ctx"], k["psum"]
    sc, xn, x, st = k["sc"], k["xn"], k["x"], k["small"]
    S = {n: signal(k, "fuse_" + n) for n in
         ("v", "pe", "act", "steps", "mix_ps", "mixed", "gated", "added", "gsteps")}
    pool4, gm = st[:, 0:4], st[:, 4:6]
    h8, lg, wts = st[0:8, 8:12], st[0:4, 12:14], st[0:4, 16:18]
    wide = k["wide"]
    g1, g2, gate = st[0:32, 20:24], st[0:32, 24:28], st[:, 28:32]
    mixw = k["mixw"]
    gx = [k["arena"][:, CH * i:CH * i + CH] for i in range(2)]
    p_mix = [ps[:, 512 * (1 + i):512 * (1 + i) + CH] for i in range(2)]
    p_red = [ps[:, 512 * (6 + i):512 * (6 + i) + CH] for i in range(2)]

    def turns(eng):
        for b2 in range(2):
            with eng.Fori(0, CPI // 2) as i:
                for par in range(2):
                    yield b2, i * 2 + par, i * 2 + (par + b2 * CPI + 1), par

    with nc.Block() as block:
        @block.vector
        def _(v):
            step = Chain(v, S["steps"])
            v.memset(k["mixw_flat"], 0.0)
            step(v.tensor_reduce(pool4, sc.rearrange("p h (b n) -> p (h b) n", b=2), AX.X, ALU.add))
            step(pooled_norm(v, k, gm))
            step(v.tensor_tensor(gm, gm, k["stats"][:, 10:12], ALU.mult))
            v.tensor_scalar(pool4, pool4, 1.0 / PIX, None, ALU.mult).then_inc(S["v"], 1)
            v.wait_ge(S["pe"], 2)
            step(v.tensor_tensor(lg, ps[0:4, 2048:2050], k["wgb2"][:, :], ALU.add))
            step(v.tensor_reduce(st[0:4, 14:15], lg, AX.X, ALU.max, negate=True))
            v.tensor_scalar(lg, lg, st[0:4, 14:15], None, ALU.add).then_inc(S["v"], 1)
            v.wait_ge(S["act"], 2)
            step(v.tensor_reduce(st[0:4, 14:15], wts, AX.X, ALU.add))
            step(v.reciprocal(st[0:4, 15:16], st[0:4, 14:15]))
            step(v.tensor_scalar(wts, wts, st[0:4, 15:16], None, ALU.mult))
            v.tensor_copy(wide[:, :].rearrange("b (v c) -> b v c", v=2),
                          wts.unsqueeze(2).to_broadcast([4, 2, C])).then_inc(S["v"], 1)
            v.wait_ge(S["pe"], 3)
            step(v.tensor_copy(st[:, 32:36], ps[:, 2560:2564]))
            for b in range(NB):
                h = b // 2
                last = v.tensor_scalar(mixw[:, b, 64 * h:64 * h + 64], k["stack2"][:, :], st[:, 32 + b:33 + b],
                                       None, ALU.mult)
            last.then_inc(S["v"], 1)
            v.wait_ge(S["act"], 5)
            v.sem_inc(S["added"], 2)
            for b2, r, n, par in turns(v):
                v.wait_ge(S["mix_ps"], n)
                xs = x[:, bass.ds(r * CH + b2 * PIX, CH)]
                v.tensor_tensor(xs, xs, p_mix[par], ALU.add).then_inc(S["added"], 1)
                v.wait_ge(S["added"], n + 2)
                v.wait_ge(S["gated"], n)
                v.tensor_tensor(xs, xs, gx[par], ALU.add).then_inc(S["mixed"], 1)

        @block.tensor
        def _(pe):
            pe.wait_ge(S["v"], 1)
            pe.matmul(ps[0:8, 0:4], k["wg1T"][:, :], pool4, start=True, stop=True)
            for h in range(2):
                mm = pe.matmul(ps[0:32, 512 * (2 + h):512 * (2 + h) + 2], k["gp1T"][64 * h:64 * h + 64, :],
                               gm[64 * h:64 * h + 64, :], start=True, stop=True)
            mm.then_inc(S["pe"], 1)
            pe.wait_ge(S["act"], 1)
            pe.matmul(ps[0:4, 2048:2050], h8, k["wg2T"][:, :], start=True, stop=True).then_inc(S["pe"], 1)
            pe.wait_ge(S["v"], 3)
            pe.matmul(ps[:, 2560:2564], wide[:, :], k["ident"][0:4, 0:4], start=True, stop=True).then_inc(S["pe"], 1)
            pe.wait_ge(S["act"], 3)
            pe.matmul(ps[0:32, 3072:3076], k["gp2T"][:, :], g1, start=True, stop=True).then_inc(S["pe"], 1)
            pe.wait_ge(S["act"], 4)
            pe.matmul(ps[:, 3584:3588], k["gp3T"][:, :], g2, start=True, stop=True).then_inc(S["pe"], 1)
            pe.wait_ge(S["v"], 4)
            pe.wait_ge(S["act"], 5)
            pe.sem_inc(S["mixed"], 2)
            for b2, r, n, par in turns(pe):
                pe.wait_ge(S["mixed"], n)
                for h in range(2):
                    pe.matmul(p_mix[par], mixw[:, 2 * h + b2, :], sc[:, h, bass.ds(r * CH + b2 * PIX, CH)],
                              start=(h == 0), stop=(h == 1))
                pe.matmul(p_red[par], k["crT"][:, :], xn[:, bass.ds(r * CH + b2 * PIX, CH)],
                          start=True, stop=True).then_inc(S["mix_ps"], 1)

        @block.scalar
        def _(act):
            act.wait_ge(S["pe"], 1)
            act.activation(g1[:, 0:2], ps[0:32, 1024:1026], ACT.Relu, bias=k["gpb1"][:, 0:1])
            act.activation(g1[:, 2:4], ps[0:32, 1536:1538], ACT.Relu, bias=k["gpb1"][:, 0:1])
            act.activation(h8, ps[0:8, 0:4], ACT.Relu, bias=k["wgb1"][:, 0:1]).then_inc(S["act"], 1)
            act.wait_ge(S["v"], 2)
            act.activation(wts, lg, ACT.Exp).then_inc(S["act"], 1)
            act.wait_ge(S["pe"], 3)
            act.sem_inc(S["act"], 1)
            act.wait_ge(S["pe"], 4)
            act.activation(g2, ps[0:32, 3072:3076], ACT.Relu, bias=k["gpb2"][:, 0:1]).then_inc(S["act"], 1)
            act.wait_ge(S["pe"], 5)
            act.activation(gate, ps[:, 3584:3588], ACT.Sigmoid,
                           bias=k["vec"][:, VC["gp_b3"]:VC["gp_b3"] + 1]).then_inc(S["act"], 1)
            act.wait_ge(S["act"], 5)
            for b2 in range(2):
                for h in range(2):
                    r = slice(64 * h, 64 * h + 64)
                    act.activation(st[r, 36 + b2:37 + b2], gate[r, 2 * h + b2:2 * h + b2 + 1], ACT.Copy)\
                        .then_inc(S["gsteps"], 1)
            act.wait_ge(S["gsteps"], 4)
            act.activation(st[:, 38:40], st[:, 36:38], ACT.Copy,
                           scale=k["vec"][:, VC["cr_b"]:VC["cr_b"] + 1]).then_inc(S["gsteps"], 1)
            act.wait_ge(S["gsteps"], 5)
            for b2, r, n, par in turns(act):
                act.wait_ge(S["mix_ps"], n)
                act.wait_ge(S["mixed"], n)
                act.activation(gx[par], p_red[par], ACT.Identity, scale=st[:, 36 + b2:37 + b2],
                               bias=st[:, 38 + b2:39 + b2]).then_inc(S["gated"], 1)


def pooled_norm(v, k, out):
    st = k["stats"]
    return v.scalar_tensor_tensor(out, st[:, 0:2], 1.0 / PIX, st[:, 2:4], ALU.mult, ALU.subtract)


def project2(nc, k, work, parts, at, qa, ka, qb, kb):
    ps, xn = k["psum"], k["xn"]
    buf = [work[:, CH * i:CH * i + CH] for i in range(11)]
    xs, y, t1, t2 = (buf[2 * i:2 * i + 2] for i in range(4))
    ty, ya, ta = buf[8:]
    S = {n: signal(k, "proj2_" + n) for n in
         ("xs", "ps", "biased", "neg_y", "prelu", "ya", "neg_a", "done", "high", "rest1", "middle", "rest2",
          "low", "stacked", "ones")}
    al = k["alphas"]
    p_y = [ps[:, 512 * i:512 * i + CH] for i in range(2)]
    p_a = [ps[:, 512 * (2 + i):512 * (2 + i) + CH] for i in range(2)]
    H_, M_, L_ = 0, 1, 2
    plan = [(qa, 0, (H_, H_, M_)), (ka, 1, (H_, M_, H_)), (qb, 0, (M_, L_, H_)), (kb, 1, (M_, H_, L_))]

    def turns(eng):
        for b2 in range(2):
            with eng.Fori(0, CPI // 2) as i:
                for par in range(2):
                    r = i * 2 + par
                    yield b2, r, bass.ds(r * CH + b2 * PIX, CH), i * 2 + (par + b2 * CPI + 1), par

    with nc.Block() as block:
        @block.gpsimd
        def _(pool):
            pool.memset(ka[96:99, :], 1.0).then_inc(S["ones"], 1)
            pool.wait_ge(S["ones"], 1)
            pool.memset(at[:, :, C:2 * C], 1.0).then_inc(S["ones"], 1)
            pool.wait_ge(S["ones"], 2)
            pool.sem_inc(S["ps"], 2)
            for b2, r, cols, n, par in turns(pool):
                pool.wait_ge(S["ps"], n)
                pool.tensor_copy(xs[par], xn[:, cols]).then_inc(S["xs"], 1)

        @block.tensor
        def _(pe):
            pe.sem_inc(S["biased"], 2)
            pe.sem_inc(S["ya"], 2)
            for b2, r, cols, n, par in turns(pe):
                pe.wait_ge(S["xs"], n)
                pe.wait_ge(S["biased"], n)
                pe.matmul(p_y[par], k["l2w"][:, :], xs[par], start=True, stop=True)
                pe.wait_ge(S["ya"], n)
                for t in range(TPC):
                    mm = pe.matmul(p_a[par][:, PT * t:PT * t + PT], xs[par][:, PT * t:PT * t + PT],
                                   k["waT"][:, :], start=True, stop=True)
                mm.then_inc(S["ps"], 1)

        @block.scalar
        def _(act):
            act.sem_inc(S["rest1"], 2)
            for b2, r, cols, n, par in turns(act):
                act.wait_ge(S["ps"], n + 2)
                act.wait_ge(S["rest1"], n)
                act.activation(y[par], p_y[par], ACT.Identity, bias=k["l2b"][:, 0:1]).then_inc(S["biased"], 1)
                act.wait_ge(S["prelu"], n)
                act.activation(parts[0][:, cols], y[par], ACT.Copy).then_inc(S["high"], 1)
                act.wait_ge(S["rest1"], n + 2)
                act.activation(parts[1][:, cols], t1[par], ACT.Copy).then_inc(S["middle"], 1)
                act.wait_ge(S["rest2"], n)
                act.activation(parts[2][:, cols], t2[par], ACT.Copy).then_inc(S["low"], 1)

        @block.vector
        def _(v):
            v.sem_inc(S["done"], 1)
            v.sem_inc(S["low"], 2)
            for b2, r, cols, n, par in turns(v):
                v.wait_ge(S["biased"], n + 2)
                v.tensor_scalar(ty, y[par], 0.0, al[:, 0:1], ALU.min, ALU.mult).then_inc(S["neg_y"], 1)
                v.wait_ge(S["neg_y"], n)
                v.scalar_tensor_tensor(y[par], y[par], 0.0, ty, ALU.max, ALU.add).then_inc(S["prelu"], 1)
                v.wait_ge(S["done"], n)
                v.tensor_tensor(ya.rearrange("p (t c) -> p t c", c=C), p_a[par].rearrange("p (t c) -> p t c", c=C),
                                k["ba"][:, :].unsqueeze(1).to_broadcast([128, 2 * TPC, C]), ALU.add)\
                    .then_inc(S["ya"], 1)
                v.wait_ge(S["ya"], n + 2)
                v.tensor_scalar(ta, ya, 0.0, al[:, 1:2], ALU.min, ALU.mult).then_inc(S["neg_a"], 1)
                v.wait_ge(S["high"], n)
                v.tensor_tensor(t1[par], y[par], parts[0][:, cols], ALU.subtract).then_inc(S["rest1"], 1)
                v.wait_ge(S["neg_a"], n)
                for h in range(2):
                    y3 = ya.rearrange("p (t h c) -> p t h c", h=2, c=C)[:, :, h, :]
                    t3 = ta.rearrange("p (t h c) -> p t h c", h=2, c=C)[:, :, h, :]
                    last = v.scalar_tensor_tensor(at[:, bass.ds((r + b2 * CPI) * TPC, TPC), 2 * C * h:2 * C * h + C],
                                                  y3, 0.0, t3, ALU.max, ALU.add)
                last.then_inc(S["done"], 1)
                v.wait_ge(S["middle"], n)
                v.wait_ge(S["low"], n)
                v.tensor_tensor(t2[par], t1[par], parts[1][:, cols], ALU.subtract).then_inc(S["rest2"], 1)

        @block.sync
        def _(sp):
            for b2 in range(2):
                sp.wait_ge(S["low"], CPI * (b2 + 1) + 2)
                for dst, e, order in plan:
                    for pos, q in enumerate(order):
                        for h in range(2):
                            u = 2 * b2 + h
                            sp.dma_start(dst[HID * pos:HID * pos + HID, PIX * u:PIX * u + PIX],
                                         parts[q][64 * h + HID * e:64 * h + HID * e + HID, PIX * b2:PIX * b2 + PIX])\
                                .then_inc(S["stacked"], 16)
            sp.wait_ge(S["stacked"], 16 * 48)


def attend2(nc, k, qa, ka, qb, kb, at):
    ctx, ps, x = k["ctx"], k["psum"], k["x"]
    A = k["atwork"]
    BF = mybir.dt.bfloat16
    SLOTS = 6
    pt = [A[:, CH * i:CH * i + CH] for i in range(SLOTS)]
    recs = [A[:, (SLOTS + i) * CH:(SLOTS + i + 1) * CH] for i in range(2)]
    at0 = (SLOTS + 2) * CH
    acc_pool, acc_v, out_sum = (A[:, at0 + CH * i:at0 + CH * i + CH] for i in range(3))
    at0 += 3 * CH
    part = A[:, at0:at0 + 18]
    mx = A[:, at0 + 18:at0 + 36]
    rest = A[:, at0 + 36:at0 + 72]
    mparts = A[:, at0 + 72:at0 + 99].bitcast(BF)
    mrow = A[:, at0 + 100:at0 + 164].bitcast(BF)
    S = {n: signal(k, "att_" + n) for n in
         ("scores", "probs", "pv", "maxmm", "maxred", "steps", "mparts", "mrow_ps", "mrow", "mset", "added",
          "sum_pool", "sum_v", "sums")}
    KA, KB = 3 * HID + 3, 3 * HID
    NJ = TPI
    LATE = 6
    NS, NM = 2, 3
    p_s = [ps[:, 512 * i:512 * i + CH] for i in range(NS)]
    p_m = [ps[:, 512 * (NS + i):512 * (NS + i) + CH] for i in range(NM)]
    p_o = [ps[:, 3072 + 512 * i:3072 + 512 * i + CH] for i in range(2)]
    p_sum = ps[:, 512 * (NS + NM):512 * (NS + NM) + CH]
    p_r = ps[0:3 * NJ, 512 * NS:512 * NS + 64].bitcast(BF)

    ADDS = {"sum_v": [7, 8, 15, 16, 17]}
    ADDS["sum_pool"] = [j for j in range(NJ) if j not in ADDS["sum_v"]]

    def add_up(eng, name, acc, u, ib, place):
        js, m = ADDS[name], len(ADDS[name]) - 1
        blk = ib + u * CPI
        j = js[place]
        eng.wait_ge(S["probs"], blk * NJ + (j + 1 + NS))
        if place == 1:
            eng.wait_ge(S["sums"], blk + 1)
            a = pt[js[0] % SLOTS]
        else:
            eng.wait_ge(S[name], (blk + 1) * m + (place - 1))
            a = acc
        eng.tensor_tensor(acc, a, pt[j % SLOTS], ALU.add).then_inc(S[name], 1)

    def blocks(eng):
        with eng.Fori(0, CPI // 2) as i:
            for par in range(2):
                yield i * 2 + par, par

    def last_step(u, ib):
        return ib * NJ + (u * CPI + 1) * NJ

    with nc.Block() as block:
        @block.gpsimd
        def _(pool):
            pool.memset(k["xp_flat"], 0.0)
            pool.sem_inc(S["sum_pool"], len(ADDS["sum_pool"]) - 1)
            for u in range(NB):
                with pool.Fori(0, CPI) as ib:
                    for place in range(1, len(ADDS["sum_pool"])):
                        add_up(pool, "sum_pool", acc_pool, u, ib, place)

        @block.sync
        def _(sp):
            for u in range(NB):
                sp.wait_ge(S["mrow"], u + 1)
                for q in range(3):
                    sp.dma_start(qa[96 + q:97 + q, PIX * u:PIX * u + PIX], mrow[NJ * q:NJ * q + NJ, :])\
                        .then_inc(S["mset"], 16)

        @block.tensor
        def _(pe):
            def maxima(u, ib, j):
                n = ib * NJ + (u * CPI * NJ + j + 1)
                pe.wait_ge(S["maxred"], n)
                pe.matmul(p_m[j % NM], qa[0:KB, bass.ds(ib * CH + (u * PIX + PT * (j // 6)), PT)],
                          ka[0:KB, u * PIX + CH * (j % 6):u * PIX + CH * (j % 6) + CH],
                          start=True, stop=True).then_inc(S["maxmm"], 1)

            def maxrow(u):
                pe.wait_ge(S["mparts"], u + 1)
                pe.transpose(p_r, mparts, k["identb"][:, :]).then_inc(S["mrow_ps"], 1)

            def scores(u, ib, j):
                n = ib * NJ + (u * CPI * NJ + j + 1)
                pe.wait_ge(S["probs"], n)
                q = bass.ds(ib * CH + u * PIX, CH)
                kk = slice(u * PIX + PT * j, u * PIX + PT * j + PT)
                pe.matmul(p_s[j % NS], ka[0:KA, kk], qa[0:KA, q], start=True, stop=False)
                pe.matmul(p_s[j % NS], kb[0:KB, kk], qb[0:KB, q], start=False, stop=True)\
                    .then_inc(S["scores"], 1)

            def values(u, ib, par, j):
                pe.wait_ge(S["probs"], ib * NJ + (u * CPI * NJ + j + 2 + NS))
                h, b2 = u % 2, u // 2
                for i in range(2):
                    mm = pe.matmul(p_o[par][64 * i:64 * i + 64, :], at[:, b2 * TPI + j + i, 2 * C * h:2 * C * h + C],
                                   pt[(j + i) % SLOTS], start=(j == 0), stop=(j == NJ - 2))
                mm.then_inc(S["pv"], 2)

            def sums(u, ib):
                h, b2, blk = u % 2, u // 2, ib + u * CPI
                own = slice(64 * h, 64 * h + 64)
                pe.wait_ge(S["sum_pool"], (blk + 2) * (len(ADDS["sum_pool"]) - 1))
                pe.wait_ge(S["added"], blk + 2)
                pe.matmul(p_sum[own, :], at[:, b2 * TPI, C:2 * C], acc_pool, start=True, stop=False)
                pe.wait_ge(S["sum_v"], (blk + 2) * (len(ADDS["sum_v"]) - 1))
                pe.matmul(p_sum[own, :], at[:, b2 * TPI, C:2 * C], acc_v, start=False, stop=True)\
                    .then_inc(S["sums"], 1)

            def block_of(u, ib, par, more):
                for j in range(NJ):
                    if j and j + 1 < NJ:
                        scores(u, ib, j + 1)
                    if u + 1 < NB and j >= LATE:
                        for m in range((j - LATE) * NJ // (NJ - LATE), (j - LATE + 1) * NJ // (NJ - LATE)):
                            maxima(u + 1, ib, m)
                    if j == 3:
                        pe.wait_ge(S["added"], ib + (u * CPI + 1))
                    if j >= 3 and j % 2 == 1:
                        values(u, ib, par, j - 3)
                if more:
                    scores(u, ib + 1, 0)
                    scores(u, ib + 1, 1)
                values(u, ib, par, NJ - 2)
                sums(u, ib)

            pe.sem_inc(S["maxred"], NM)
            pe.sem_inc(S["probs"], NS)
            pe.sem_inc(S["pv"], SLOTS)
            pe.sem_inc(S["added"], 2)
            pe.sem_inc(S["sums"], 1)
            with pe.Fori(0, CPI) as ib:
                for j in range(NJ):
                    maxima(0, ib, j)
            maxrow(0)
            for u in range(NB):
                pe.wait_ge(S["mset"], 48 * (u + 1))
                scores(u, 0, 0)
                scores(u, 0, 1)
                with pe.Fori(0, CPI // 2 - 1) as i:
                    for par in range(2):
                        block_of(u, i * 2 + par, par, True)
                block_of(u, CPI - 2, 0, True)
                block_of(u, CPI - 1, 1, False)
                if u + 1 < NB:
                    maxrow(u + 1)

        @block.scalar
        def _(act):
            for u in range(NB):
                with act.Fori(0, CPI) as ib:
                    for j in range(NJ):
                        n = ib * NJ + (u * CPI * NJ + j + 1)
                        act.wait_ge(S["scores"], n)
                        act.wait_ge(S["pv"], n)
                        last = (j - SLOTS) % NJ
                        for name, js in ADDS.items():
                            if last in js:
                                m = len(js) - 1
                                act.wait_ge(S[name], (ib + (u * CPI + (j >= SLOTS))) * m + max(1, js.index(last)))
                        act.activation(pt[j % SLOTS], p_s[j % NS], ACT.Exp).then_inc(S["probs"], 1)

        @block.vector
        def _(v):
            step = Chain(v, S["steps"])

            def add_at(u, ib, j):
                js = ADDS["sum_v"]
                if j in js and js.index(j):
                    add_up(v, "sum_v", acc_v, u, ib, js.index(j))

            def maxima(u, ib, adds=True):
                for j in range(NJ):
                    if adds:
                        add_at(u - 1, ib, j)
                    v.wait_ge(S["maxmm"], ib * NJ + (u * CPI * NJ + j + 1))
                    v.tensor_reduce(part[:, j:j + 1], p_m[j % NM], AX.X, ALU.max).then_inc(S["maxred"], 1)
                v.wait_ge(S["maxred"], last_step(u, ib) + NM)
                step(v.tensor_reduce(mx[:, bass.ds(ib * 3, 3)], part.rearrange("p (i c) -> p i c", c=6), AX.X,
                                     ALU.max, negate=True))

            def split_maxima(u):
                m = [mparts[:, NJ * q:NJ * q + NJ] for q in range(3)]
                step(v.tensor_copy(m[0], mx))
                step(v.tensor_tensor(rest[:, 0:NJ], mx, m[0], ALU.subtract))
                step(v.tensor_copy(m[1], rest[:, 0:NJ]))
                step(v.tensor_tensor(rest[:, NJ:2 * NJ], rest[:, 0:NJ], m[1], ALU.subtract))
                v.tensor_copy(m[2], rest[:, NJ:2 * NJ]).then_inc(S["mparts"], 1)
                v.wait_ge(S["mrow_ps"], u + 1)
                if u:
                    v.wait_ge(S["mset"], 48 * u)
                v.tensor_copy(mrow[0:3 * NJ, :], p_r).then_inc(S["mrow"], 1)

            v.sem_inc(S["sum_v"], len(ADDS["sum_v"]) - 1)
            with v.Fori(0, CPI) as ib, step.body(ib, 1, CPI):
                maxima(0, ib, False)
            split_maxima(0)
            for u in range(NB):
                h, b2 = u % 2, u // 2
                more = u + 1 < NB
                per = 5 if more else 4
                start = step.n
                for ib, par in blocks(v):
                    step.off, step.n = ib * per + start, 0
                    if more:
                        maxima(u + 1, ib)
                    else:
                        for j in range(NJ):
                            add_at(u, ib, j)
                    v.wait_ge(S["pv"], last_step(u, ib) + SLOTS)
                    own, other = slice(64 * h, 64 * h + 64), slice(64 - 64 * h, 128 - 64 * h)
                    rec = recs[par]
                    v.wait_ge(S["added"], ib + (u * CPI + 2))
                    step(v.tensor_copy(out_sum[own, :], p_o[par][other, :]))
                    step(v.tensor_tensor(out_sum[own, :], out_sum[own, :], p_o[par][own, :], ALU.add))
                    v.wait_ge(S["sums"], ib + (u * CPI + 2))
                    step(v.reciprocal(rec[own, :], p_sum[own, :]))
                    step(v.tensor_tensor(rec[own, :], rec[own, :], out_sum[own, :], ALU.mult))
                    xs = x[own, bass.ds(ib * CH + b2 * PIX, CH)]
                    v.tensor_tensor(xs, xs, rec[own, :], ALU.add).then_inc(S["added"], 1)
                step.off, step.n = 0, start + per * CPI
                if more:
                    split_maxima(u + 1)


def weights3(k):
    A, n = k["arena"], C // 4 * TAPS * C
    return A[:, 0:n], A[:, n:n + TAPS * C]


def dynamic3(nc, k):
    ps, x, xp, d = k["psum"], k["x"], k["xp"], k["dram"]
    A = k["arena"]
    QC = C // 4
    w2, b2t = weights3(k)
    n_w = QC * TAPS * C
    at = n_w + TAPS * C
    gen = A[:, at:at + n_w]
    at += n_w
    wbd = A[:, at:at + 2 * TAPS * 128].rearrange("p (b t o) -> p b t o", b=2, t=TAPS)
    at += 2 * TAPS * 128
    hb = A[:, at:at + NB]
    hbd = A[:, at + NB:at + NB + 128]
    gm = k["small"][:, 4:6]
    N_G = n_w // CH
    S = {n: signal(k, "dyn_" + n) for n in
         ("steps", "pooled", "h_ps", "hbd", "gen_ps", "gen_act", "gen_v", "cleared", "moved0", "moved1", "wbd",
          "conv_ps", "added", "stored")}
    p_g = [ps[:, 512 * i:512 * i + CH] for i in range(4)]
    p_c = [ps[:, 512 * (4 + i):512 * (4 + i) + CH] for i in range(2)]
    w3 = w2.rearrange("p (g n) -> p g n", n=CH)
    g3 = gen.rearrange("p (g n) -> p g n", n=CH)

    def turns(eng):
        for b2 in range(2):
            with eng.Fori(0, CPI // 2) as i:
                for par in range(2):
                    yield b2, i * 2 + par, i * 2 + (par + b2 * CPI + 1), par

    with nc.Block() as block:
        @block.gpsimd
        def _(pool):
            pool.memset(wbd.rearrange("p b t o -> p (b t o)"), 0.0).then_inc(S["cleared"], 1)

        @block.sync
        def _(sp):
            sp.wait_ge(S["cleared"], 1)
            sp.wait_ge(S["gen_act"], N_G // 2)
            sp.wait_ge(S["gen_v"], N_G // 2)
            for b2 in range(2):
                for h in range(2):
                    for q in range(4):
                        b = 2 * h + b2
                        sp.dma_start(wbd[64 * h + QC * q:64 * h + QC * q + QC, b2, :, 64 * h:64 * h + 64],
                                     gen[32 * q + b:32 * q + b + 1, :]
                                     .rearrange("a (c t o) -> a c t o", c=QC, t=TAPS)).then_inc(S[f"moved{b2}"], 16)
            for b2, r, n, par in turns(sp):
                sp.wait_ge(S["added"], n + 2)
                for h in range(2):
                    sp.dma_start(d["out"].rearrange("b c y x -> b c (y x)")[2 * h + b2, :, bass.ds(r * CH, CH)],
                                 x[64 * h:64 * h + 64, bass.ds(r * CH + b2 * PIX, CH)]).then_inc(S["stored"], 16)
            sp.wait_ge(S["stored"], 2 * 2 * CPI * 16)

        @block.tensor
        def _(pe):
            pe.wait_ge(S["pooled"], 1)
            for h in range(2):
                r = slice(64 * h, 64 * h + 64)
                mm = pe.matmul(ps[:, 512 * (6 + h):512 * (6 + h) + 2], k["w31T"][r, :], gm[r, :],
                               start=True, stop=True)
            mm.then_inc(S["h_ps"], 1)
            pe.wait_ge(S["hbd"], 4)
            for g in range(N_G):
                if g >= 4:
                    pe.wait_ge(S[("gen_act", "gen_v")[g % 2]], g // 2 - 1)
                pe.matmul(p_g[g % 4], hbd, w3[:, g, :], start=True, stop=True).then_inc(S["gen_ps"], 1)
            pe.sem_inc(S["added"], 2)
            for b2, r, n, par in turns(pe):
                pe.wait_ge(S["wbd"], 2 * (b2 + 1))
                pe.wait_ge(S["added"], n)
                for t in range(TAPS):
                    mm = pe.matmul(p_c[par].rearrange("p (y x) -> p y x", y=ROWS),
                                   wbd[:, b2, t, :], chunk_window(xp, b2, r, t),
                                   start=(t == 0), stop=(t == TAPS - 1))
                mm.then_inc(S["conv_ps"], 1)

        @block.scalar
        def _(act):
            for g in range(0, N_G, 2):
                act.wait_ge(S["gen_ps"], g + 1)
                act.activation(g3[:, g, :], p_g[g % 4], ACT.Copy).then_inc(S["gen_act"], 1)

        @block.vector
        def _(v):
            step = Chain(v, S["steps"])
            step(v.memset(hbd, 0.0))
            step(pooled_norm(v, k, gm))
            v.tensor_tensor(gm, gm, k["stats"][:, 10:12], ALU.mult).then_inc(S["pooled"], 1)
            v.wait_ge(S["h_ps"], 1)
            step(v.tensor_scalar(hb.rearrange("p (h b) -> p h b", h=2),
                                 ps[:, 3072:4096].rearrange("p (h n) -> p h n", h=2)[:, :, 0:2],
                                 k["b1_3"][:, 0:1], 0.0, ALU.add, ALU.max))
            for q in range(4):
                r = slice(32 * q, 32 * q + 32)
                v.tensor_copy(hbd[r, 32 * q:32 * q + NB], hb[r, :]).then_inc(S["hbd"], 1)
            for g in range(1, N_G, 2):
                v.wait_ge(S["gen_ps"], g + 1)
                v.tensor_copy(g3[:, g, :], p_g[g % 4]).then_inc(S["gen_v"], 1)
            for b2 in range(2):
                v.wait_ge(S[f"moved{b2}"], 16 * 8)
                for h in range(2):
                    r = slice(64 * h, 64 * h + 64)
                    w = wbd[r, b2, :, 64 * h:64 * h + 64]
                    v.tensor_tensor(w, w, b2t[r, :].rearrange("p (t o) -> p t o", t=TAPS), ALU.add)\
                        .then_inc(S["wbd"], 1)
            for b2, r, n, par in turns(v):
                v.wait_ge(S["conv_ps"], n)
                xs = x[:, bass.ds(r * CH + b2 * PIX, CH)]
                v.tensor_tensor(xs, xs, p_c[par], ALU.add).then_inc(S["added"], 1)


def clear_borders(nc, k):
    cleared = signal(k, "borders_cleared")
    with nc.Block() as block:
        @block.gpsimd
        def _(pool):
            pool.memset(k["xp_flat"], 0.0).then_inc(cleared, 1)
            pool.wait_ge(cleared, 1)


def store_x(nc, k):
    stored = signal(k, "dbg_stored")
    with nc.Block() as block:
        @block.sync
        def _(sp):
            for h in range(2):
                sp.dma_start(k["dram"]["out"][2 * h:2 * h + 2].rearrange("b c y x -> c b (y x)"),
                             k["x"][64 * h:64 * h + 64, :].rearrange("c (b n) -> c b n", b=2)).then_inc(stored, 16)
            sp.wait_ge(stored, 32)


STAGES = 4
WIDE = 1


def program(nc, dram):
    with ExitStack() as ctx:
        k = {"ctx": ctx, "dram": dram, "nc": nc, "signals": []}

        def sb(name, shape, dt=F32):
            k[name] = ctx.enter_context(nc.sbuf_tensor(name + "_sb", shape, dt))
            return k[name]

        sb("x", [128, COLS])
        sb("xn", [128, COLS])
        sb("xp", [128, 2, PH, PH])
        for name, shape in [("vec", [128, len(V64)]), ("dw", [128, TAPS]), ("ident", [128, 128]),
                            ("pairm", [128, 128]), ("halfm", [128, 128]), ("b_om", [128, OM]), 
                            ("b1_3", [128, 1]), ("ba", [128, C]), ("offb", [72, 1]), ("dbs", [128, 1]),
                            ("wg1T", [128, 8]), ("wgb1", [8, 1]), ("wg2T", [8, 2]), ("wgb2", [4, 2]),
                            ("gp1T", [128, 32]), ("gpb1", [32, 1]), ("gp2T", [32, 32]), ("gpb2", [32, 1]),
                            ("gp3T", [32, 128]), ("l2b", [128, 1]), ("stack2", [128, 64]), ("alphas", [128, 2]),
                            ("wom", [128, 2 * OM]), ("win", [128, 128]), ("wout", [128, 128]),
                            ("crT", [128, 128]), ("waT", [128, 128]), ("w31T", [128, 128]),
                            ("offw", [128, TAPS, 72]), ("l2w", [128, 128]), ("drop", [R3, 2]),
                            ("eps", [128, 1]), ("ones", [128, 1]), ("dwdiag", [128, TAPS, 128]), ("bn", [128, 6]),
                            ("stats", [128, 12]), ("small", [128, 40]), ("wide", [4, 128]),
                            ("mixw", [128, NB, 128])]:
            if name != "dwdiag":
                sb(name, shape)
        sb("identb", [128, 128], mybir.dt.bfloat16)
        sb("flag", [1, 1], mybir.dt.int32)
        sb("sel", [3 * 2 * G * 5, 5, 128], mybir.dt.bfloat16)
        sb("istage", [128, 2, MG], U32)
        for name in ("wom", "win", "wout", "crT", "waT", "l2w"):
            k[name + "_flat"] = k[name][:, :]
        k["offw_flat"] = k["offw"][:, :, :]
        k["mixw_flat"] = k["mixw"][:, :, :]
        k["xp_flat"] = k["xp"][:, :, :, :].rearrange("p b y x -> p (b y x)")
        AR = 32500
        arena = sb("arena", [128, AR])[:, :]
        k["arena"] = arena
        k["dwdiag"] = arena[:, 15000:15000 + TAPS * 128].rearrange("p (t n) -> p t n", t=TAPS)
        k["psum"] = ctx.enter_context(nc.psum_tensor("ps", [128, 4096], F32))[:, :]
        k["xw"] = nc.dram_tensor("pixel_major", (NB, PW, PW, C), F32).ap()
        k["tab"] = nc.dram_tensor("quads", (NB * TR, TR * 4 * C), F32).ap()

        loads = load_stage(nc, k)

        xq0 = AR - 2 * PQ * PQ
        k["xproj"] = arena[:, xq0:AR].rearrange("p (b y x) -> p b y x", b=2, y=PQ)
        group_norm(nc, k, "gn0", True, loads)
        vector_setup(nc, k)
        M = 2 * NT
        om0 = arena[:, 0:M * OM].rearrange("p (t n) -> p t n", n=OM)
        k["work0"] = arena[:, M * OM:M * OM + 8 * CH]
        offsets0(nc, k, om0)
        window_counts(nc, k, om0)
        wide = nc.values_load(k["flag"][0:1, 0:1], min_val=0, max_val=1)
        with nc.If(wide < WIDE):
            n = M * 2 * MG
            at = M * OM
            hp, hn = arena[:, at:at + n], arena[:, at + n:at + 2 * n]
            at += 2 * n
            A = arena[:, at:at + M * G * W * W]
            assert at + M * G * W * W <= xq0
            BF = mybir.dt.bfloat16
            n = NT * 3 * 2 * G * W * W // 2
            parts = arena[:, 0:n].bitcast(BF)
            parts = parts.rearrange("p (j u q n v) -> p j u q n v", u=W, q=3, n=2 * G, v=W)
            rest = k["rest0"] = arena[:, n:n + M * G * W * W]
            window_weights(nc, k, om0, hp, hn, A, parts, rest, (k["xn"][:, :], k["xp_flat"]))
            att = arena[:, n:n + W * CH // 2].bitcast(BF)
            n += W * CH // 2
            window_taps(nc, k, parts, att, arena[:, n:n + W * W * CH], arena[:, n + W * W * CH:n + (W * W + 2) * CH])
        with nc.Else():
            xq = k["xproj"]
            pixels_out(nc, k, "pix0", lambda b2, r: xq[:, b2, bass.ds(r * ROWS + 2, ROWS), 2:2 + WW],
                       k["work0"])
            at = AR - M * 2 * MG
            frac0 = arena[:, at:AR].rearrange("p (t n) -> p t n", n=2 * MG)
            at -= M * MG
            mask0 = arena[:, at:at + M * MG].rearrange("p (t n) -> p t n", n=MG)
            at -= (M + 2) * MG
            idx0 = arena[:, at:at + (M + 2) * MG].bitcast(U32).rearrange("p (t n) -> p t n", n=MG)
            yield_places(nc, k, "pl0", om0, idx0, frac0, mask0, MG, True, at, AR)
            quads(nc, k, "quads0", G)
            sample(nc, k, "smp0", idx0, frac0, mask0, MG, True, 4 * C // G, True)
        clear_borders(nc, k)
        end_layer(nc, k)
        if STAGES == 1:
            return store_x(nc, k)

        group_norm(nc, k, "gn1", True)
        BF = mybir.dt.bfloat16
        om1 = arena[:, 0:M * NO1].rearrange("p (t n) -> p t n", n=NO1)
        size = S1 * CH
        work1 = arena[:, M * NO1:M * NO1 + 3 * CH]
        at = M * NO1 + 3 * CH
        k["rel1"] = arena[0:R3, at:at + CH]
        k["rep1"] = arena[0:2 * NO1, at + CH:at + CH + 2 * R3].rearrange("p (h n) -> p h n", h=2)
        assert at + CH + 2 * R3 <= size
        bmat = [arena[0:KW, 0:size]]
        o3 = arena[0:K3, size:size + 2 * PIX].bitcast(BF)
        at = size + 2 * PIX

        def window_slot(at):
            return arena[0:KW, at:at + 2 * (WW // IW) * C].rearrange("p (u t c) -> p u t c", u=2, c=C)

        win = [window_slot(at)]
        at += 2 * (WW // IW) * C
        k["dws"] = arena[:, at:at + TAPS * C].rearrange("p (t o) -> p t o", o=C)
        at += TAPS * C
        k["sc"] = arena[:, at:at + 2 * COLS].rearrange("p (h n) -> p h n", h=2)
        raw = arena[0:2 * NO1, at:at + COLS]
        at += 2 * COLS
        k["dws2_flat"] = arena[:, at:at + TAPS * 128]
        k["dws2"] = k["dws2_flat"].rearrange("p (t o) -> p t o", o=128)
        out1 = arena[:, at:at + 2 * (ROWS * PW + ROWS // 2 * 128)]
        low1 = at + TAPS * 128
        bmat.append(arena[0:KW, at:at + size])
        at += size
        win.append(window_slot(at))
        at += 2 * (WW // IW) * C
        k["sel1"] = arena[0:K3, at:at + NO1 * KW // 2].bitcast(BF).rearrange("p (s n) -> p s n", s=NO1)
        assert at + NO1 * KW // 2 <= AR
        loads = [(k["rel1"], dram["rel1"]), (k["rep1"], dram["rep1"]), (k["sel1"], dram["sel1"])] + \
            [(k["dws"][64 * v:64 * v + 64, :, :], dram["dws"][v].rearrange("t c o -> c t o")) for v in range(2)]
        xn = k["xn"]
        pixels_out(nc, k, "pix1", lambda b2, r: xn[:, bass.ds(r * CH + b2 * PIX, CH)]
                   .rearrange("p (y x) -> p y x", y=ROWS), out1, loads)
        offsets1(nc, k, raw, o3, work1)
        widest1(nc, k, raw)
        wide = nc.values_load(k["flag"][0:1, 0:1], min_val=0, max_val=1)
        with nc.If(wide < WIDE):
            smp = k["xp_flat"][:, 0:TAPS * CH]
            windows1(nc, k, o3, bmat, win, k["sc"], smp, k["xp_flat"][:, TAPS * CH:TAPS * CH + 4 * CH])
        with nc.Else():
            turn_offsets1(nc, k, raw, om1, work1)
            at = AR - M * NO1
            frac1 = arena[:, at:AR].rearrange("p (t n) -> p t n", n=NO1)
            at -= (M + 2) * S1
            idx1 = arena[:, at:at + (M + 2) * S1].bitcast(U32).rearrange("p (t n) -> p t n", n=S1)
            assert low1 <= at
            yield_places(nc, k, "pl1", om1, idx1, frac1, None, S1, False, at, AR)
            quads(nc, k, "quads1", 1)
            sample(nc, k, "smp1", idx1, frac1, None, S1, False, 4 * C, False)
        fuse1(nc, k)
        if STAGES == 2:
            return store_x(nc, k)

        group_norm(nc, k, "gn2", False)
        BF = mybir.dt.bfloat16
        stacks = [arena[:, COLS * i:COLS * i + COLS].bitcast(BF) for i in range(4)]
        parts = [k["xp_flat"][:, 0:PIX].bitcast(BF), k["xp_flat"][:, PIX:COLS].bitcast(BF),
                 arena[:, 4 * COLS:4 * COLS + PIX].bitcast(BF)]
        low = 4 * COLS + PIX
        at = arena[:, low:low + NT * 3 * C].rearrange("p (t c) -> p t c", c=3 * C)
        project2(nc, k, arena[:, low + NT * 3 * C:AR], parts, at, *stacks)
        k["atwork"] = arena[:, low + NT * 3 * C:AR]
        attend2(nc, k, *stacks, at)
        if STAGES == 3:
            return store_x(nc, k)

        w2, b2t = weights3(k)
        group_norm(nc, k, "gn3", True, [(w2, dram["W2"])] + [(b2t[64 * h:64 * h + 64, :], dram["b2"]) for h in range(2)])
        dynamic3(nc, k)


def yield_places(nc, k, tag, om, idx, frac, mask, ns, xfirst, low, AR):
    M = 2 * NT
    base = k[f"base_{tag}"] = k["ctx"].enter_context(nc.sbuf_tensor("base_" + tag, [128, TPI, 2 * ns], F32))
    goff = k["ctx"].enter_context(nc.sbuf_tensor("goff_" + tag, [128, NB, ns], F32))
    loaded = signal(k, tag + "_consts")
    with nc.Block() as block:
        @block.sync
        def _(sp):
            sp.dma_start(base[:, :, :], k["dram"]["base_" + tag]).then_inc(loaded, 16)
            sp.dma_start(goff[:, :, :], k["dram"]["goff_" + tag].partition_broadcast(128)).then_inc(loaded, 16)
            sp.wait_ge(loaded, 32)
    A = k["arena"]
    n = M * 2 * ns
    at = M * om.shape[2]
    assert at + 2 * n <= low
    r1, r2 = A[:, at:at + n], A[:, at + n:at + 2 * n]
    places(nc, k, tag, om, base[:, :, :], goff[:, :, :], idx, frac, ns, xfirst, (r1, r2), mask)


def kernel(**inputs):
    import ml_dtypes
    import numpy as np
    import concourse.bacc as _bacc
    from concourse.bass_utils import run_bass_kernel_spmd as _run

    I = {n: np.asarray(a) for n, a in inputs.items()}
    f = np.float32
    a = {"x": I["x"]}
    L0 = {n[8:]: v for n, v in I.items() if n.startswith("L0_conv_")}
    L1 = {n[8:]: v for n, v in I.items() if n.startswith("L1_conv_")}
    L2 = {n[8:]: v for n, v in I.items() if n.startswith("L2_conv_")}
    L3 = {n[8:]: v for n, v in I.items() if n.startswith("L3_conv_")}
    vecs = dict(L0, gp_b3=L1["gp_b3"], cr_b=L1["cr_b"])
    a["vec64"] = np.stack([vecs[n] for n in V64], 1)
    a["dw_w"] = L0["dw_w"].reshape(C, TAPS)
    a["ident"] = np.eye(128, dtype=f)
    rows = np.arange(3 * 2 * G * 5)
    a["sel"] = ((rows % 5)[:, None, None] == np.arange(5)[None, :, None]) & \
        (((rows // 5) % (2 * G))[:, None, None] == (np.arange(128) // 16)[None, None, :])
    a["sel"] = a["sel"].astype(ml_dtypes.bfloat16)
    a["pairm"] = np.kron(np.eye(64), np.full((2, 2), 1.0 / (2 * PIX))).astype(f)
    a["halfm"] = np.kron(np.eye(2), np.full((64, 64), 1.0 / 64)).astype(f)
    a["stack2"] = np.concatenate([np.eye(64, dtype=f)] * 2, 0)
    a["b_om"] = np.concatenate([L0["b_off"], L0["b_mask"]])
    a["b1_3"] = np.tile(L3["b1"], 4)[:, None]
    a["ba"] = L2["ba"]
    a["offb"] = np.concatenate([L1["off_b0"], L1["off_b1"]] * 2)[:, None]
    a["dbs"] = np.concatenate([L1["db0"], L1["db1"]])[:, None]
    a["wg1T"] = L1["wg_w1"].T
    a["wgb1"] = L1["wg_b1"][:, None]
    a["wg2T"] = L1["wg_w2"].T
    a["wgb2"] = L1["wg_b2"]
    a["gp1T"] = np.concatenate([L1["gp_w1"].T] * 2, 0)
    a["gpb1"] = L1["gp_b1"][:, None]
    a["gp2T"] = L1["gp_w2"].T
    a["gpb2"] = L1["gp_b2"][:, None]
    a["gp3T"] = np.concatenate([L1["gp_w3"].T] * 2, 1)
    a["l2b"] = np.concatenate([L2["b1"], L2["b2"]] * 2)[:, None]
    a["alphas"] = np.stack([np.concatenate([np.broadcast_to(L2[n], HID) for n in ("a1", "a2")] * 2),
                            np.broadcast_to(L2["aa"], 128)], 1)
    a["w_om"] = np.concatenate([L0["w_off"], L0["w_mask"]], 1)
    a["w_in"] = L0["w_in"]
    a["w_out"] = L0["w_out"]
    a["crT"] = L1["cr_w"].T
    a["waT"] = L2["wa"].T
    a["w31T"] = np.tile(L3["W1"].T, (1, 4))
    a["offw"] = np.concatenate([L1["off_w0"], L1["off_w1"]], 0).reshape(36, C, TAPS).transpose(1, 2, 0)
    a["l2w"] = np.concatenate([L2["w1"].T, L2["w2"].T], 1)
    a["dws"] = np.stack([L1["dw0"], L1["dw1"]]).reshape(2, C, C, TAPS).transpose(0, 3, 2, 1)
    row = np.arange(R3) % NO1
    tap, axis = row // 2 % TAPS, row % 2
    y, xx = np.divmod(np.arange(CH), WW)
    a["rel1"] = np.where(axis[:, None] == 0, y % IH + tap[:, None] // 3 + 2,
                         xx % IW + tap[:, None] % 3 + 2).astype(f)
    a["drop"] = np.stack([np.arange(R3) >= NO1, np.arange(R3) >= 2 * NO1], 1).astype(f) * f(-1)
    half, i, j = (v.ravel() for v in np.meshgrid(range(2), range(WH), range(IW), indexing="ij"))
    own = -np.stack([i, IW * half + j])[np.arange(NO1) % 2][None]
    spread = np.repeat((row[:, None] == np.arange(NO1))[:, :, None], KW, 2)
    a["sel1"] = np.concatenate([spread, own]).astype(ml_dtypes.bfloat16)
    a["rep1"] = (np.arange(2 * NO1)[:, None, None] == NO1 * np.arange(2)[:, None] + row).astype(f)
    a["W2"] = L3["W2"].reshape(C, C, TAPS, HID).transpose(3, 1, 2, 0).reshape(HID, 4, -1).transpose(1, 0, 2)\
        .reshape(128, -1)
    a["b2"] = L3["b2"].reshape(C, C, TAPS).transpose(1, 2, 0).reshape(C, -1)
    pix = np.arange(PIX).reshape(TPI, PT).T
    y, xx = pix // WW, pix % WW
    tap = np.arange(TAPS)
    b0 = np.stack([xx[..., None] + tap // 3, y[..., None] + tap % 3], -1)
    a["base_pl0"] = np.tile(b0[:, :, None], (1, 1, G, 1, 1)).reshape(128, TPI, 2 * MG).astype(f)
    b1 = np.stack([y[..., None] + tap // 3, xx[..., None] + tap % 3], -1)
    a["base_pl1"] = np.tile(b1[:, :, None], (1, 1, 2, 1, 1)).reshape(128, TPI, 2 * S1).astype(f)
    img = np.arange(NB) * TR * TR
    a["goff_pl0"] = (img[:, None] * G + np.repeat(np.arange(G), TAPS)[None]).astype(f)
    a["goff_pl1"] = np.repeat(img[:, None], S1, 1).astype(f)

    nc = _bacc.Bacc("TRN2", target_bir_lowering=False, num_devices=1)
    arrays, dram = {}, {}
    for n, v in a.items():
        arrays["in_" + n] = np.ascontiguousarray(v)
        dram[n] = nc.dram_tensor("in_" + n, arrays["in_" + n].shape,
                                 mybir.dt.from_np(arrays["in_" + n].dtype), kind="ExternalInput").ap()
    dram["out"] = nc.dram_tensor("out_x", (NB, C, HH, WW), F32, kind="ExternalOutput").ap()
    program(nc, dram)
    r = _run(nc, [arrays], core_ids=[0])
    return r.results[0]["out_x"]
```
